# Optimizing a Trainium2 kernel written in Bass

```python
import numpy as np
import jax
import jax.numpy as jnp

def _softmax(x, axis=-1):
    return jax.nn.softmax(x, axis=axis)

def _gelu(x):
    return jax.nn.gelu(x, approximate=True)

def _silu(x):
    return jax.nn.silu(x)

def _sigmoid(x):
    return jax.nn.sigmoid(x)

def _layernorm(x, axis=-1, eps=1e-05):
    m = jnp.mean(x, axis=axis, keepdims=True)
    v = jnp.var(x, axis=axis, keepdims=True)
    return (x - m) / jnp.sqrt(v + eps)

def _scatter_add(tgt, idx, src, axis=0):
    return tgt.at[idx].add(src)

def _segment_sum(src, seg, n):
    return jax.ops.segment_sum(src, seg, n)
kernel_name = 'mk_adaln_attn_ffn_d1_seqx_r4_3b4c06'

def setup_inputs(seed: int=0):
    np.random.seed(seed)
    _w = jnp.asarray

    def _rec_inputs():
        import jax
        import jax.numpy as jnp
        _rk = jax.random.key(seed)
        x = -0.000125 + 0.9999 * jax.random.normal(jax.random.fold_in(_rk, 1), (32, 64, 1024), jnp.float32)
        _lenS = 64 - jax.random.randint(jax.random.fold_in(_rk, 7), (32,), 0, max(1, 64 // 4) + 1, jnp.int32)
        _lenS2 = 64 - jax.random.randint(jax.random.fold_in(_rk, 8), (32,), 0, max(1, 64 // 4) + 1, jnp.int32)
        itok_B_0_2 = jax.random.randint(jax.random.fold_in(_rk, 11), (32,), 0, 3, jnp.int32)
        itok_B_0_7 = jax.random.randint(jax.random.fold_in(_rk, 12), (32,), 0, 8, jnp.int32)
        return (x, itok_B_0_2, itok_B_0_7)
    x, itok_B_0_2, itok_B_0_7 = _rec_inputs()

    def _L0_cond_setup():
        import jax, jax.numpy as jnp
        import numpy as np
        B, S, D_IN, D_OUT = (4, 512, 1024, 1024)
        R, NUM_LABELERS = (32, 5)
        LORA_SCALING = 16 / 32
        key = jax.random.key(seed)
        k1, k2, k3, k4, k5 = jax.random.split(key, 5)
        x = jax.random.normal(k1, (B, S, D_IN), dtype=jnp.float32)
        labeler_index = jax.random.randint(k2, (B,), 0, NUM_LABELERS, dtype=jnp.int64)
        W = jax.random.normal(k3, (D_OUT, D_IN), dtype=jnp.float32) * 0.02
        lora_A = jax.random.normal(k4, (NUM_LABELERS, D_IN, R), dtype=jnp.float32) * 0.02
        lora_B_w = jax.random.normal(k5, (D_OUT, R), dtype=jnp.float32) * 0.02
        return {'x': x, 'labeler_index': labeler_index, 'W': W, 'lora_A': lora_A, 'lora_B_w': lora_B_w}
    _L0_cond_all = _L0_cond_setup()
    _L0_cond_in = {k: v for k, v in _L0_cond_all.items() if k in ('W', 'lora_A', 'lora_B_w')}
    del _L0_cond_all

    def _L0_attn_setup():
        import jax, jax.numpy as jnp
        import numpy as np
        import math
        D_MODEL = 1024
        NUM_HEADS = 32
        NUM_KV_HEADS = 8
        HEAD_DIM = D_MODEL // NUM_HEADS
        GROUP = NUM_HEADS // NUM_KV_HEADS
        SEQ_LEN = 512
        BATCH = 2
        ROPE_THETA = 10000.0

        def apply_rope(x, start_pos=0):
            b, h, s, hd = x.shape
            inv_freq = 1.0 / ROPE_THETA ** (jnp.arange(0, hd, 2, dtype=jnp.float32) / hd)
            pos = jnp.arange(start_pos, start_pos + s, dtype=jnp.float32)
            ang = pos[:, None] * inv_freq[None, :]
            cos = jnp.cos(ang).astype(x.dtype)
            sin = jnp.sin(ang).astype(x.dtype)
            xr = x[..., 0::2]
            xi = x[..., 1::2]
            out_r = xr * cos - xi * sin
            out_i = xr * sin + xi * cos
            return jnp.stack([out_r, out_i], axis=-1).reshape(b, h, s, hd)
        key = jax.random.key(seed)
        ks = jax.random.split(key, 5)
        qkv_dim = HEAD_DIM * (NUM_HEADS + 2 * NUM_KV_HEADS)
        scale = 1.0 / math.sqrt(D_MODEL)
        return {'x': jax.random.normal(ks[0], (BATCH, SEQ_LEN, D_MODEL), jnp.float32), 'w_qkv': jax.random.normal(ks[1], (qkv_dim, D_MODEL), jnp.float32) * scale, 'b_qkv': jax.random.normal(ks[2], (qkv_dim,), jnp.float32) * 0.01, 'w_o': jax.random.normal(ks[3], (D_MODEL, D_MODEL), jnp.float32) * scale, 'b_o': jax.random.normal(ks[4], (D_MODEL,), jnp.float32) * 0.01}
    _L0_attn_all = _L0_attn_setup()
    _L0_attn_in = {k: v for k, v in _L0_attn_all.items() if k in ('w_qkv', 'b_qkv', 'w_o', 'b_o')}
    del _L0_attn_all

    def _L0_cond2_setup():
        import jax, jax.numpy as jnp
        import numpy as np
        TOP_K = 2
        LANG_BIAS = 5.0
        SCALING = 32.0 / 16.0
        LANGUAGE_PAD_ID = -1
        key = jax.random.key(seed)
        ks = jax.random.split(key, 6)
        B, T, D, O, E, R = (4, 512, 1024, 1024, 8, 16)
        x = jax.random.normal(ks[0], (B, T, D), dtype=jnp.float32)
        language_ids = jax.random.randint(ks[1], (B,), 0, E).astype(jnp.int64)
        W = jax.random.normal(ks[2], (O, D), dtype=jnp.float32) * (1.0 / np.sqrt(D))
        Wr = jax.random.normal(ks[3], (E, D), dtype=jnp.float32) * (1.0 / np.sqrt(D))
        A = jax.random.normal(ks[4], (E, R, D), dtype=jnp.float32) * (1.0 / np.sqrt(D))
        Bm = jax.random.normal(ks[5], (O, R), dtype=jnp.float32) * 0.0
        Bm = jnp.broadcast_to(Bm, (E, O, R)) + jax.random.normal(ks[5], (E, O, R), dtype=jnp.float32) * 0.02
        return {'x': x, 'language_ids': language_ids, 'W': W, 'Wr': Wr, 'A': A, 'B': Bm}
    _L0_cond2_all = _L0_cond2_setup()
    _L0_cond2_in = {k: v for k, v in _L0_cond2_all.items() if k in ('W', 'Wr', 'A', 'B')}
    del _L0_cond2_all

    def _L0_ffn_setup():
        import jax, jax.numpy as jnp
        import numpy as np
        R = 16
        NUM_EXPERTS = 8
        TOP_K = 2
        LORA_ALPHA = 32
        SCALING = LORA_ALPHA / R
        key = jax.random.key(seed)
        ks = jax.random.split(key, 6)
        d_in, d_out = (1024, 1024)
        x = jax.random.normal(ks[0], (4, 512, d_in), dtype=jnp.float32)
        W_base = jax.random.normal(ks[1], (d_out, d_in), dtype=jnp.float32) * 0.02
        b_base = jax.random.normal(ks[2], (d_out,), dtype=jnp.float32) * 0.02
        W_router = jax.random.normal(ks[3], (NUM_EXPERTS, d_in), dtype=jnp.float32) * 0.01
        A = jax.random.normal(ks[4], (NUM_EXPERTS, R, d_in), dtype=jnp.float32) * 0.02
        B = jax.random.normal(ks[5], (NUM_EXPERTS, d_out, R), dtype=jnp.float32) * 0.02
        return {'x': x, 'W_base': W_base, 'b_base': b_base, 'W_router': W_router, 'A': A, 'B': B}
    _L0_ffn_all = _L0_ffn_setup()
    _L0_ffn_in = {k: v for k, v in _L0_ffn_all.items() if k in ('W_base', 'b_base', 'W_router', 'A', 'B')}
    del _L0_ffn_all
    return {'x': x, 'itok_B_0_2': itok_B_0_2, 'itok_B_0_7': itok_B_0_7, 'L0_cond_W': _L0_cond_in['W'], 'L0_cond_lora_A': _L0_cond_in['lora_A'], 'L0_cond_lora_B_w': _L0_cond_in['lora_B_w'], 'L0_attn_w_qkv': _L0_attn_in['w_qkv'], 'L0_attn_b_qkv': _L0_attn_in['b_qkv'], 'L0_attn_w_o': _L0_attn_in['w_o'], 'L0_attn_b_o': _L0_attn_in['b_o'], 'L0_cond2_W': _L0_cond2_in['W'], 'L0_cond2_Wr': _L0_cond2_in['Wr'], 'L0_cond2_A': _L0_cond2_in['A'], 'L0_cond2_B': _L0_cond2_in['B'], 'L0_ffn_W_base': _L0_ffn_in['W_base'], 'L0_ffn_b_base': _L0_ffn_in['b_base'], 'L0_ffn_W_router': _L0_ffn_in['W_router'], 'L0_ffn_A': _L0_ffn_in['A'], 'L0_ffn_B': _L0_ffn_in['B']}

def reference(x, itok_B_0_2, itok_B_0_7, L0_cond_W, L0_cond_lora_A, L0_cond_lora_B_w, L0_attn_w_qkv, L0_attn_b_qkv, L0_attn_w_o, L0_attn_b_o, L0_cond2_W, L0_cond2_Wr, L0_cond2_A, L0_cond2_B, L0_ffn_W_base, L0_ffn_b_base, L0_ffn_W_router, L0_ffn_A, L0_ffn_B):
    import jax
    import jax.numpy as jnp

    def _L0_cond_ref(x, labeler_index, W, lora_A, lora_B_w):
        import jax, jax.numpy as jnp
        import numpy as np
        B, S, D_IN, D_OUT = (4, 512, 1024, 1024)
        R, NUM_LABELERS = (32, 5)
        LORA_SCALING = 16 / 32
        base = jnp.einsum('bsi,oi->bso', x, W)
        labelers_A = lora_A[labeler_index]
        low = jnp.einsum('bsi,bir->bsr', x, labelers_A)
        delta = jnp.einsum('bsr,or->bso', low, lora_B_w) * LORA_SCALING
        return base + delta

    def _L0_attn_ref(x, w_qkv, b_qkv, w_o, b_o):
        import jax, jax.numpy as jnp
        import numpy as np
        import math
        D_MODEL = 1024
        NUM_HEADS = 32
        NUM_KV_HEADS = 8
        HEAD_DIM = D_MODEL // NUM_HEADS
        GROUP = NUM_HEADS // NUM_KV_HEADS
        SEQ_LEN = 512
        BATCH = 2
        ROPE_THETA = 10000.0

        def apply_rope(x, start_pos=0):
            b, h, s, hd = x.shape
            inv_freq = 1.0 / ROPE_THETA ** (jnp.arange(0, hd, 2, dtype=jnp.float32) / hd)
            pos = jnp.arange(start_pos, start_pos + s, dtype=jnp.float32)
            ang = pos[:, None] * inv_freq[None, :]
            cos = jnp.cos(ang).astype(x.dtype)
            sin = jnp.sin(ang).astype(x.dtype)
            xr = x[..., 0::2]
            xi = x[..., 1::2]
            out_r = xr * cos - xi * sin
            out_i = xr * sin + xi * cos
            return jnp.stack([out_r, out_i], axis=-1).reshape(b, h, s, hd)
        bs, seq_len, d_model = x.shape
        qkv = x @ w_qkv.T + b_qkv
        q_dim = NUM_HEADS * HEAD_DIM
        kv_dim = NUM_KV_HEADS * HEAD_DIM
        q, k, v = jnp.split(qkv, [q_dim, q_dim + kv_dim], axis=-1)
        q = q.reshape(bs, seq_len, NUM_HEADS, HEAD_DIM).transpose(0, 2, 1, 3)
        k = k.reshape(bs, seq_len, NUM_KV_HEADS, HEAD_DIM).transpose(0, 2, 1, 3)
        v = v.reshape(bs, seq_len, NUM_KV_HEADS, HEAD_DIM).transpose(0, 2, 1, 3)
        q = apply_rope(q, 0)
        k = apply_rope(k, 0)
        k = jnp.repeat(k, GROUP, axis=1)
        v = jnp.repeat(v, GROUP, axis=1)
        scores = jnp.einsum('bhqd,bhkd->bhqk', q, k) / math.sqrt(HEAD_DIM)
        causal = jnp.tril(jnp.ones((seq_len, seq_len), dtype=bool))
        scores = jnp.where(causal[None, None, :, :], scores, jnp.float32(-1e+20))
        attn = jax.nn.softmax(scores, axis=-1)
        out = jnp.einsum('bhqk,bhkd->bhqd', attn, v)
        out = out.transpose(0, 2, 1, 3).reshape(bs, seq_len, d_model)
        return out @ w_o.T + b_o

    def _L0_cond2_ref(x, language_ids, W, Wr, A, B):
        import jax, jax.numpy as jnp
        import numpy as np
        TOP_K = 2
        LANG_BIAS = 5.0
        SCALING = 32.0 / 16.0
        LANGUAGE_PAD_ID = -1
        base = jnp.einsum('btd,od->bto', x, W)
        E = Wr.shape[0]
        logits = jnp.einsum('btd,ed->bte', x.astype(jnp.float32), Wr.astype(jnp.float32))
        expert_targets = language_ids
        valid = expert_targets >= 0
        tgt = jnp.where(valid, expert_targets, 0)
        bias = jax.nn.one_hot(tgt, E, dtype=logits.dtype) * LANG_BIAS
        bias = jnp.where(valid[:, None], bias, 0.0)
        logits = logits + bias[:, None, :]
        topw, topi = jax.lax.top_k(logits, TOP_K)
        weights = jax.nn.softmax(topw, axis=-1)
        gates = jnp.sum(jax.nn.one_hot(topi, E, dtype=weights.dtype) * weights[..., None], axis=-2)
        gates = gates.astype(x.dtype)
        h = jnp.einsum('btd,erd->bter', x, A)
        lora_out = jnp.einsum('bter,bte,eor->bto', h, gates, B)
        return base + SCALING * lora_out

    def _L0_ffn_ref(x, W_base, b_base, W_router, A, B):
        import jax, jax.numpy as jnp
        import numpy as np
        R = 16
        NUM_EXPERTS = 8
        TOP_K = 2
        LORA_ALPHA = 32
        SCALING = LORA_ALPHA / R
        orig_shape = x.shape
        d_in = x.shape[-1]
        x_flat = x.reshape(-1, d_in)
        logits = x_flat @ W_router.T
        probs = jax.nn.softmax(logits, axis=-1)
        topk_probs, topk_idx = jax.lax.top_k(probs, TOP_K)
        topk_probs = topk_probs / jnp.sum(topk_probs, axis=-1, keepdims=True)
        onehot = jax.nn.one_hot(topk_idx, NUM_EXPERTS, dtype=x.dtype)
        combine = jnp.einsum('nk,nke->ne', topk_probs, onehot)
        h = jnp.einsum('nd,erd->ner', x_flat, A)
        hw = h * combine[:, :, None]
        expert_out = jnp.einsum('ner,eor->no', hw, B) * SCALING
        base_out = x_flat @ W_base.T + b_base
        out = base_out + expert_out
        return out.reshape(*orig_shape[:-1], W_base.shape[0])
    x = x + _L0_attn_ref(_L0_cond_ref(x, itok_B_0_2, L0_cond_W, L0_cond_lora_A, L0_cond_lora_B_w), L0_attn_w_qkv, L0_attn_b_qkv, L0_attn_w_o, L0_attn_b_o)
    x = x + _L0_ffn_ref(_L0_cond2_ref(x, itok_B_0_7, L0_cond2_W, L0_cond2_Wr, L0_cond2_A, L0_cond2_B), L0_ffn_W_base, L0_ffn_b_base, L0_ffn_W_router, L0_ffn_A, L0_ffn_B)
    return x

_drawn_inputs = setup_inputs


def setup_inputs(seed=0):
    import zlib

    import numpy as np

    out = dict(_drawn_inputs(seed))
    spreads = {}
    factors = {'L0_cond_lora_A': 4.409,
     'L0_cond_lora_B_w': 4.52,
     'L0_attn_b_qkv': 4.865,
     'L0_attn_b_o': 4.787,
     'L0_cond2_Wr': 5.097,
     'L0_ffn_b_base': 3.378}
    for name, (base, spread) in spreads.items():
        noise = np.random.default_rng([zlib.crc32(name.encode()), seed]).standard_normal(out[name].shape)
        drawn = base * np.exp(spread * noise) if base else spread * noise
        out[name] = jnp.asarray(drawn.astype(out[name].dtype))
    for name, factor in factors.items():
        out[name] = (out[name] * factor).astype(out[name].dtype)
    return out
```

```python
import numpy as np
import concourse.bass as bass
from concourse import mybir
from contextlib import ExitStack

F32 = mybir.dt.float32
F32R = mybir.dt.float32r
BF16 = mybir.dt.bfloat16
I32 = mybir.dt.int32
ALU = mybir.AluOpType
ACT = mybir.ActivationFunctionType
AX = mybir.AxisListType

P = 128
BATCH, SEQ, D = 32, 64, 1024
TOK = BATCH * SEQ
UNITS = TOK // P
BPU = P // SEQ
KT = D // P
HEADS, KVH, HD = 32, 8, 32
GRP = HEADS // KVH
QUADS = KVH // 4
QKV = (HEADS + 2 * KVH) * HD
QK = (HEADS + KVH) * HD
BANK = 512
NCH = QKV // BANK
LAB, LR = 5, 32
EXP, ER = 8, 16
ERS = EXP * ER
GATED = EXP + ERS
FOUT = D + GATED
FCOLS = FOUT + GATED
FCH = 256
SCALE = float(HD) ** -0.5
LORA_SCALE = 0.5
MOE_SCALE = 2.0
LANG_BIAS = 5.0
HALF = KT // 2


def need(engine, semaphore, value):
    if isinstance(value, int) and value <= 0:
        return
    engine.wait_ge(semaphore, value)


def build(nc, a):
    with ExitStack() as ctx:
        names = {}

        def sem(name):
            if name not in names:
                names[name] = ctx.enter_context(nc.semaphore(name))
            return names[name]

        attn_dram = nc.dram_tensor("attn_scratch", (UNITS, P, KT * P), F32, kind="Internal").ap()
        fold_qkv(nc, a, sem, attn_dram)
        fold_ffn(nc, a, sem, attn_dram)


def fold_qkv(nc, a, sem, attn_dram):
    with ExitStack() as keep:
        def sb(name, shape, dt=F32, stack=keep):
            return stack.enter_context(nc.sbuf_tensor(name, shape, dt))

        p1_h = sb("p1_h", [P, NCH, KT, BANK], F32R)
        p1_l = sb("p1_l", [P, NCH, KT, BANK], F32R)
        pb = sb("pb", [P, QKV], F32R)
        with ExitStack() as st:
            w_h, w_l = sb("w_h", [P, KT, D], F32R, st), sb("w_l", [P, KT, D], F32R, st)
            c_h, c_l = sb("c_h", [P, 2, KT, FCH], F32R, st), sb("c_l", [P, 2, KT, FCH], F32R, st)
            raw = sb("raw", [P, D], F32, st)

            def part(p1):
                return lambda i, ch: p1[:, ch // 2, i, (ch % 2) * FCH:(ch % 2 + 1) * FCH]

            def low_rows(ch, src):
                for r in (slice(LR, 2 * LR), slice(3 * LR, 4 * LR)):
                    out = pb[r, ch * FCH:(ch + 1) * FCH]
                    yield out, out, src[r]

            fold_program(nc, sem, "f1", st, a["w_cond"], [a["wqkv_t"][n] for n in range(QKV // FCH)],
                         [FCH] * (QKV // FCH), raw, w_h, w_l, c_h, c_l, part(p1_h), part(p1_l),
                         a["lora_b"], LR, lambda ch: pb[:, ch * FCH:(ch + 1) * FCH], low_rows)
        attention(nc, a, sem, attn_dram, keep, p1_h, p1_l, pb)


def fold_program(nc, sem, tag, st, w_dram, c_dram, widths, raw, w_h, w_l, c_h, c_l, out_h, out_l, lb_dram, lr, lora_h, lora_l):
    chunks = len(widths)
    lb_raw = st.enter_context(nc.sbuf_tensor(f"{tag}_lb_raw", [P, KT, lr], F32))
    lb_h = st.enter_context(nc.sbuf_tensor(f"{tag}_lb_h", [P, KT, P], F32R))
    lb_l = st.enter_context(nc.sbuf_tensor(f"{tag}_lb_l", [P, KT, P], F32R))
    ps = [st.enter_context(nc.psum_tensor(f"{tag}_ps{n}", [P, BANK], F32)) for n in range(4)]
    loaded = sem(f"{tag}_raw_loaded")
    high = sem(f"{tag}_high")
    low = sem(f"{tag}_low")
    lb_loaded = sem(f"{tag}_lb_loaded")
    lb_high, lb_low = sem(f"{tag}_lb_high"), sem(f"{tag}_lb_low")
    done = sem(f"{tag}_tile_done")
    out_high, out_low = sem(f"{tag}_out_high"), sem(f"{tag}_out_low")
    tiles = KT + 1
    reps = P // lr

    def piece(n):
        if n < KT:
            return raw[:, :], w_h[:, n, :], w_l[:, n, :], w_dram[:, n, :]
        ch, h = divmod(n - KT, 2)
        w, ks = widths[ch], slice(h * HALF, (h + 1) * HALF)
        return (raw[:, 0:HALF * w].rearrange("p (k c) -> p k c", k=HALF), c_h[:, ch % 2, ks, 0:w],
                c_l[:, ch % 2, ks, 0:w], c_dram[ch][:, ks, :])

    def chunk_pieces(ch):
        return range(KT + 2 * ch, KT + 2 * ch + 2)

    with nc.Block() as block:
        @block.sync
        def _(sp):
            sp.dma_start(lb_raw[:, :, :], lb_dram).then_inc(lb_loaded, 16)
            for n in range(KT + 2 * chunks):
                dst, _, _, src = piece(n)
                need(sp, low, n)
                sp.dma_start(dst, src).then_inc(loaded, 16)

        @block.scalar
        def _(act):
            def split(n):
                dst, hi, _, _ = piece(n)
                act.wait_ge(loaded, 16 * (n + 1))
                act.activation(hi, dst, ACT.Copy).then_inc(high, 1)

            act.wait_ge(lb_loaded, 16)
            for r in range(reps):
                last = act.activation(lb_h[:, :, r * lr:(r + 1) * lr], lb_raw[:, :, :], ACT.Copy)
            last.then_inc(lb_high, 1)
            for n in range(KT + 2):
                split(n)
            for ch in range(chunks):
                for i in range(tiles):
                    t = ch * tiles + i
                    act.wait_ge(done, t + 1)
                    act.activation(out_h(i, ch) if i < KT else lora_h(ch), ps[t % 4][:, 0:widths[ch]],
                                   ACT.Copy).then_inc(out_high, 1)
                    if i == 0 and ch + 1 < chunks:
                        for n in chunk_pieces(ch + 1):
                            split(n)

        @block.vector
        def _(dve):
            def split(n):
                dst, hi, lo, _ = piece(n)
                dve.wait_ge(high, n + 1)
                dve.tensor_tensor(lo, dst, hi.bitcast(F32), ALU.subtract).then_inc(low, 1)

            dve.wait_ge(lb_high, 1)
            for r in range(reps):
                rs = slice(r * lr, (r + 1) * lr)
                last = dve.tensor_tensor(lb_l[:, :, rs], lb_raw[:, :, :], lb_h[:, :, rs].bitcast(F32), ALU.subtract)
            last.then_inc(lb_low, 1)
            for n in range(KT + 2):
                split(n)
            for ch in range(chunks):
                for i in range(tiles):
                    t = ch * tiles + i
                    dve.wait_ge(out_high, t + 1)
                    src = ps[t % 4][:, 0:widths[ch]]
                    pairs = [(out_l(i, ch), out_h(i, ch), src)] if i < KT else lora_l(ch, src)
                    for lo, hi, s in pairs:
                        last = dve.tensor_tensor(lo, s, hi.bitcast(F32), ALU.subtract)
                    last.then_inc(out_low, 1)
                    if i == 0 and ch + 1 < chunks:
                        for n in chunk_pieces(ch + 1):
                            split(n)

        @block.tensor
        def _(pe):
            pe.wait_ge(lb_low, 1)
            for ch in range(chunks):
                pe.wait_ge(low, KT + 2 * (ch + 1))
                w = widths[ch]
                for i in range(tiles):
                    t = ch * tiles + i
                    need(pe, out_low, t - 3)
                    o = ps[t % 4][:, 0:w]
                    for k in range(KT):
                        cols = slice(i * P, (i + 1) * P)
                        sh, sl = (w_h[:, k, cols], w_l[:, k, cols]) if i < KT else (lb_h[:, k, :], lb_l[:, k, :])
                        pe.matmul(o, sh, c_h[:, ch % 2, k, 0:w], start=k == 0, stop=False)
                        pe.matmul(o, sh, c_l[:, ch % 2, k, 0:w], start=False, stop=False)
                        mm = pe.matmul(o, sl, c_h[:, ch % 2, k, 0:w], start=False, stop=k == KT - 1)
                    mm.then_inc(done, 1)



def attention(nc, a, sem, attn_dram, keep, p1_h, p1_l, pb):
    def sb(name, shape, dt=F32):
        return keep.enter_context(nc.sbuf_tensor(name, shape, dt))

    x_raw = sb("x_raw", [P, KT, P])
    x_h, x_l = sb("x_h", [P, KT, P], F32R), sb("x_l", [P, KT, P], F32R)
    a_raw = sb("a_raw", [P, BPU, KT, LR])
    a_h, a_l = sb("a_h", [P, KT, BPU * LR], F32R), sb("a_l", [P, KT, BPU * LR], F32R)
    low4 = sb("low4", [P, 4, LR])
    lows = sb("lows", [P, P], F32R)
    qkv = sb("qkv", [P, QKV])
    b_bc = sb("b_bc", [P, QKV])
    NH = HEADS + KVH
    rot_t = sb("rot_t", [P, 2, NH, HD // 2])
    roped = sb("roped", [P, NH, HD // 2, 2])
    q_h, q_l = (sb(n, [P, BPU, QUADS, GRP, SEQ], F32R) for n in ("q_h", "q_l"))
    k_h, k_l = (sb(n, [P, QUADS, BPU, 4, SEQ], F32R) for n in ("k_h", "k_l"))
    v_hl = sb("v_hl", [P, 2, QUADS, 2, 2, HD], F32R)
    vb_h, vb_l = (sb(n, [P, BPU, QUADS, 2, 4, HD], F32R) for n in ("vb_h", "vb_l"))
    prob = sb("prob", [P, BPU, 2, KVH, SEQ])
    smax, ssum, sinv = (sb(n, [P, BPU, 2, KVH]) for n in ("smax", "ssum", "sinv"))
    pt_h, pt_l = (sb(n, [P, QUADS, 2, 2, P], F32R) for n in ("pt_h", "pt_l"))
    attn = sb("attn", [P, KT, BPU, SEQ])
    cos, sin = sb("cos", [P, HD // 2]), sb("sin", [P, HD // 2])
    hmask = sb("hmask", [P, 4])
    ident = sb("ident", [P, P])
    mask_l = sb("mask_l", [P, P], BF16)
    mask_r = sb("mask_r", [P, BANK], BF16)
    mask_f = prob[:, 0, :, :, :].rearrange("p g c k -> p (g c k)")
    index = sb("index", [1, BATCH], I32)
    bank = [keep.enter_context(nc.psum_tensor(f"bank{n}", [P, BANK], F32)) for n in range(4)]
    s_ps = keep.enter_context(nc.psum_tensor("s_ps", [P, 2, BANK], F32))
    t_ps = keep.enter_context(nc.psum_tensor("t_ps", [P, 2, BANK], F32))

    const_in, index_in, mask_ready = sem("const_in"), sem("index_in"), sem("mask_ready")
    x_in = [sem("x_in0"), sem("x_in1")]
    a_in = sem("a_in")
    x_high, x_low, a_high, a_low = sem("x_high"), sem("x_low"), sem("a_high"), sem("a_low")
    half_done = sem("half_done")
    low_copied, low_t, low_high, low_ready = sem("low_copied"), sem("low_t"), sem("low_high"), sem("low_ready")
    qkv_done, qkv_out = sem("qkv_done"), sem("qkv_out")
    rot_re, rot_im, rotated = sem("rot_re"), sem("rot_im"), sem("rotated")
    qk_t, qk_high, qk_low = sem("qk_t"), sem("qk_high"), sem("qk_low")
    v_high, v_low, vb_zero, vb_high, vb_low = (sem(n) for n in ("v_high", "v_low", "vb_zero", "vb_high", "vb_low"))
    s_done, s_max, s_sub, s_exp, s_sum, s_inv, s_norm = (
        sem(n) for n in ("s_done", "s_max", "s_sub", "s_exp", "s_sum", "s_inv", "s_norm"))
    pt_done, pt_high, pt_low = sem("pt_done"), sem("pt_high"), sem("pt_low")
    pv_done, pv_out, stored = sem("pv_done"), sem("pv_out"), sem("attn_stored")
    consts = [(b_bc[:, :], a["b_qkv"].partition_broadcast(P)), (cos[:, :], a["cos"]), (sin[:, :], a["sin"]),
              (hmask[:, :], a["hmask"]), (ident[:, :], a["ident"]), (mask_f[:, BANK:BANK + P], a["mask_l"]),
              (mask_f[:, 0:BANK], a["mask_r"])]

    def k_ps():
        return t_ps[:, 0, 0:QUADS * P].rearrange("p (n t) -> p n t", t=SEQ)

    def diag(vb, b, h):
        flat = vb[h * SEQ:(h + 1) * SEQ, b, :, :, :, :].rearrange("p q j c d -> p q (j c d)")
        return flat.rearrange("p q (m d) -> p q m d", d=HD)[:, :, h:h + 7:6, :]

    def steps(engine, step):
        step(0, True, False, True)
        with engine.Fori(1, UNITS - 1) as u:
            step(u, True, True, True)
        step(UNITS - 1, True, True, False)
        step(UNITS, False, True, False)

    def ks(half):
        return slice(half * HALF, (half + 1) * HALF)

    with nc.Block() as block:
        @block.sync
        def _(sp):
            sp.dma_start(index[:, :], a["labeler"]).then_inc(index_in, 16)
            for dst, src in consts:
                sp.dma_start(dst, src).then_inc(const_in, 16)

            def load(u):
                for half in range(2):
                    need(sp, x_high, 2 * u + half - 1)
                    need(sp, x_low, 2 * u + half - 1)
                    sp.dma_start(x_raw[:, ks(half), :], a["x_t"][bass.ds(u, 1), :, ks(half), :].rearrange("o p k t -> (o p) k t")).then_inc(x_in[half], 16)
                need(sp, a_high, u)
                need(sp, a_low, u)
                for b in range(BPU):
                    lab = sp.value_load(index[0:1, bass.ds(u * BPU + b, 1)], min_val=0, max_val=LAB - 1)
                    sp.dma_start(a_raw[:, b, :, :], a["lora_a"][bass.ds(lab, 1), :, :, :].rearrange("o p k r -> (o p) k r")).then_inc(a_in, 16)

            def step(u, main, att, nxt):
                v = u - 1
                if nxt:
                    load(u + 1)
                if att:
                    sp.wait_ge(pv_out, 2 * v + 2)
                    sp.dma_start(attn_dram[bass.ds(v, 1), :, :].rearrange("o p c -> (o p) c"),
                                 attn[:, :, :, :].rearrange("p k b t -> p (k b t)")).then_inc(stored, 16)

            sp.wait_ge(index_in, 16)
            load(0)
            steps(sp, step)
            sp.wait_ge(stored, 16 * UNITS)

        @block.scalar
        def _(act):
            def split_x(u, half):
                act.wait_ge(x_in[half], 16 * (u + 1))
                need(act, half_done, 2 * u + half - 1)
                act.activation(x_h[:, ks(half), :], x_raw[:, ks(half), :], ACT.Copy).then_inc(x_high, 1)

            def split_a(u):
                act.wait_ge(a_in, 32 * (u + 1))
                need(act, half_done, 2 * u)
                act.activation(a_h[:, :, :].rearrange("p k (b r) -> p b k r", b=BPU), a_raw[:, :, :, :], ACT.Copy).then_inc(a_high, 1)

            def step(u, main, att, nxt):
                v = u - 1
                if att:
                    act.wait_ge(qkv_out, v + 1)
                    act.activation(v_hl[:, 0, :, :, :, :].rearrange("p q j h d -> p (q j h d)"), qkv[:, QK:QKV], ACT.Copy).then_inc(v_high, 1)
                    act.wait_ge(v_high, v + 1)
                    act.wait_ge(vb_zero, 2)
                    need(act, pv_done, 2 * v)
                    for b in range(BPU):
                        for h in range(2):
                            last = act.activation(diag(vb_h, b, h),
                                                  v_hl[b * SEQ:(b + 1) * SEQ, 0, :, :, h, :].bitcast(F32), ACT.Copy)
                    last.then_inc(vb_high, 1)
                    for q in range(QUADS):
                        act.wait_ge(qk_t, 3 * v + q + 1)
                        act.activation(q_h[:, :, q, :, :].rearrange("p b g t -> p g b t"),
                                       t_ps[:, q, :].rearrange("p (g b t) -> p g b t", g=GRP, b=BPU), ACT.Copy).then_inc(qk_high, 1)
                    act.wait_ge(qk_t, 3 * v + 3)
                    act.wait_ge(const_in, 16 * len(consts))
                    for c in range(4):
                        last = act.activation(k_h[:, :, :, c, :].rearrange("p q b t -> p (q b) t"), k_ps(), ACT.Copy, scale=hmask[:, c:c + 1])
                    last.then_inc(qk_high, 1)
                    for b in range(BPU):
                        act.wait_ge(s_sub, 2 * v + b + 1)
                        act.activation(prob[:, b, :, :, :], prob[:, b, :, :, :], ACT.Exp, scale=SCALE).then_inc(s_exp, 1)
                if nxt and main:
                    split_x(u + 1, 0)
                if att:
                    for b in range(BPU):
                        act.wait_ge(pt_done, 2 * v + b + 1)
                        act.activation(pt_h[:, :, :, :, :].rearrange("p q j g t -> p q (j g t)"), t_ps[:, :, :], ACT.Copy).then_inc(pt_high, 1)
                        act.wait_ge(pv_done, 2 * v + b + 1)
                        if b == 0:
                            need(act, stored, 16 * v)
                        act.activation(attn[:, :, b, :], s_ps[:, b, :].rearrange("p (k t) -> p k t", k=KT), ACT.Copy).then_inc(pv_out, 1)
                if main:
                    act.wait_ge(half_done, 2 * u + 2)
                    for b in range(BPU):
                        rows = slice(b * SEQ, (b + 1) * SEQ)
                        last = act.activation(low4[rows, :, :], bank[3][rows, b * LR:(b + 1) * LR].unsqueeze(1).to_broadcast([SEQ, 4, LR]), ACT.Copy, scale=LORA_SCALE)
                    last.then_inc(low_copied, 1)
                    act.wait_ge(low_t, u + 1)
                    act.activation(lows[:, :], bank[3][:, P:2 * P], ACT.Copy).then_inc(low_high, 1)
                if nxt:
                    split_x(u + 1, 1)
                    split_a(u + 1)

            act.wait_ge(const_in, 16 * len(consts))
            act.activation(mask_r[:, :], mask_f[:, 0:BANK], ACT.Copy)
            act.activation(mask_l[:, :], mask_f[:, BANK:BANK + P], ACT.Copy).then_inc(mask_ready, 1)
            split_x(0, 0)
            split_x(0, 1)
            split_a(0)
            steps(act, step)

        @block.gpsimd
        def _(pool):
            pool.memset(vb_h[:, :, :, :, :, :].bitcast(F32), 0.0).then_inc(vb_zero, 1)
            pool.memset(vb_l[:, :, :, :, :, :].bitcast(F32), 0.0).then_inc(vb_zero, 1)

            def split_x(u, half):
                pool.wait_ge(x_high, 2 * u + half + 1)
                pool.tensor_tensor(x_l[:, ks(half), :], x_raw[:, ks(half), :], x_h[:, ks(half), :].bitcast(F32), ALU.subtract).then_inc(x_low, 1)

            def split_a(u):
                pool.wait_ge(a_high, u + 1)
                pool.tensor_tensor(a_l[:, :, :].rearrange("p k (b r) -> p b k r", b=BPU), a_raw[:, :, :, :],
                                   a_h[:, :, :].bitcast(F32).rearrange("p k (b r) -> p b k r", b=BPU), ALU.subtract).then_inc(a_low, 1)

            def step(u, main, att, nxt):
                v = u - 1
                if att:
                    pool.wait_ge(rot_re, v + 1)
                    pool.tensor_tensor(roped[:, :, :, 0], roped[:, :, :, 0], rot_t[:, 0, :, :], ALU.subtract).then_inc(rotated, 1)
                    pool.wait_ge(rot_im, v + 1)
                    pool.tensor_tensor(roped[:, :, :, 1], roped[:, :, :, 1], rot_t[:, 1, :, :], ALU.add).then_inc(rotated, 1)
                    for b in range(BPU):
                        pool.wait_ge(s_inv, 2 * v + b + 1)
                        pool.tensor_tensor(prob[:, b, :, :, :].rearrange("p g c k -> p (g c) k"), prob[:, b, :, :, :].rearrange("p g c k -> p (g c) k"),
                                           sinv[:, b, :, :].rearrange("p g c -> p (g c)").unsqueeze(2).to_broadcast([P, 2 * KVH, SEQ]), ALU.mult).then_inc(s_norm, 1)
                        if nxt and b == 0:
                            split_x(u + 1, 0)
                elif nxt:
                    split_x(u + 1, 0)
                if nxt:
                    split_x(u + 1, 1)
                    split_a(u + 1)

            split_x(0, 0)
            split_x(0, 1)
            split_a(0)
            steps(pool, step)

        @block.vector
        def _(dve):
            def step(u, main, att, nxt):
                v = u - 1
                if att:
                    even = qkv[:, 0:QK].rearrange("p (h i two) -> p h i two", i=HD // 2, two=2)
                    bc = lambda t: t[:, :].unsqueeze(1).to_broadcast([P, NH, HD // 2])
                    dve.wait_ge(qkv_out, v + 1)
                    dve.wait_ge(const_in, 16 * len(consts))
                    need(dve, rotated, 2 * v)
                    need(dve, qk_t, 3 * v)
                    dve.tensor_tensor(roped[:, :, :, 0], even[:, :, :, 0], bc(cos), ALU.mult)
                    dve.tensor_tensor(rot_t[:, 0, :, :], even[:, :, :, 1], bc(sin), ALU.mult).then_inc(rot_re, 1)
                    dve.tensor_tensor(roped[:, :, :, 1], even[:, :, :, 0], bc(sin), ALU.mult)
                    dve.tensor_tensor(rot_t[:, 1, :, :], even[:, :, :, 1], bc(cos), ALU.mult).then_inc(rot_im, 1)
                    dve.wait_ge(v_high, v + 1)
                    dve.tensor_tensor(v_hl[:, 1, :, :, :, :].rearrange("p q j h d -> p (q j h d)"), qkv[:, QK:QKV],
                                      v_hl[:, 0, :, :, :, :].rearrange("p q j h d -> p (q j h d)").bitcast(F32), ALU.subtract).then_inc(v_low, 1)
                    dve.wait_ge(v_low, v + 1)
                    dve.wait_ge(vb_zero, 2)
                    need(dve, pv_done, 2 * v)
                    for b in range(BPU):
                        for h in range(2):
                            last = dve.tensor_copy(diag(vb_l, b, h), v_hl[b * SEQ:(b + 1) * SEQ, 1, :, :, h, :].bitcast(F32))
                    last.then_inc(vb_low, 1)
                    for q in range(QUADS):
                        dve.wait_ge(qk_high, 3 * v + q + 1)
                        dve.tensor_tensor(q_l[:, :, q, :, :].rearrange("p b g t -> p g b t"),
                                          t_ps[:, q, :].rearrange("p (g b t) -> p g b t", g=GRP, b=BPU),
                                          q_h[:, :, q, :, :].bitcast(F32).rearrange("p b g t -> p g b t"), ALU.subtract).then_inc(qk_low, 1)
                    dve.wait_ge(qk_high, 3 * v + 3)
                    for c in range(4):
                        last = dve.scalar_tensor_tensor(k_l[:, :, :, c, :].rearrange("p q b t -> p (q b) t"), k_ps(), hmask[:, c:c + 1],
                                                        k_h[:, :, :, c, :].bitcast(F32).rearrange("p q b t -> p (q b) t"), ALU.mult, ALU.subtract)
                    last.then_inc(qk_low, 1)
                    scores = s_ps[:, :, :].rearrange("p g (c k) -> p (g c) k", k=SEQ)
                    for b in range(BPU):
                        flat = prob[:, b, :, :, :].rearrange("p g c k -> p (g c) k")
                        row = lambda t: t[:, b, :, :].rearrange("p g c -> p (g c)")
                        dve.wait_ge(s_done, 2 * v + b + 1)
                        dve.tensor_reduce(row(smax), scores, AX.X, ALU.max).then_inc(s_max, 1)
                        dve.wait_ge(s_max, 2 * v + b + 1)
                        dve.tensor_tensor(flat, scores, row(smax).unsqueeze(2).to_broadcast([P, 2 * KVH, SEQ]), ALU.subtract).then_inc(s_sub, 1)
                    for b in range(BPU):
                        flat = prob[:, b, :, :, :].rearrange("p g c k -> p (g c) k")
                        row = lambda t: t[:, b, :, :].rearrange("p g c -> p (g c)")
                        dve.wait_ge(s_exp, 2 * v + b + 1)
                        dve.tensor_reduce(row(ssum), flat, AX.X, ALU.add).then_inc(s_sum, 1)
                        dve.wait_ge(s_sum, 2 * v + b + 1)
                        dve.reciprocal(row(sinv), row(ssum)).then_inc(s_inv, 1)
                    for b in range(BPU):
                        dve.wait_ge(pt_high, 2 * v + b + 1)
                        dve.tensor_tensor(pt_l[:, :, :, :, :].rearrange("p q j g t -> p q (j g t)"), t_ps[:, :, :],
                                          pt_h[:, :, :, :, :].bitcast(F32).rearrange("p q j g t -> p q (j g t)"), ALU.subtract).then_inc(pt_low, 1)
                if main:
                    dve.wait_ge(low_high, u + 1)
                    rows = slice(2 * LR, 4 * LR)
                    dve.tensor_tensor(lows[rows, :], bank[3][rows, P:2 * P], lows[rows, :].bitcast(F32), ALU.subtract).then_inc(low_ready, 1)
                    dve.wait_ge(qkv_done, u + 1)
                    need(dve, v_high, u)
                    need(dve, v_low, u)
                    need(dve, rot_im, u)
                    dve.wait_ge(const_in, 16 * len(consts))
                    for n in range(NCH):
                        cols = slice(n * BANK, (n + 1) * BANK)
                        last = dve.tensor_tensor(qkv[:, cols], bank[n][:, :], b_bc[:, cols], ALU.add)
                    last.then_inc(qkv_out, 1)

            steps(dve, step)

        @block.tensor
        def _(pe):
            def project(u, k):
                if k % HALF == 0:
                    half = k // HALF
                    pe.wait_ge(x_low, 2 * u + half + 1)
                    if k == 0:
                        pe.wait_ge(a_low, u + 1)
                        need(pe, qkv_out, u)
                for sx, wc, wa in ((x_h, p1_h, a_h), (x_h, p1_l, a_l), (x_l, p1_h, a_h)):
                    first, last = k == 0 and sx is x_h and wc is p1_h, k == KT - 1 and sx is x_l
                    for n in range(NCH):
                        pe.matmul(bank[n][:, :], sx[:, k, :], wc[:, n, k, :], start=first, stop=False)
                    mm = pe.matmul(bank[3][:, 0:BPU * LR], sx[:, k, :], wa[:, k, :], start=first, stop=last)
                if k % HALF == HALF - 1:
                    mm.then_inc(half_done, 1)

            def transpose_qk(v):
                pe.wait_ge(const_in, 16 * len(consts))
                pe.wait_ge(rotated, 2 * v + 2)
                need(pe, pt_low, 2 * v)
                flat = roped[:, :, :, :].rearrange("p h i two -> p (h i two)")
                for n in range(QK // P):
                    if n == 2 * GRP:
                        pe.wait_ge(qk_low, 3 * v + 1)
                    at = (n % GRP) * P
                    mm = pe.transpose(t_ps[:, (n // GRP) % 2, at:at + P], flat[:, n * P:(n + 1) * P], ident[:, :])
                    if n in (GRP - 1, 2 * GRP - 1, QK // P - 1):
                        mm.then_inc(qk_t, 1)

            def scores(v, b):
                if b == 0:
                    pe.wait_ge(qk_low, 3 * v + 3)
                    need(pe, pv_out, 2 * v)
                else:
                    pe.wait_ge(s_sub, 2 * v + 1)
                for g in range(2):
                    pe.matmul(s_ps[:, g, :], mask_l[:, :], mask_r[:, :], start=True, stop=False)
                    for q in range(QUADS):
                        o = s_ps[:, g, q * 4 * SEQ:(q + 1) * 4 * SEQ]
                        cols = slice(2 * g, 2 * g + 2)
                        for n, (qq, kk) in enumerate(((q_h, k_h), (q_h, k_l), (q_l, k_h))):
                            mm = pe.matmul(o, qq[:, b, q, cols, :].rearrange("p g t -> p (g t)"), kk[:, q, b, :, :].rearrange("p c t -> p (c t)"),
                                           start=False, stop=q == QUADS - 1 and n == 2)
                mm.then_inc(s_done, 1)

            def transpose_p(v, b):
                pe.wait_ge(s_norm, 2 * v + b + 1)
                if b == 1:
                    pe.wait_ge(pt_low, 2 * v + 1)
                for q in range(QUADS):
                    for j in range(2):
                        for g in range(2):
                            at = (j * 2 + g) * P
                            c = q * 4 + j * 2
                            mm = pe.transpose(t_ps[:, q, at:at + P], prob[:, b, g, c:c + 2, :].rearrange("p c k -> p (c k)"), ident[:, :])
                mm.then_inc(pt_done, 1)

            def attend(v, b):
                pe.wait_ge(pt_low, 2 * v + b + 1)
                if b == 0:
                    pe.wait_ge(vb_high, v + 1)
                    pe.wait_ge(vb_low, v + 1)
                    pe.wait_ge(s_sub, 2 * v + 2)
                n = 0
                for q in range(QUADS):
                    for j in range(2):
                        for vv, pp in ((vb_h, pt_h), (vb_h, pt_l), (vb_l, pt_h)):
                            mm = pe.matmul(s_ps[:, b, q * 4 * SEQ:(q + 1) * 4 * SEQ], vv[:, b, q, j, :, :].rearrange("p c d -> p (c d)"),
                                           pp[:, q, j, :, :].rearrange("p g t -> p (g t)"), start=n % 6 == 0, stop=n % 6 == 5)
                            n += 1
                mm.then_inc(pv_done, 1)

            def finish(u):
                pe.wait_ge(const_in, 16 * len(consts))
                pe.wait_ge(low_copied, u + 1)
                pe.transpose(bank[3][:, P:2 * P], low4[:, :, :].rearrange("p n r -> p (n r)"), ident[:, :]).then_inc(low_t, 1)
                pe.wait_ge(low_ready, u + 1)
                for n in range(NCH):
                    mm = pe.matmul(bank[n][:, :], lows[:, :], pb[:, n * BANK:(n + 1) * BANK], start=False, stop=True)
                mm.then_inc(qkv_done, 1)

            def step(u, main, att, nxt):
                v = u - 1
                plan = [(project, u, k) for k in range(KT)] if main else []
                if att:
                    other = [(3, (transpose_qk, v)), (4, (scores, v, 0)), (5, (scores, v, 1)), (6, (transpose_p, v, 0)),
                             (7, (attend, v, 0)), (7, (transpose_p, v, 1)), (8, (attend, v, 1))]
                    for at, what in reversed(other):
                        plan.insert(min(at, len(plan)) if main else 0, what)
                for what, *args in plan:
                    what(*args)
                if main:
                    finish(u)

            pe.wait_ge(mask_ready, 1)
            steps(pe, step)


def fold_ffn(nc, a, sem, attn_dram):
    with ExitStack() as keep:
        fr_h, fr_l = (keep.enter_context(nc.sbuf_tensor(n, [P, KT, FCOLS], F32R)) for n in ("fr_h", "fr_l"))
        g_h, g_l = (keep.enter_context(nc.sbuf_tensor(n, [P, FOUT], F32R)) for n in ("g_h", "g_l"))
        base_chunks = D // FCH
        with ExitStack() as st:
            def tb(name, shape, dt=F32R):
                return st.enter_context(nc.sbuf_tensor(name, shape, dt))

            w_h, w_l = tb("w2_h", [P, KT, D]), tb("w2_l", [P, KT, D])
            c_h, c_l = tb("c2_h", [P, 2, KT, FCH]), tb("c2_l", [P, 2, KT, FCH])
            raw = tb("raw2", [P, D], F32)

            def part(fr):
                return lambda i, ch: fr[:, i, ch * FCH:(ch + 1) * FCH] if ch < base_chunks else fr[:, i, FOUT:FCOLS]

            def up(g):
                return lambda ch: g[:, ch * FCH:(ch + 1) * FCH] if ch < base_chunks else g[:, D:FOUT]

            fold_program(nc, sem, "f2", st, a["w_2"], [a["last_t"][n] for n in range(base_chunks)] + [a["last_gate_t"]],
                         [FCH] * base_chunks + [GATED], raw, w_h, w_l, c_h, c_l, part(fr_h), part(fr_l),
                         a["b2_up"], ERS, up(g_h), lambda ch, src: [(up(g_l)(ch), up(g_h)(ch), src)])
        feed_forward(nc, a, sem, attn_dram, keep, fr_h, fr_l, g_h, g_l)


def feed_forward(nc, a, sem, attn_dram, keep, fr_h, fr_l, g_h, g_l):
    def sb(name, shape, dt=F32):
        return keep.enter_context(nc.sbuf_tensor(name, shape, dt))

    wo_h, wo_l = sb("wo_h", [P, KT, D], F32R), sb("wo_l", [P, KT, D], F32R)
    bf_h, bf_l = sb("bf_h", [P, D], F32R), sb("bf_l", [P, D], F32R)
    w_raw = sb("w_raw", [P, 2, KT * GATED])
    at_raw = sb("at_raw", [P, KT, P])
    at_h, at_l = sb("at_h", [P, KT, P], F32R), sb("at_l", [P, KT, P], F32R)
    x_raw = sb("x_tok", [P, D])
    x1, x1_out = sb("x1", [P, D]), sb("x1_out", [P, D])
    x1t_h, x1t_l = sb("x1t_h", [P, KT, P], F32R), sb("x1t_l", [P, KT, P], F32R)
    bo_bc, bb_bc = sb("bo_bc", [P, D]), sb("bb_bc", [P, D])
    ident = sb("ident4", [P, P])
    before = sb("before", [P, EXP, EXP])
    experts = sb("experts", [P, EXP])
    lang, lang_f = sb("lang", [P, UNITS], I32), sb("lang_f", [P, UNITS])
    lang_bias = sb("lang_bias", [P, UNITS, EXP])
    lg, ex, rank, pick, gate = (sb(n, [P, EXP]) for n in ("lg", "ex", "rank", "pick", "gate"))
    above, ties = sb("above", [P, EXP, EXP]), sb("ties", [P, EXP, EXP])
    top, total, share = sb("top", [P, 1]), sb("total", [P, 1]), sb("share", [P, 1])
    z = sb("z", [P, EXP, ER])
    zt_h, zt_l = sb("zt_h", [P, P], F32R), sb("zt_l", [P, P], F32R)
    w_ps = keep.enter_context(nc.psum_tensor("w_ps", [P, 2, BANK], F32))
    b_ps = keep.enter_context(nc.psum_tensor("b_ps", [P, 3, BANK], F32))
    x_ps = keep.enter_context(nc.psum_tensor("x_ps", [P, 2, BANK], F32))
    z_ps = keep.enter_context(nc.psum_tensor("z_ps", [P, BANK], F32))

    consts_in = sem("consts4_in")
    w_in = [sem("w4_in0"), sem("w4_in1")]
    w_high, w_low = sem("w4_high"), sem("w4_low")
    at_in = [sem("at_in0"), sem("at_in1")]
    x_in, x_bias = sem("xt_in"), sem("x_bias")
    at_high, at_low, wo_half = sem("at_high"), sem("at_low"), sem("wo_half")
    x1_ready, x1_t, x1_high, x1_low, x1_biased = (sem(n) for n in ("x1_ready", "x1_t", "x1_high", "x1_low", "x1_biased"))
    lang_step, f_done, up_done, base_done = sem("lang_step"), sem("f_done"), sem("up_done"), sem("base_done")
    route_step, route_exp, z_ready = sem("route_step"), sem("route_exp"), sem("z_ready")
    z_t, z_high, z_low = sem("z_t"), sem("z_high"), sem("z_low")
    out_ready, out_stored = sem("out_ready"), sem("out_stored")
    ROUTE_STEPS = 13
    consts = [(bo_bc[:, :], a["b_o"].partition_broadcast(P)), (bb_bc[:, :], a["b_base"].partition_broadcast(P)),
              (ident[:, :], a["ident"]), (before[:, :, :].rearrange("p e j -> p (e j)"), a["before"]), (experts[:, :], a["experts"])]
    consts += [(lang[b * SEQ:(b + 1) * SEQ, :], a["language"][b, :].partition_broadcast(SEQ)) for b in range(BPU)]
    weights = [(w_raw[:, k % 2, 0:D], wo_h[:, k, :], wo_l[:, k, :], a["wo_t"][:, k, :]) for k in range(KT)]
    weights += [(w_raw[:, 0, 0:D], bf_h[:, :], bf_l[:, :], a["bf_up"]),
                (w_raw[:, 1, :].rearrange("p (k c) -> p k c", k=KT), fr_h[:, :, D:FOUT], fr_l[:, :, D:FOUT], a["gate2_t"])]

    def steps(engine, step):
        step(0, True, False, True)
        with engine.Fori(1, UNITS - 1) as u:
            step(u, True, True, True)
        step(UNITS - 1, True, True, False)
        step(UNITS, False, True, False)

    def ks(half):
        return slice(half * HALF, (half + 1) * HALF)

    with nc.Block() as block:
        @block.sync
        def _(sp):
            for dst, src in consts:
                sp.dma_start(dst, src).then_inc(consts_in, 16)
            for n, (raw, _, _, src) in enumerate(weights):
                need(sp, w_low, n - 1)
                sp.dma_start(raw, src).then_inc(w_in[n % 2], 16)

            def load_attn(u):
                for half in range(2):
                    need(sp, at_high, 2 * u + half - 1)
                    need(sp, at_low, 2 * u + half - 1)
                    sp.dma_start(at_raw[:, ks(half), :], attn_dram[bass.ds(u, 1), :, half * HALF * P:(half + 1) * HALF * P]
                                 .rearrange("o p (k t) -> (o p) k t", k=HALF)).then_inc(at_in[half], 16)

            def load_x(u):
                need(sp, x1_ready, u)
                sp.dma_start(x_raw[:, :], a["x_tok"][bass.ds(u, 1), :, :].rearrange("o p d -> (o p) d")).then_inc(x_in, 16)

            def step(u, main, gating, nxt):
                v = u - 1
                if nxt:
                    load_attn(u + 1)
                    load_x(u + 1)
                if gating:
                    sp.wait_ge(out_ready, v + 1)
                    sp.dma_start(a["out"][bass.ds(v, 1), :, :].rearrange("o p d -> (o p) d"), x1_out[:, :]).then_inc(out_stored, 16)

            load_attn(0)
            load_x(0)
            steps(sp, step)
            sp.wait_ge(out_stored, 16 * UNITS)

        @block.scalar
        def _(act):
            for n, (raw, hi, _, _) in enumerate(weights):
                act.wait_ge(w_in[n % 2], 16 * (n // 2 + 1))
                act.activation(hi, raw, ACT.Copy).then_inc(w_high, 1)

            def split_attn(u, half):
                act.wait_ge(at_in[half], 16 * (u + 1))
                need(act, wo_half, 2 * u + half - 1)
                act.activation(at_h[:, ks(half), :], at_raw[:, ks(half), :], ACT.Copy).then_inc(at_high, 1)

            def gated(v, r):
                act.wait_ge(route_step, (v * 2 + r) * ROUTE_STEPS + 3)
                act.activation(ex[:, :], ex[:, :], ACT.Exp).then_inc(route_exp, 1)
                act.wait_ge(z_t, 2 * v + r + 1)
                act.activation(zt_h[:, :], z_ps[:, 0:P], ACT.Copy).then_inc(z_high, 1)

            def step(u, main, gating, nxt):
                v = u - 1
                if gating:
                    gated(v, 0)
                if nxt:
                    split_attn(u + 1, 0)
                if gating:
                    gated(v, 1)
                if main:
                    act.wait_ge(x1_t, u + 1)
                    act.activation(x1t_h[:, :, :].rearrange("p k t -> p (k t)"), x_ps[:, :, :].rearrange("p a c -> p (a c)"), ACT.Copy).then_inc(x1_high, 1)
                if nxt:
                    split_attn(u + 1, 1)

            split_attn(0, 0)
            split_attn(0, 1)
            steps(act, step)

        @block.gpsimd
        def _(pool):
            def split_attn(u, half):
                pool.wait_ge(at_high, 2 * u + half + 1)
                pool.tensor_tensor(at_l[:, ks(half), :], at_raw[:, ks(half), :], at_h[:, ks(half), :].bitcast(F32), ALU.subtract).then_inc(at_low, 1)

            def bias_x(u):
                pool.wait_ge(x_in, 16 * (u + 1))
                pool.tensor_tensor(x_raw[:, :], x_raw[:, :], bo_bc[:, :], ALU.add).then_inc(x_bias, 1)

            def step(u, main, gating, nxt):
                if nxt:
                    split_attn(u + 1, 0)
                if main:
                    pool.wait_ge(x1_ready, u + 1)
                    need(pool, out_stored, 16 * u)
                    pool.tensor_tensor(x1_out[:, :], x1[:, :], bb_bc[:, :], ALU.add).then_inc(x1_biased, 1)
                if nxt:
                    split_attn(u + 1, 1)
                    bias_x(u + 1)

            pool.wait_ge(consts_in, 16 * len(consts))
            split_attn(0, 0)
            split_attn(0, 1)
            bias_x(0)
            steps(pool, step)

        @block.vector
        def _(dve):
            for n, (raw, hi, lo, _) in enumerate(weights):
                dve.wait_ge(w_high, n + 1)
                dve.tensor_tensor(lo, raw, hi.bitcast(F32), ALU.subtract).then_inc(w_low, 1)
            dve.wait_ge(consts_in, 16 * len(consts))
            dve.tensor_copy(lang_f[:, :], lang[:, :]).then_inc(lang_step, 1)
            dve.wait_ge(lang_step, 1)
            dve.tensor_tensor(lang_bias[:, :, :], experts[:, :].unsqueeze(1).to_broadcast([P, UNITS, EXP]),
                              lang_f[:, :].unsqueeze(2).to_broadcast([P, UNITS, EXP]), ALU.is_equal).then_inc(lang_step, 1)
            dve.wait_ge(lang_step, 2)
            dve.tensor_scalar(lang_bias[:, :, :], lang_bias[:, :, :], LANG_BIAS, None, ALU.mult).then_inc(lang_step, 1)
            dve.wait_ge(lang_step, 3)

            def route(v, r):
                steps_before = (v * 2 + r) * ROUTE_STEPS
                count = [0]

                def link(instruction):
                    count[0] += 1
                    instruction.then_inc(route_step, 1)
                    dve.wait_ge(route_step, steps_before + count[0])

                at = r * GATED
                logits, down = b_ps[:, 2, at:at + EXP], b_ps[:, 2, at + EXP:at + GATED]
                if r == 0:
                    dve.wait_ge(f_done, v + 1)
                    link(dve.tensor_tensor(lg[:, :], logits, lang_bias[:, bass.ds(v, 1), :].rearrange("p o e -> p (o e)"), ALU.add))
                else:
                    dve.wait_ge(up_done, v + 1)
                    link(dve.tensor_copy(lg[:, :], logits))
                link(dve.tensor_reduce(top[:, :], lg[:, :], AX.X, ALU.max))
                link(dve.tensor_scalar(ex[:, :], lg[:, :], top[:, :], None, ALU.subtract))
                mine = lg[:, :].unsqueeze(2).to_broadcast([P, EXP, EXP])
                other = lg[:, :].unsqueeze(1).to_broadcast([P, EXP, EXP])
                link(dve.tensor_tensor(ties[:, :, :], other, mine, ALU.is_equal))
                link(dve.tensor_tensor(above[:, :, :], other, mine, ALU.is_gt))
                link(dve.tensor_tensor(ties[:, :, :], ties[:, :, :], before[:, :, :], ALU.mult))
                link(dve.tensor_tensor(above[:, :, :], above[:, :, :], ties[:, :, :], ALU.add))
                link(dve.tensor_reduce(rank[:, :], above[:, :, :], AX.X, ALU.add))
                dve.wait_ge(route_exp, 2 * v + r + 1)
                link(dve.scalar_tensor_tensor(pick[:, :], rank[:, :], 1.5, ex[:, :], ALU.is_lt, ALU.mult))
                link(dve.tensor_reduce(total[:, :], pick[:, :], AX.X, ALU.add))
                link(dve.reciprocal(share[:, :], total[:, :]))
                link(dve.tensor_scalar(gate[:, :], pick[:, :], share[:, :], MOE_SCALE, ALU.mult, ALU.mult))
                link(dve.tensor_tensor(z[:, :, :], down.rearrange("p (e r) -> p e r", e=EXP),
                                       gate[:, :].unsqueeze(2).to_broadcast([P, EXP, ER]), ALU.mult))
                assert count[0] == ROUTE_STEPS
                dve.wait_ge(z_high, 2 * v + r + 1)
                dve.tensor_tensor(zt_l[:, :], z_ps[:, 0:P], zt_h[:, :].bitcast(F32), ALU.subtract).then_inc(z_low, 1)

            def step(u, main, gating, nxt):
                v = u - 1
                if gating:
                    route(v, 0)
                    route(v, 1)
                if main:
                    dve.wait_ge(wo_half, 2 * u + 2)
                    dve.wait_ge(x_bias, u + 1)
                    need(dve, x1_biased, u)
                    need(dve, x1_t, u)
                    dve.tensor_tensor(x1[:, :], w_ps[:, :, :].rearrange("p a c -> p (a c)"), x_raw[:, :], ALU.add).then_inc(x1_ready, 1)
                if gating:
                    dve.wait_ge(base_done, v + 1)
                    dve.wait_ge(x1_biased, v + 1)
                    dve.tensor_tensor(x1_out[:, :], b_ps[:, 0:2, :].rearrange("p a c -> p (a c)"), x1_out[:, :], ALU.add).then_inc(out_ready, 1)
                if main:
                    dve.wait_ge(x1_high, u + 1)
                    dve.tensor_tensor(x1t_l[:, :, :].rearrange("p k t -> p (k t)"), x_ps[:, :, :].rearrange("p a c -> p (a c)"),
                                      x1t_h[:, :, :].rearrange("p k t -> p (k t)").bitcast(F32), ALU.subtract).then_inc(x1_low, 1)

            steps(dve, step)

        @block.tensor
        def _(pe):
            def project(u, k):
                if k % HALF == 0:
                    pe.wait_ge(at_low, 2 * u + k // HALF + 1)
                if k == 0:
                    need(pe, x1_ready, u)
                for sx, w in ((at_h, wo_h), (at_h, wo_l), (at_l, wo_h)):
                    for n in range(2):
                        mm = pe.matmul(w_ps[:, n, :], sx[:, k, :], w[:, k, n * BANK:(n + 1) * BANK],
                                       start=k == 0 and sx is at_h and w is wo_h, stop=k == KT - 1 and sx is at_l)
                if k % HALF == HALF - 1:
                    mm.then_inc(wo_half, 1)

            def transpose_z(v, r):
                pe.wait_ge(route_step, (v * 2 + r + 1) * ROUTE_STEPS)
                need(pe, z_low, 2 * v + r)
                pe.transpose(z_ps[:, 0:P], z[:, :, :].rearrange("p e r -> p (e r)"), ident[:, :]).then_inc(z_t, 1)

            def second_up(v):
                pe.wait_ge(z_low, 2 * v + 1)
                for n in (2, 0, 1):
                    cols = slice(n * BANK, min((n + 1) * BANK, FOUT))
                    o = b_ps[:, 2, GATED:2 * GATED] if n == 2 else b_ps[:, n, :]
                    for s, w in ((zt_h, g_h), (zt_h, g_l), (zt_l, g_h)):
                        mm = pe.matmul(o, s[:, :], w[:, cols], start=False, stop=n == 2 and s is zt_l, skip_group_check=n == 2)
                    if n == 2:
                        mm.then_inc(up_done, 1)

            def last_up(v):
                pe.wait_ge(z_low, 2 * v + 2)
                for n in range(2):
                    for s, w in ((zt_h, bf_h), (zt_h, bf_l), (zt_l, bf_h)):
                        mm = pe.matmul(b_ps[:, n, :], s[:, :], w[:, n * BANK:(n + 1) * BANK], start=False, stop=s is zt_l)
                mm.then_inc(base_done, 1)

            def transpose_x1(u):
                pe.wait_ge(x1_ready, u + 1)
                need(pe, x1_low, u)
                for k in range(KT):
                    at = (k % 4) * P
                    mm = pe.transpose(x_ps[:, k // 4, at:at + P], x1[:, k * P:(k + 1) * P], ident[:, :])
                mm.then_inc(x1_t, 1)

            def forward(u):
                pe.wait_ge(x1_low, u + 1)
                need(pe, out_ready, u)
                need(pe, route_step, 2 * u * ROUTE_STEPS)
                for k in range(KT):
                    for s, w in ((x1t_h, fr_h), (x1t_h, fr_l), (x1t_l, fr_h)):
                        for n in range(3):
                            cols = slice(n * BANK, min((n + 1) * BANK, FCOLS))
                            mm = pe.matmul(b_ps[:, n, 0:cols.stop - cols.start], s[:, k, :], w[:, k, cols],
                                           start=k == 0 and s is x1t_h and w is fr_h,
                                           stop=n == 2 and k == KT - 1 and s is x1t_l)
                mm.then_inc(f_done, 1)

            def step(u, main, gating, nxt):
                v = u - 1
                for k in range(KT):
                    if main:
                        project(u, k)
                    if gating and k == 3:
                        transpose_z(v, 0)
                    if gating and k == 4:
                        second_up(v)
                if gating:
                    transpose_z(v, 1)
                    last_up(v)
                if main:
                    transpose_x1(u)
                    forward(u)

            pe.wait_ge(consts_in, 16 * len(consts))
            pe.wait_ge(w_low, len(weights))
            steps(pe, step)


def kernel(**inputs):
    import concourse.bacc as bacc
    from concourse.bass_utils import run_bass_kernel_spmd

    arrays = layout({k: np.asarray(v) for k, v in inputs.items()})
    nc = bacc.Bacc("TRN2", target_bir_lowering=False, num_devices=1, dynamic_dma_scratch_size=1024)
    tensors = {n: nc.dram_tensor(f"in_{n}", v.shape, mybir.dt.from_np(v.dtype), kind="ExternalInput").ap() for n, v in arrays.items()}
    tensors["out"] = nc.dram_tensor("out", (UNITS, P, D), F32, kind="ExternalOutput").ap()
    build(nc, tensors)
    r = run_bass_kernel_spmd(nc, [{f"in_{n}": v for n, v in arrays.items()}], core_ids=[0])
    return r.results[0]["out"].reshape(BATCH, SEQ, D)


def layout(x):
    def by_k(w):
        return w.reshape(KT, P, -1).transpose(1, 0, 2)

    def heads_first(w):
        w = w.reshape(QUADS, 4, GRP, HD, -1)
        return w.transpose(0, 2, 1, 3, 4).reshape(HEADS * HD, -1)

    tok = x["x"].reshape(UNITS, P, D)
    w_qkv, nq = x["L0_attn_w_qkv"], HEADS * HD
    w_qkv = np.concatenate([heads_first(w_qkv[:nq]), w_qkv[nq:]])
    b_qkv = x["L0_attn_b_qkv"]
    b_qkv = np.concatenate([heads_first(b_qkv[:nq])[:, 0], b_qkv[nq:]])
    last = np.concatenate([x["L0_ffn_W_base"], x["L0_ffn_W_router"], x["L0_ffn_A"].reshape(ERS, D)])
    gate2 = np.concatenate([x["L0_cond2_Wr"], x["L0_cond2_A"].reshape(ERS, D)])
    last_t = by_k(last.T)
    pos = (np.arange(P) % SEQ).astype(np.float32)
    inv = np.float32(1.0) / np.float32(10000.0) ** (np.arange(0, HD, 2, dtype=np.float32) / np.float32(HD))
    ang = (pos[:, None] * inv[None, :]).astype(np.float32)
    mask_l = np.zeros((P, P), np.float32)
    mask_l[np.arange(P) % SEQ, np.arange(P)] = 1
    mask_r = np.zeros((P, KVH, SEQ), np.float32)
    mask_r[:SEQ] = np.where(np.arange(SEQ)[:, None] >= np.arange(SEQ)[None, :], 0.0, -1e20)[:, None, :]
    part = np.arange(P)
    out = {
        "x_t": tok.reshape(UNITS, P, KT, P).transpose(0, 3, 2, 1),
        "x_tok": tok,
        "labeler": x["itok_B_0_2"].reshape(1, BATCH),
        "language": x["itok_B_0_7"].reshape(UNITS, BPU).T,
        "w_cond": by_k(x["L0_cond_W"]),
        "wqkv_t": by_k(w_qkv.T).reshape(P, KT, QKV // FCH, FCH).transpose(2, 0, 1, 3),
        "b_qkv": b_qkv,
        "lora_a": x["L0_cond_lora_A"].reshape(LAB, KT, P, LR).transpose(0, 2, 1, 3),
        "lora_b": by_k(x["L0_cond_lora_B_w"]),
        "wo_t": by_k(heads_first(x["L0_attn_w_o"].T)),
        "b_o": x["L0_attn_b_o"],
        "w_2": by_k(x["L0_cond2_W"]),
        "b2_up": by_k(x["L0_cond2_B"].transpose(1, 0, 2).reshape(D, ERS)),
        "gate2_t": by_k(gate2.T),
        "last_t": last_t[:, :, :D].reshape(P, KT, D // FCH, FCH).transpose(2, 0, 1, 3),
        "last_gate_t": last_t[:, :, D:],
        "bf_up": x["L0_ffn_B"].transpose(0, 2, 1).reshape(ERS, D),
        "b_base": x["L0_ffn_b_base"],
        "cos": np.cos(ang).astype(np.float32),
        "sin": np.sin(ang).astype(np.float32),
        "ident": np.eye(P, dtype=np.float32),
        "mask_l": mask_l,
        "mask_r": mask_r.reshape(P, BANK),
        "hmask": (part[:, None] // HD == np.arange(4)[None, :]).astype(np.float32),
        "experts": np.broadcast_to(np.arange(EXP, dtype=np.float32), (P, EXP)),
        "before": np.broadcast_to(np.tril(np.ones((EXP, EXP), np.float32), -1).reshape(1, EXP * EXP), (P, EXP * EXP)),
    }
    return {n: np.ascontiguousarray(v) for n, v in out.items()}
```

```python
import numpy as np
import concourse.bass as bass
from concourse import mybir
from contextlib import ExitStack

F32 = mybir.dt.float32
F32R = mybir.dt.float32r
BF16 = mybir.dt.bfloat16
I32 = mybir.dt.int32
ALU = mybir.AluOpType
ACT = mybir.ActivationFunctionType
AX = mybir.AxisListType

P = 128
BATCH, SEQ, D = 32, 64, 1024
TOK = BATCH * SEQ
UNITS = TOK // P
BPU = P // SEQ
KT = D // P
HEADS, KVH, HD = 32, 8, 32
GRP = HEADS // KVH
QUADS = KVH // 4
QKV = (HEADS + 2 * KVH) * HD
QK = (HEADS + KVH) * HD
BANK = 512
NCH = QKV // BANK
LAB, LR = 5, 32
EXP, ER = 8, 16
ERS = EXP * ER
GATED = EXP + ERS
FOUT = D + GATED
FCOLS = FOUT + GATED
FCH = 256
SCALE = float(HD) ** -0.5
LORA_SCALE = 0.5
MOE_SCALE = 2.0
LANG_BIAS = 5.0
HALF = KT // 2


def need(engine, semaphore, value):
    if isinstance(value, int) and value <= 0:
        return
    engine.wait_ge(semaphore, value)


def build(nc, a):
    with ExitStack() as ctx:
        names = {}

        def sem(name):
            if name not in names:
                names[name] = ctx.enter_context(nc.semaphore(name))
            return names[name]

        attn_dram = nc.dram_tensor("attn_scratch", (UNITS, P, KT * P), F32, kind="Internal").ap()
        ring = ctx.enter_context(nc.sbuf_tensor("ring", [P, 4, D], F32))
        fold_qkv(nc, a, sem, attn_dram, ring)
        fold_ffn(nc, a, sem, attn_dram, ring)


def fold_qkv(nc, a, sem, attn_dram, ring):
    with ExitStack() as keep:
        def sb(name, shape, dt=F32, stack=keep):
            return stack.enter_context(nc.sbuf_tensor(name, shape, dt))

        with nc.sbuf_tensor("w_raw", [P, KT, D], F32) as w_raw:
            pass
        p1_h = sb("p1_h", [P, NCH, KT, BANK], F32R)
        p1_l = sb("p1_l", [P, NCH, KT, BANK], F32R)
        pb = sb("pb", [P, QKV], F32R)
        with ExitStack() as st:
            w_h, w_l = sb("w_h", [P, KT, D], F32R, st), sb("w_l", [P, KT, D], F32R, st)
            c_h, c_l = sb("c_h", [P, 2, KT, FCH], F32R, st), sb("c_l", [P, 2, KT, FCH], F32R, st)

            def part(p1):
                return lambda i, j, e, w: p1[:, bass.ds(j, 1), i, e * FCH:e * FCH + w].rearrange("p o c -> p (o c)")

            def up(j, e, w):
                return pb[:, bass.ds((2 * j + e) * FCH, w)]

            def low_rows(j, e, w, src):
                for r in (slice(LR, 2 * LR), slice(3 * LR, 4 * LR)):
                    out = up(j, e, w)[r]
                    yield out, out, src[r]

            fold_program(nc, sem, "f1", st, ring, a["w_cond"], a["wqkv_t"], FCH, w_raw, w_h, w_l, c_h, c_l,
                         part(p1_h), part(p1_l), a["lora_b"], LR, up, low_rows, lambda sp: None, False)
        attention(nc, a, sem, attn_dram, ring, keep, p1_h, p1_l, pb)


def start_fold(sp, sem, tag, ring, c_dram, lb_dram, lr):
    sp.dma_start(ring[:, 2, 0:KT * lr].rearrange("p (k r) -> p k r", k=KT), lb_dram).then_inc(sem(f"{tag}_lb_loaded"), 16)
    for h in range(2):
        load_chunk(sp, sem, tag, ring, c_dram, 0, h)


def load_chunk(sp, sem, tag, ring, c_dram, ch, h):
    sp.dma_start(ring[:, h, :].rearrange("p (k c) -> p k c", k=HALF),
                 c_dram[bass.ds(ch, 1), :, h * HALF:(h + 1) * HALF, :].rearrange("o p k c -> (o p) k c")).then_inc(sem(f"{tag}_chunk_loaded{h}"), 16)


def fold_program(nc, sem, tag, st, ring, w_dram, c_dram, last_width, w_raw, w_h, w_l, c_h, c_l, out_h, out_l,
                 lb_dram, lr, lora_h, lora_l, at_end, started):
    chunks = c_dram.shape[0]
    looped = (chunks - 1) // 2 * 2
    lb_raw = ring[:, 2, 0:KT * lr].rearrange("p (k r) -> p k r", k=KT)
    lb_h = st.enter_context(nc.sbuf_tensor(f"{tag}_lb_h", [P, KT, P], F32R))
    lb_l = st.enter_context(nc.sbuf_tensor(f"{tag}_lb_l", [P, KT, P], F32R))
    BANKS = 3
    ps = [st.enter_context(nc.psum_tensor(f"{tag}_ps{n}", [P, BANK], F32)) for n in range(BANKS)]
    lb_loaded, lb_high, lb_low = sem(f"{tag}_lb_loaded"), sem(f"{tag}_lb_high"), sem(f"{tag}_lb_low")
    w_loaded = [sem(f"{tag}_w_loaded{k}") for k in range(KT)]
    w_high, w_low = sem(f"{tag}_w_high"), sem(f"{tag}_w_low")
    chunk_loaded = [sem(f"{tag}_chunk_loaded{h}") for h in range(2)]
    chunk_high, chunk_low = sem(f"{tag}_chunk_high"), sem(f"{tag}_chunk_low")
    done = sem(f"{tag}_tile_done")
    out_high, bank_free = sem(f"{tag}_out_high"), sem(f"{tag}_bank_free")
    tiles = KT + 1
    assert tiles % BANKS == 0
    reps = P // lr

    def steps(engine, step):
        with engine.Fori(0, looped // 2) as j:
            for e in range(2):
                step(j, e, FCH, True)
        for ch in range(looped, chunks):
            step(ch // 2, ch % 2, last_width if ch == chunks - 1 else FCH, ch + 1 < chunks)

    def half(h):
        return slice(h * HALF, (h + 1) * HALF)

    def raw_chunk(h):
        return ring[:, h, :].rearrange("p (k c) -> p k c", k=HALF)

    with nc.Block() as block:
        @block.sync
        def _(sp):
            if not started:
                start_fold(sp, sem, tag, ring, c_dram, lb_dram, lr)
            for k in range(KT):
                sp.dma_start(w_raw[:, k, :], w_dram[:, k, :]).then_inc(w_loaded[k], 16)

            def step(j, e, width, nxt):
                if nxt:
                    ch = 2 * j + e + 1
                    for h in range(2):
                        sp.wait_ge(chunk_low, 2 * ch - 1 + h)
                        load_chunk(sp, sem, tag, ring, c_dram, ch, h)

            steps(sp, step)
            at_end(sp)

        @block.scalar
        def _(act):
            def split_chunk(ch, e):
                for h in range(2):
                    act.wait_ge(chunk_loaded[h], 16 * (ch + 1))
                    act.activation(c_h[:, e, half(h), :], raw_chunk(h), ACT.Copy).then_inc(chunk_high, 1)

            split_chunk(0, 0)
            for k in range(KT):
                act.wait_ge(w_loaded[k], 16)
                act.activation(w_h[:, k, :], w_raw[:, k, :], ACT.Copy).then_inc(w_high, 1)
            act.wait_ge(lb_loaded, 16)
            for r in range(reps):
                last = act.activation(lb_h[:, :, r * lr:(r + 1) * lr], lb_raw, ACT.Copy)
            last.then_inc(lb_high, 1)

            def step(j, e, width, nxt):
                ch = 2 * j + e
                for i in range(tiles):
                    act.wait_ge(done, ch * tiles + i + 1)
                    dst = out_h(i, j, e, width) if i < KT else lora_h(j, e, width)
                    act.activation(dst, ps[i % BANKS][:, 0:width], ACT.Copy).then_inc(out_high, 1)
                    if i == 0 and nxt:
                        split_chunk(ch + 1, 1 - e)

            steps(act, step)

        @block.vector
        def _(dve):
            def split_chunk(ch, e):
                for h in range(2):
                    dve.wait_ge(chunk_high, 2 * ch + h + 1)
                    dve.tensor_tensor(c_l[:, e, half(h), :], raw_chunk(h), c_h[:, e, half(h), :].bitcast(F32), ALU.subtract).then_inc(chunk_low, 1)

            dve.sem_inc(bank_free, BANKS)
            split_chunk(0, 0)
            for k in range(KT):
                dve.wait_ge(w_high, k + 1)
                dve.tensor_tensor(w_l[:, k, :], w_raw[:, k, :], w_h[:, k, :].bitcast(F32), ALU.subtract).then_inc(w_low, 1)
            dve.wait_ge(lb_high, 1)
            for r in range(reps):
                rs = slice(r * lr, (r + 1) * lr)
                last = dve.tensor_tensor(lb_l[:, :, rs], lb_raw, lb_h[:, :, rs].bitcast(F32), ALU.subtract)
            last.then_inc(lb_low, 1)

            def step(j, e, width, nxt):
                ch = 2 * j + e
                for i in range(tiles):
                    dve.wait_ge(out_high, ch * tiles + i + 1)
                    src = ps[i % BANKS][:, 0:width]
                    pairs = [(out_l(i, j, e, width), out_h(i, j, e, width), src)] if i < KT else lora_l(j, e, width, src)
                    for lo, hi, s in pairs:
                        last = dve.tensor_tensor(lo, s, hi.bitcast(F32), ALU.subtract)
                    last.then_inc(bank_free, 1)
                    if i == 0 and nxt:
                        split_chunk(ch + 1, 1 - e)

            steps(dve, step)

        @block.tensor
        def _(pe):
            def step(j, e, width, nxt):
                ch = 2 * j + e
                pe.wait_ge(chunk_low, 2 * ch + 2)
                for i in range(tiles):
                    pe.wait_ge(bank_free, ch * tiles + i + 1)
                    if i == KT:
                        pe.wait_ge(lb_low, 1)
                    o = ps[i % BANKS][:, 0:width]
                    for k in range(KT):
                        if i == 0:
                            pe.wait_ge(w_low, k + 1)
                        cols = slice(i * P, (i + 1) * P)
                        sh, sl = (w_h[:, k, cols], w_l[:, k, cols]) if i < KT else (lb_h[:, k, :], lb_l[:, k, :])
                        pe.matmul(o, sh, c_h[:, e, k, 0:width], start=k == 0, stop=False)
                        pe.matmul(o, sh, c_l[:, e, k, 0:width], start=False, stop=False)
                        mm = pe.matmul(o, sl, c_h[:, e, k, 0:width], start=False, stop=k == KT - 1)
                    mm.then_inc(done, 1)

            steps(pe, step)


def attention(nc, a, sem, attn_dram, ring, keep, p1_h, p1_l, pb):
    def sb(name, shape, dt=F32):
        return keep.enter_context(nc.sbuf_tensor(name, shape, dt))

    x_raw = sb("x_raw", [P, KT, P])
    x_h, x_l = sb("x_h", [P, KT, P], F32R), sb("x_l", [P, KT, P], F32R)
    a_raw = sb("a_raw", [P, BPU, KT, LR])
    a_h, a_l = sb("a_h", [P, KT, BPU * LR], F32R), sb("a_l", [P, KT, BPU * LR], F32R)
    low4 = sb("low4", [P, 4, LR])
    lows = sb("lows", [P, P], F32R)
    qkv = sb("qkv", [P, QKV])
    b_bc = sb("b_bc", [P, QKV])
    NH = HEADS + KVH
    rot_t = sb("rot_t", [P, 2, NH, HD // 2])
    roped = sb("roped", [P, NH, HD // 2, 2])
    q_h, q_l = (sb(n, [P, BPU, QUADS * GRP, SEQ], F32R) for n in ("q_h", "q_l"))
    keys = sb("keys", [P, QUADS * P])
    k_h, k_l = (sb(n, [P, QUADS, BPU, 4, SEQ], F32R) for n in ("k_h", "k_l"))
    v_hl = sb("v_hl", [P, 2, QUADS, 2, 2, HD], F32R)
    vb_h, vb_l = (sb(n, [P, BPU, QUADS, 2, 4, HD], F32R) for n in ("vb_h", "vb_l"))
    prob = sb("prob", [P, BPU, 2, KVH, SEQ])
    smax, ssum, sinv = (sb(n, [P, BPU, 2, KVH]) for n in ("smax", "ssum", "sinv"))
    pt_h, pt_l = (sb(n, [P, QUADS, 2, 2, P], F32R) for n in ("pt_h", "pt_l"))
    attn = sb("attn", [P, KT, BPU, SEQ])
    cos, sin = sb("cos", [P, HD // 2]), sb("sin", [P, HD // 2])
    hmask = sb("hmask", [P, 4])
    ident = sb("ident", [P, P])
    mask_l = sb("mask_l", [P, P], BF16)
    mask_r = sb("mask_r", [P, BANK], BF16)
    mask_f = prob[:, 0, :, :, :].rearrange("p g c k -> p (g c k)")
    index = sb("index", [1, BATCH], I32)
    bank = [keep.enter_context(nc.psum_tensor(f"bank{n}", [P, BANK], F32)) for n in range(4)]
    s_ps = keep.enter_context(nc.psum_tensor("s_ps", [P, 2, BANK], F32))
    t_ps = keep.enter_context(nc.psum_tensor("t_ps", [P, 2, BANK], F32))

    const_in, index_in, mask_ready = sem("const_in"), sem("index_in"), sem("mask_ready")
    x_in = [sem("x_in0"), sem("x_in1")]
    a_in = sem("a_in")
    x_high, x_low, a_high, a_low = sem("x_high"), sem("x_low"), sem("a_high"), sem("a_low")
    half_done = sem("half_done")
    low_copied, low_t, low_high, low_ready = sem("low_copied"), sem("low_t"), sem("low_high"), sem("low_ready")
    qkv_done, qkv_out = sem("qkv_done"), sem("qkv_out")
    bank_out, low_done = sem("bank_out"), sem("low_done")
    rot_re, rot_im, rotated = sem("rot_re"), sem("rot_im"), sem("rotated")
    qk_t, qk_high, qk_low = sem("qk_t"), sem("qk_high"), sem("qk_low")
    k_out, k_high, k_low = sem("k_out"), sem("k_high"), sem("k_low")
    v_high, v_low, vb_zero, vb_high, vb_low = (sem(n) for n in ("v_high", "v_low", "vb_zero", "vb_high", "vb_low"))
    s_done, s_max, s_sub, s_exp, s_sum, s_inv, s_norm = (
        sem(n) for n in ("s_done", "s_max", "s_sub", "s_exp", "s_sum", "s_inv", "s_norm"))
    pt_done, pt_high, pt_low = sem("pt_done"), sem("pt_high"), sem("pt_low")
    pv_done, pv_out, stored = sem("pv_done"), sem("pv_out"), sem("attn_stored")
    consts = [(b_bc[:, :], a["b_qkv"].partition_broadcast(P)), (cos[:, :], a["cos"]), (sin[:, :], a["sin"]),
              (hmask[:, :], a["hmask"]), (ident[:, :], a["ident"]), (mask_f[:, BANK:BANK + P], a["mask_l"]),
              (mask_f[:, 0:BANK], a["mask_r"])]

    def k_tiles():
        return keys[:, :].rearrange("p (n t) -> p n t", t=SEQ)

    def q_ps(turn, at, n):
        return t_ps[:, turn, at * P:(at + n) * P].rearrange("p (n b t) -> p n b t", n=n, b=BPU)

    def diag(vb, b, h):
        flat = vb[h * SEQ:(h + 1) * SEQ, b, :, :, :, :].rearrange("p q j c d -> p q (j c d)")
        return flat.rearrange("p q (m d) -> p q m d", d=HD)[:, :, h:h + 7:6, :]

    TURNS = [(0, ["k0", "k1", 0, 1]), (1, [2, 3, 4, 5]), (0, [6, 7])]

    def steps(engine, step):
        step(0, True, False, False, True)
        step(1, True, True, False, True)
        with engine.Fori(2, UNITS - 1) as u:
            step(u, True, True, True, True)
        step(UNITS - 1, True, True, True, False)
        step(UNITS, False, True, True, False)
        step(UNITS + 1, False, False, True, False)

    def ks(half):
        return slice(half * HALF, (half + 1) * HALF)

    with nc.Block() as block:
        @block.sync
        def _(sp):
            def load_x(u):
                for half in range(2):
                    need(sp, x_low, 2 * u + half - 1)
                    sp.dma_start(x_raw[:, ks(half), :], a["x_t"][bass.ds(u, 1), :, ks(half), :].rearrange("o p k t -> (o p) k t")).then_inc(x_in[half], 16)

            def load_a(u):
                need(sp, a_low, u)
                for b in range(BPU):
                    lab = sp.value_load(index[0:1, bass.ds(u * BPU + b, 1)], min_val=0, max_val=LAB - 1)
                    sp.dma_start(a_raw[:, b, :, :], a["lora_a"][bass.ds(lab, 1), :, :, :].rearrange("o p k r -> (o p) k r")).then_inc(a_in, 16)

            def step(u, main, score, value, nxt):
                w = u - 2
                if nxt:
                    load_x(u + 1)
                    load_a(u + 1)
                if value:
                    sp.wait_ge(pv_out, 2 * w + 2)
                    sp.dma_start(attn_dram[bass.ds(w, 1), :, :].rearrange("o p c -> (o p) c"),
                                 attn[:, :, :, :].rearrange("p k b t -> p (k b t)")).then_inc(stored, 16)

            sp.dma_start(index[:, :], a["labeler"]).then_inc(index_in, 16)
            load_x(0)
            sp.wait_ge(index_in, 16)
            load_a(0)
            for dst, src in consts:
                sp.dma_start(dst, src).then_inc(const_in, 16)
            start_fold(sp, sem, "f2", ring, a["last_t"], a["b2_up"], ERS)
            steps(sp, step)
            sp.wait_ge(stored, 16 * UNITS)

        @block.scalar
        def _(act):
            def split_x(u, half):
                act.wait_ge(x_in[half], 16 * (u + 1))
                need(act, half_done, 2 * u + half - 1)
                act.activation(x_h[:, ks(half), :], x_raw[:, ks(half), :], ACT.Copy).then_inc(x_high, 1)

            def split_a(u):
                act.wait_ge(a_in, 32 * (u + 1))
                need(act, low_done, u)
                act.activation(a_h[:, :, :].rearrange("p k (b r) -> p b k r", b=BPU), a_raw[:, :, :, :], ACT.Copy).then_inc(a_high, 1)

            def queries(v, turn, at, n0, n1):
                return act.activation(q_h[:, :, n0:n1, :].rearrange("p b n t -> p n b t"), q_ps(turn, at, n1 - n0), ACT.Copy)

            def values_out(w, b):
                act.wait_ge(pv_done, 2 * w + b + 1)
                if b == 0:
                    need(act, stored, 16 * w)
                act.activation(attn[:, :, b, :], s_ps[:, b, :].rearrange("p (k t) -> p k t", k=KT), ACT.Copy).then_inc(pv_out, 1)

            def probs_high(w, b):
                act.wait_ge(pt_done, 2 * w + b + 1)
                act.activation(pt_h[:, :, :, :, :].rearrange("p q j g t -> p q (j g t)"), t_ps[:, :, :], ACT.Copy).then_inc(pt_high, 1)

            def step(u, main, score, value, nxt):
                v, w = u - 1, u - 2
                if value:
                    probs_high(w, 0)
                if score:
                    act.wait_ge(qkv_out, v + 1)
                    act.activation(v_hl[:, 0, :, :, :, :].rearrange("p q j h d -> p (q j h d)"), qkv[:, QK:QKV], ACT.Copy).then_inc(v_high, 1)
                if value:
                    values_out(w, 0)
                    probs_high(w, 1)
                    values_out(w, 1)
                if score:
                    act.wait_ge(qk_t, 3 * v + 1)
                    need(act, k_low, v)
                    act.activation(keys[:, :], t_ps[:, 0, 0:QUADS * P], ACT.Copy).then_inc(k_out, 1)
                    queries(v, 0, 2, 0, 2).then_inc(qk_high, 1)
                    act.wait_ge(qk_t, 3 * v + 2)
                    queries(v, 1, 0, 2, 6).then_inc(qk_high, 1)
                    act.wait_ge(k_out, v + 1)
                    for c in range(4):
                        last = act.activation(k_h[:, :, :, c, :].rearrange("p q b t -> p (q b) t"), k_tiles(), ACT.Copy, scale=hmask[:, c:c + 1])
                    last.then_inc(k_high, 1)
                    act.wait_ge(qk_t, 3 * v + 3)
                    queries(v, 0, 0, 6, 8).then_inc(qk_high, 1)
                    act.wait_ge(v_high, v + 1)
                    act.wait_ge(vb_zero, 2)
                    need(act, pv_done, 2 * v)
                    for b in range(BPU):
                        for h in range(2):
                            last = act.activation(diag(vb_h, b, h), v_hl[b * SEQ:(b + 1) * SEQ, 0, :, :, h, :].bitcast(F32), ACT.Copy)
                    last.then_inc(vb_high, 1)
                if nxt:
                    split_x(u + 1, 0)
                if score:
                    for b in range(BPU):
                        act.wait_ge(s_sub, 2 * v + b + 1)
                        act.activation(prob[:, b, :, :, :], prob[:, b, :, :, :], ACT.Exp, scale=SCALE).then_inc(s_exp, 1)
                if main:
                    act.wait_ge(low_done, u + 1)
                    for b in range(BPU):
                        rows = slice(b * SEQ, (b + 1) * SEQ)
                        last = act.activation(low4[rows, :, :], bank[3][rows, b * LR:(b + 1) * LR].unsqueeze(1).to_broadcast([SEQ, 4, LR]), ACT.Copy, scale=LORA_SCALE)
                    last.then_inc(low_copied, 1)
                if nxt:
                    split_a(u + 1)
                if main:
                    act.wait_ge(low_t, u + 1)
                    act.activation(lows[:, :], bank[3][:, P:2 * P], ACT.Copy).then_inc(low_high, 1)
                if nxt:
                    split_x(u + 1, 1)

            split_x(0, 0)
            split_a(0)
            split_x(0, 1)
            act.wait_ge(const_in, 16 * len(consts))
            act.activation(mask_r[:, :], mask_f[:, 0:BANK], ACT.Copy)
            act.activation(mask_l[:, :], mask_f[:, BANK:BANK + P], ACT.Copy).then_inc(mask_ready, 1)
            steps(act, step)

        @block.gpsimd
        def _(pool):
            pool.memset(vb_h[:, :, :, :, :, :].bitcast(F32), 0.0).then_inc(vb_zero, 1)
            pool.memset(vb_l[:, :, :, :, :, :].bitcast(F32), 0.0).then_inc(vb_zero, 1)

            def split_x(u, half):
                pool.wait_ge(x_high, 2 * u + half + 1)
                pool.tensor_tensor(x_l[:, ks(half), :], x_raw[:, ks(half), :], x_h[:, ks(half), :].bitcast(F32), ALU.subtract).then_inc(x_low, 1)

            def split_a(u):
                pool.wait_ge(a_high, u + 1)
                pool.tensor_tensor(a_l[:, :, :].rearrange("p k (b r) -> p b k r", b=BPU), a_raw[:, :, :, :],
                                   a_h[:, :, :].bitcast(F32).rearrange("p k (b r) -> p b k r", b=BPU), ALU.subtract).then_inc(a_low, 1)

            def normalise(v, b):
                pool.wait_ge(s_inv, 2 * v + b + 1)
                rows = prob[:, b, :, :, :].rearrange("p g c k -> p (g c) k")
                pool.tensor_tensor(rows, rows, sinv[:, b, :, :].rearrange("p g c -> p (g c)").unsqueeze(2).to_broadcast([P, 2 * KVH, SEQ]),
                                   ALU.mult).then_inc(s_norm, 1)

            def step(u, main, score, value, nxt):
                v = u - 1
                if score:
                    pool.wait_ge(rot_re, v + 1)
                    pool.tensor_tensor(roped[:, :, :, 0], roped[:, :, :, 0], rot_t[:, 0, :, :], ALU.subtract).then_inc(rotated, 1)
                    pool.wait_ge(rot_im, v + 1)
                    pool.tensor_tensor(roped[:, :, :, 1], roped[:, :, :, 1], rot_t[:, 1, :, :], ALU.add).then_inc(rotated, 1)
                if nxt:
                    split_x(u + 1, 0)
                if score:
                    normalise(v, 0)
                if nxt:
                    split_a(u + 1)
                    split_x(u + 1, 1)
                if score:
                    normalise(v, 1)

            split_x(0, 0)
            split_a(0)
            split_x(0, 1)
            steps(pool, step)

        @block.vector
        def _(dve):
            def rotate(v, part):
                pairs = qkv[:, 0:QK].rearrange("p (h i two) -> p h i two", i=HD // 2, two=2)
                for n, (dst, table) in enumerate(((roped[:, :, :, part], (cos, sin)[part]), (rot_t[:, part, :, :], (sin, cos)[part]))):
                    last = dve.tensor_tensor(dst, pairs[:, :, :, n], table[:, :].unsqueeze(1).to_broadcast([P, NH, HD // 2]), ALU.mult)
                last.then_inc((rot_re, rot_im)[part], 1)

            def probs_low(w, b):
                dve.wait_ge(pt_high, 2 * w + b + 1)
                dve.tensor_tensor(pt_l[:, :, :, :, :].rearrange("p q j g t -> p q (j g t)"), t_ps[:, :, :],
                                  pt_h[:, :, :, :, :].bitcast(F32).rearrange("p q j g t -> p q (j g t)"), ALU.subtract).then_inc(pt_low, 1)

            def queries(v, turn, at, n0, n1):
                dve.tensor_tensor(q_l[:, :, n0:n1, :].rearrange("p b n t -> p n b t"), q_ps(turn, at, n1 - n0),
                                  q_h[:, :, n0:n1, :].bitcast(F32).rearrange("p b n t -> p n b t"), ALU.subtract).then_inc(qk_low, 1)

            def step(u, main, score, value, nxt):
                v, w = u - 1, u - 2
                if value:
                    probs_low(w, 0)
                if score:
                    dve.wait_ge(qkv_out, v + 1)
                    dve.wait_ge(const_in, 16 * len(consts))
                    need(dve, rotated, 2 * v)
                    need(dve, qk_t, 3 * v)
                    rotate(v, 0)
                    rotate(v, 1)
                    dve.wait_ge(v_high, v + 1)
                    dve.tensor_tensor(v_hl[:, 1, :, :, :, :].rearrange("p q j h d -> p (q j h d)"), qkv[:, QK:QKV],
                                      v_hl[:, 0, :, :, :, :].rearrange("p q j h d -> p (q j h d)").bitcast(F32), ALU.subtract).then_inc(v_low, 1)
                if value:
                    probs_low(w, 1)
                if score:
                    dve.wait_ge(qk_high, 3 * v + 1)
                    queries(v, 0, 2, 0, 2)
                    dve.wait_ge(qk_high, 3 * v + 2)
                    queries(v, 1, 0, 2, 6)
                    dve.wait_ge(k_high, v + 1)
                    for c in range(4):
                        last = dve.scalar_tensor_tensor(k_l[:, :, :, c, :].rearrange("p q b t -> p (q b) t"), k_tiles(), hmask[:, c:c + 1],
                                                        k_h[:, :, :, c, :].bitcast(F32).rearrange("p q b t -> p (q b) t"), ALU.mult, ALU.subtract)
                    last.then_inc(k_low, 1)
                    dve.wait_ge(qk_high, 3 * v + 3)
                    queries(v, 0, 0, 6, 8)
                    dve.wait_ge(v_low, v + 1)
                    dve.wait_ge(vb_zero, 2)
                    need(dve, pv_done, 2 * v)
                    for b in range(BPU):
                        for h in range(2):
                            last = dve.tensor_copy(diag(vb_l, b, h), v_hl[b * SEQ:(b + 1) * SEQ, 1, :, :, h, :].bitcast(F32))
                    last.then_inc(vb_low, 1)
                    scores = s_ps[:, :, :].rearrange("p g (c k) -> p (g c) k", k=SEQ)

                    def flat(b):
                        return prob[:, b, :, :, :].rearrange("p g c k -> p (g c) k")

                    def row(t, b):
                        return t[:, b, :, :].rearrange("p g c -> p (g c)")

                    def less_max(b):
                        dve.wait_ge(s_done, 2 * v + b + 1)
                        dve.tensor_reduce(row(smax, b), scores, AX.X, ALU.max).then_inc(s_max, 1)
                        dve.wait_ge(s_max, 2 * v + b + 1)
                        dve.tensor_tensor(flat(b), scores, row(smax, b).unsqueeze(2).to_broadcast([P, 2 * KVH, SEQ]), ALU.subtract).then_inc(s_sub, 1)

                    def inverse_sum(b):
                        dve.wait_ge(s_exp, 2 * v + b + 1)
                        dve.tensor_reduce(row(ssum, b), flat(b), AX.X, ALU.add).then_inc(s_sum, 1)
                        dve.wait_ge(s_sum, 2 * v + b + 1)
                        dve.reciprocal(row(sinv, b), row(ssum, b)).then_inc(s_inv, 1)

                    less_max(0)
                    inverse_sum(0)
                    less_max(1)
                if main:
                    dve.wait_ge(low_high, u + 1)
                    rows = slice(2 * LR, 4 * LR)
                    dve.tensor_tensor(lows[rows, :], bank[3][rows, P:2 * P], lows[rows, :].bitcast(F32), ALU.subtract).then_inc(low_ready, 1)
                if score:
                    inverse_sum(1)
                if main:
                    dve.wait_ge(qkv_done, u + 1)
                    need(dve, v_high, u)
                    need(dve, v_low, u)
                    need(dve, rot_im, u)
                    dve.wait_ge(const_in, 16 * len(consts))
                    for n in range(NCH):
                        cols = slice(n * BANK, (n + 1) * BANK)
                        dve.tensor_tensor(qkv[:, cols], bank[n][:, :], b_bc[:, cols], ALU.add).then_inc(bank_out if n < NCH - 1 else qkv_out, 1)

            steps(dve, step)

        @block.tensor
        def _(pe):
            def passes(k):
                for n, (sx, wc, wa) in enumerate(((x_h, p1_h, a_h), (x_h, p1_l, a_l), (x_l, p1_h, a_h))):
                    yield sx, wc, wa, k == 0 and n == 0, k == KT - 1 and n == 2

            def project(u, k):
                if k % HALF == 0:
                    pe.wait_ge(x_low, 2 * u + k // HALF + 1)
                if k == 0:
                    pe.wait_ge(a_low, u + 1)

                def down(sx, wa, first, last):
                    mm = pe.matmul(bank[3][:, 0:BPU * LR], sx[:, k, :], wa[:, k, :], start=first, stop=last)
                    if last:
                        mm.then_inc(low_done, 1)

                if k == KT - 1:
                    for sx, wc, wa, first, last in passes(k):
                        down(sx, wa, first, last)
                for sx, wc, wa, first, last in passes(k):
                    if k < KT - 1:
                        down(sx, wa, first, last)
                    for n in range(NCH):
                        if first and n < NCH - 1:
                            need(pe, bank_out, (NCH - 1) * (u - 1) + n + 1)
                        elif first:
                            need(pe, qkv_out, u)
                        mm = pe.matmul(bank[n][:, :], sx[:, k, :], wc[:, n, k, :], start=first, stop=False)
                    if k == KT - 1 and wc is p1_l:
                        transpose_down(u)
                if k % HALF == HALF - 1:
                    mm.then_inc(half_done, 1)

            def transpose_qk(v, turns):
                if 0 in turns:
                    pe.wait_ge(rotated, 2 * v + 2)
                    need(pe, pt_low, 2 * v)
                flat = roped[:, :, :, :].rearrange("p h i two -> p (h i two)")
                for turn in turns:
                    to, tiles = TURNS[turn]
                    if turn == 2:
                        pe.wait_ge(qk_low, 3 * v + 1)
                    for at, n in enumerate(tiles):
                        col = (QUADS * GRP + int(n[1]) if isinstance(n, str) else n) * P
                        mm = pe.transpose(t_ps[:, to, at * P:(at + 1) * P], flat[:, col:col + P], ident[:, :])
                    mm.then_inc(qk_t, 1)

            def scores(v, b):
                if b == 0:
                    pe.wait_ge(qk_low, 3 * v + 3)
                    pe.wait_ge(k_low, v + 1)
                    need(pe, pv_out, 2 * v)
                else:
                    pe.wait_ge(s_sub, 2 * v + 1)
                for g in range(2):
                    pe.matmul(s_ps[:, g, :], mask_l[:, :], mask_r[:, :], start=True, stop=False)
                    for q in range(QUADS):
                        o = s_ps[:, g, q * 4 * SEQ:(q + 1) * 4 * SEQ]
                        cols = slice(q * GRP + 2 * g, q * GRP + 2 * g + 2)
                        for n, (qq, kk) in enumerate(((q_h, k_h), (q_h, k_l), (q_l, k_h))):
                            mm = pe.matmul(o, qq[:, b, cols, :].rearrange("p g t -> p (g t)"), kk[:, q, b, :, :].rearrange("p c t -> p (c t)"),
                                           start=False, stop=q == QUADS - 1 and n == 2)
                mm.then_inc(s_done, 1)

            def transpose_p(v, b):
                pe.wait_ge(s_norm, 2 * v + b + 1)
                if b == 1:
                    pe.wait_ge(pt_low, 2 * v + 1)
                for q in range(QUADS):
                    for j in range(2):
                        for g in range(2):
                            at = (j * 2 + g) * P
                            c = q * 4 + j * 2
                            mm = pe.transpose(t_ps[:, q, at:at + P], prob[:, b, g, c:c + 2, :].rearrange("p c k -> p (c k)"), ident[:, :])
                mm.then_inc(pt_done, 1)

            def attend(v, b):
                pe.wait_ge(pt_low, 2 * v + b + 1)
                if b == 0:
                    pe.wait_ge(vb_high, v + 1)
                    pe.wait_ge(vb_low, v + 1)
                    pe.wait_ge(s_sub, 2 * v + 2)
                n = 0
                for q in range(QUADS):
                    for j in range(2):
                        for vv, pp in ((vb_h, pt_h), (vb_h, pt_l), (vb_l, pt_h)):
                            mm = pe.matmul(s_ps[:, b, q * 4 * SEQ:(q + 1) * 4 * SEQ], vv[:, b, q, j, :, :].rearrange("p c d -> p (c d)"),
                                           pp[:, q, j, :, :].rearrange("p g t -> p (g t)"), start=n % 6 == 0, stop=n % 6 == 5)
                            n += 1
                mm.then_inc(pv_done, 1)

            def transpose_down(u):
                if isinstance(u, int) and u == 0:
                    pe.wait_ge(const_in, 16 * len(consts))
                    pe.wait_ge(mask_ready, 1)
                pe.wait_ge(low_copied, u + 1)
                pe.transpose(bank[3][:, P:2 * P], low4[:, :, :].rearrange("p n r -> p (n r)"), ident[:, :]).then_inc(low_t, 1)

            def up(u):
                pe.wait_ge(low_ready, u + 1)
                for n in range(NCH):
                    mm = pe.matmul(bank[n][:, :], lows[:, :], pb[:, n * BANK:(n + 1) * BANK], start=False, stop=True)
                mm.then_inc(qkv_done, 1)

            BESIDE = {0: [(transpose_p, 2, 0)], 1: [(attend, 2, 0), (transpose_p, 2, 1)], 2: [(attend, 2, 1), (transpose_qk, 1, (0, 1))],
                      3: [(transpose_qk, 1, (2,))], 4: [(scores, 1, 0)], 6: [(scores, 1, 1)]}

            def step(u, main, score, value, nxt):
                for k in range(KT):
                    for what, back, which in BESIDE.get(k, []):
                        if (back == 1 and score) or (back == 2 and value):
                            what(u - back, which)
                    if main:
                        project(u, k)
                if main:
                    up(u)

            steps(pe, step)


def fold_ffn(nc, a, sem, attn_dram, ring):
    with ExitStack() as keep:
        with nc.sbuf_tensor("w2_raw", [P, KT, D], F32) as w_raw:
            pass
        fr_h, fr_l = (keep.enter_context(nc.sbuf_tensor(n, [P, KT, FCOLS], F32R)) for n in ("fr_h", "fr_l"))
        g_h, g_l = (keep.enter_context(nc.sbuf_tensor(n, [P, FOUT], F32R)) for n in ("g_h", "g_l"))
        with ExitStack() as st:
            def tb(name, shape, dt=F32R):
                return st.enter_context(nc.sbuf_tensor(name, shape, dt))

            w_h, w_l = tb("w2_h", [P, KT, D]), tb("w2_l", [P, KT, D])
            c_h, c_l = tb("c2_h", [P, 2, KT, FCH]), tb("c2_l", [P, 2, KT, FCH])

            def part(fr):
                return lambda i, j, e, w: fr[:, i, bass.ds((2 * j + e) * FCH, w)] if w == FCH else fr[:, i, FOUT:FCOLS]

            def up(g):
                return lambda j, e, w: g[:, bass.ds((2 * j + e) * FCH, w)]

            fold_program(nc, sem, "f2", st, ring, a["w_2"], a["last_t"], GATED, w_raw, w_h, w_l, c_h, c_l,
                         part(fr_h), part(fr_l), a["b2_up"], ERS, up(g_h),
                         lambda j, e, w, src: [(up(g_l)(j, e, w), up(g_h)(j, e, w), src)],
                         lambda sp: start_forward(sp, sem, a, attn_dram, ring), True)
        feed_forward(nc, a, sem, attn_dram, ring, keep, fr_h, fr_l, g_h, g_l)


def weight_piece(ring, a, n):
    slot = ring[:, n % 2, :]
    if n < KT:
        return slot, a["wo_t"][:, n, :]
    if n == KT:
        return slot, a["bf_up"]
    h = n - KT - 1
    return (slot[:, 0:HALF * GATED].rearrange("p (k c) -> p k c", k=HALF), a["gate2_t"][:, h * HALF:(h + 1) * HALF, :])


def load_weight(sp, sem, ring, a, n):
    dst, src = weight_piece(ring, a, n)
    sp.dma_start(dst, src).then_inc(sem(f"w4_in{n % 2}"), 16)


def load_attn(sp, sem, attn_dram, ring, u, half):
    sp.dma_start(ring[:, 3, half * HALF * P:(half + 1) * HALF * P],
                 attn_dram[bass.ds(u, 1), :, half * HALF * P:(half + 1) * HALF * P].rearrange("o p c -> (o p) c")).then_inc(sem(f"at_in{half}"), 16)


def load_tokens(sp, sem, a, ring, u):
    sp.dma_start(ring[:, 2, :], a["x_tok"][bass.ds(u, 1), :, :].rearrange("o p d -> (o p) d")).then_inc(sem("xt_in"), 16)


def start_forward(sp, sem, a, attn_dram, ring):
    for half in range(2):
        load_attn(sp, sem, attn_dram, ring, 0, half)
    sp.wait_ge(sem("f2_lb_low"), 1)
    load_tokens(sp, sem, a, ring, 0)
    sp.wait_ge(sem("f2_chunk_low"), 2 * a["last_t"].shape[0])
    for n in range(2):
        load_weight(sp, sem, ring, a, n)


def feed_forward(nc, a, sem, attn_dram, ring, keep, fr_h, fr_l, g_h, g_l):
    def sb(name, shape, dt=F32):
        return keep.enter_context(nc.sbuf_tensor(name, shape, dt))

    wo_h, wo_l = sb("wo_h", [P, KT, D], F32R), sb("wo_l", [P, KT, D], F32R)
    bf_h, bf_l = sb("bf_h", [P, D], F32R), sb("bf_l", [P, D], F32R)
    at_raw = ring[:, 3, :].rearrange("p (k t) -> p k t", k=KT)
    x_raw = ring[:, 2, :]
    at_h, at_l = sb("at_h", [P, KT, P], F32R), sb("at_l", [P, KT, P], F32R)
    x1, x1_out = sb("x1", [P, D]), sb("x1_out", [P, D])
    x1t_h, x1t_l = sb("x1t_h", [P, KT, P], F32R), sb("x1t_l", [P, KT, P], F32R)
    bo_bc, bb_bc = sb("bo_bc", [P, D]), sb("bb_bc", [P, D])
    ident = sb("ident4", [P, P])
    before = sb("before", [P, EXP, EXP])
    experts = sb("experts", [P, EXP])
    lang, lang_f = sb("lang", [P, UNITS], I32), sb("lang_f", [P, UNITS])
    lang_bias = sb("lang_bias", [P, UNITS, EXP])
    lg, ex, rank, pick, gate = (sb(n, [P, EXP]) for n in ("lg", "ex", "rank", "pick", "gate"))
    above, ties = sb("above", [P, EXP, EXP]), sb("ties", [P, EXP, EXP])
    top, total, share = sb("top", [P, 1]), sb("total", [P, 1]), sb("share", [P, 1])
    z = sb("z", [P, EXP, ER])
    zt_h, zt_l = sb("zt_h", [P, P], F32R), sb("zt_l", [P, P], F32R)
    w_ps = keep.enter_context(nc.psum_tensor("w_ps", [P, 2, BANK], F32))
    b_ps = keep.enter_context(nc.psum_tensor("b_ps", [P, 3, BANK], F32))
    x_ps = keep.enter_context(nc.psum_tensor("x_ps", [P, 2, BANK], F32))
    z_ps = keep.enter_context(nc.psum_tensor("z_ps", [P, BANK], F32))

    consts_in = sem("consts4_in")
    w_in = [sem("w4_in0"), sem("w4_in1")]
    w_high, w_low = sem("w4_high"), sem("w4_low")
    at_in = [sem("at_in0"), sem("at_in1")]
    x_in, x_bias = sem("xt_in"), sem("x_bias")
    at_high, at_low, wo_done = sem("at_high"), sem("at_low"), sem("wo_done")
    x1_ready, x1_t, x1_high, x1_low, x1_biased = (sem(n) for n in ("x1_ready", "x1_t", "x1_high", "x1_low", "x1_biased"))
    lang_step, f_done, up_done, base_done = sem("lang_step"), sem("f_done"), sem("up_done"), sem("base_done")
    route_step, route_exp, z_ready = sem("route_step"), sem("route_exp"), sem("z_ready")
    z_t, z_high, z_low = sem("z_t"), sem("z_high"), sem("z_low")
    out_ready, out_stored = sem("out_ready"), sem("out_stored")
    ROUTE_STEPS = 13
    consts = [(bo_bc[:, :], a["b_o"].partition_broadcast(P)), (bb_bc[:, :], a["b_base"].partition_broadcast(P)),
              (ident[:, :], a["ident"]), (before[:, :, :].rearrange("p e j -> p (e j)"), a["before"]), (experts[:, :], a["experts"])]
    consts += [(lang[b * SEQ:(b + 1) * SEQ, :], a["language"][b, :].partition_broadcast(SEQ)) for b in range(BPU)]
    weights = [(wo_h[:, k, :], wo_l[:, k, :]) for k in range(KT)] + [(bf_h[:, :], bf_l[:, :])]
    weights += [(fr_h[:, ks, D:FOUT], fr_l[:, ks, D:FOUT]) for ks in (slice(0, HALF), slice(HALF, KT))]

    def steps(engine, step):
        step(0, True, False, True)
        with engine.Fori(1, UNITS - 1) as u:
            step(u, True, True, True)
        step(UNITS - 1, True, True, False)
        step(UNITS, False, True, False)

    def ks(half):
        return slice(half * HALF, (half + 1) * HALF)

    with nc.Block() as block:
        @block.sync
        def _(sp):
            for dst, src in consts:
                sp.dma_start(dst, src).then_inc(consts_in, 16)
            for n in range(2, len(weights)):
                sp.wait_ge(w_low, n - 1)
                load_weight(sp, sem, ring, a, n)

            def step(u, main, gating, nxt):
                v = u - 1
                if nxt:
                    for half in range(2):
                        sp.wait_ge(at_low, 2 * u + half + 1)
                        load_attn(sp, sem, attn_dram, ring, u + 1, half)
                    sp.wait_ge(x1_ready, 2 * u + 2)
                    load_tokens(sp, sem, a, ring, u + 1)
                if gating:
                    sp.wait_ge(out_ready, 2 * v + 2)
                    sp.dma_start(a["out"][bass.ds(v, 1), :, :].rearrange("o p d -> (o p) d"), x1_out[:, :]).then_inc(out_stored, 16)

            steps(sp, step)
            sp.wait_ge(out_stored, 16 * UNITS)

        @block.scalar
        def _(act):
            def split_weights(which):
                for n in which:
                    act.wait_ge(w_in[n % 2], 16 * (n // 2 + 1))
                    act.activation(weights[n][0], weight_piece(ring, a, n)[0], ACT.Copy).then_inc(w_high, 1)

            def split_attn(u, half):
                act.wait_ge(at_in[half], 16 * (u + 1))
                need(act, wo_done, 2 * u)
                act.activation(at_h[:, ks(half), :], at_raw[:, ks(half), :], ACT.Copy).then_inc(at_high, 1)

            def gated(v, r):
                act.wait_ge(route_step, (v * 2 + r) * ROUTE_STEPS + 3)
                act.activation(ex[:, :], ex[:, :], ACT.Exp).then_inc(route_exp, 1)
                act.wait_ge(z_t, 2 * v + r + 1)
                act.activation(zt_h[:, :], z_ps[:, 0:P], ACT.Copy).then_inc(z_high, 1)

            def step(u, main, gating, nxt):
                v = u - 1
                if gating:
                    gated(v, 0)
                if gating:
                    gated(v, 1)
                if main:
                    for half in range(2):
                        act.wait_ge(x1_t, 2 * u + half + 1)
                        act.activation(x1t_h[:, ks(half), :].rearrange("p k t -> p (k t)"), x_ps[:, half, :], ACT.Copy).then_inc(x1_high, 1)
                if nxt:
                    split_attn(u + 1, 0)
                    split_attn(u + 1, 1)

            split_attn(0, 0)
            split_attn(0, 1)
            split_weights(range(len(weights)))
            steps(act, step)

        @block.gpsimd
        def _(pool):
            def split_attn(u, half):
                pool.wait_ge(at_high, 2 * u + half + 1)
                pool.tensor_tensor(at_l[:, ks(half), :], at_raw[:, ks(half), :], at_h[:, ks(half), :].bitcast(F32), ALU.subtract).then_inc(at_low, 1)

            def bias_x(u):
                pool.wait_ge(x_in, 16 * (u + 1))
                pool.tensor_tensor(x_raw, x_raw, bo_bc[:, :], ALU.add).then_inc(x_bias, 1)

            def step(u, main, gating, nxt):
                if main:
                    pool.wait_ge(x1_ready, 2 * u + 2)
                    need(pool, out_stored, 16 * u)
                    pool.tensor_tensor(x1_out[:, :], x1[:, :], bb_bc[:, :], ALU.add).then_inc(x1_biased, 1)
                if nxt:
                    split_attn(u + 1, 0)
                    split_attn(u + 1, 1)
                    bias_x(u + 1)

            pool.wait_ge(consts_in, 16 * len(consts))
            split_attn(0, 0)
            split_attn(0, 1)
            bias_x(0)
            steps(pool, step)

        @block.vector
        def _(dve):
            for n, (hi, lo) in enumerate(weights):
                dve.wait_ge(w_high, n + 1)
                dve.tensor_tensor(lo, weight_piece(ring, a, n)[0], hi.bitcast(F32), ALU.subtract).then_inc(w_low, 1)
            dve.wait_ge(consts_in, 16 * len(consts))
            dve.tensor_copy(lang_f[:, :], lang[:, :]).then_inc(lang_step, 1)
            dve.wait_ge(lang_step, 1)
            dve.tensor_tensor(lang_bias[:, :, :], experts[:, :].unsqueeze(1).to_broadcast([P, UNITS, EXP]),
                              lang_f[:, :].unsqueeze(2).to_broadcast([P, UNITS, EXP]), ALU.is_equal).then_inc(lang_step, 1)
            dve.wait_ge(lang_step, 2)
            dve.tensor_scalar(lang_bias[:, :, :], lang_bias[:, :, :], LANG_BIAS, None, ALU.mult).then_inc(lang_step, 1)
            dve.wait_ge(lang_step, 3)

            def route(v, r):
                steps_before = (v * 2 + r) * ROUTE_STEPS
                count = [0]

                def link(instruction):
                    count[0] += 1
                    instruction.then_inc(route_step, 1)
                    dve.wait_ge(route_step, steps_before + count[0])

                at = r * GATED
                logits, down = b_ps[:, 2, at:at + EXP], b_ps[:, 2, at + EXP:at + GATED]
                if r == 0:
                    dve.wait_ge(f_done, v + 1)
                    link(dve.tensor_tensor(lg[:, :], logits, lang_bias[:, bass.ds(v, 1), :].rearrange("p o e -> p (o e)"), ALU.add))
                else:
                    dve.wait_ge(up_done, v + 1)
                    link(dve.tensor_copy(lg[:, :], logits))
                link(dve.tensor_reduce(top[:, :], lg[:, :], AX.X, ALU.max))
                link(dve.tensor_scalar(ex[:, :], lg[:, :], top[:, :], None, ALU.subtract))
                mine = lg[:, :].unsqueeze(2).to_broadcast([P, EXP, EXP])
                other = lg[:, :].unsqueeze(1).to_broadcast([P, EXP, EXP])
                link(dve.tensor_tensor(ties[:, :, :], other, mine, ALU.is_equal))
                link(dve.tensor_tensor(above[:, :, :], other, mine, ALU.is_gt))
                link(dve.tensor_tensor(ties[:, :, :], ties[:, :, :], before[:, :, :], ALU.mult))
                link(dve.tensor_tensor(above[:, :, :], above[:, :, :], ties[:, :, :], ALU.add))
                link(dve.tensor_reduce(rank[:, :], above[:, :, :], AX.X, ALU.add))
                dve.wait_ge(route_exp, 2 * v + r + 1)
                link(dve.scalar_tensor_tensor(pick[:, :], rank[:, :], 1.5, ex[:, :], ALU.is_lt, ALU.mult))
                link(dve.tensor_reduce(total[:, :], pick[:, :], AX.X, ALU.add))
                link(dve.reciprocal(share[:, :], total[:, :]))
                link(dve.tensor_scalar(gate[:, :], pick[:, :], share[:, :], MOE_SCALE, ALU.mult, ALU.mult))
                link(dve.tensor_tensor(z[:, :, :], down.rearrange("p (e r) -> p e r", e=EXP),
                                       gate[:, :].unsqueeze(2).to_broadcast([P, EXP, ER]), ALU.mult))
                assert count[0] == ROUTE_STEPS
                dve.wait_ge(z_high, 2 * v + r + 1)
                dve.tensor_tensor(zt_l[:, :], z_ps[:, 0:P], zt_h[:, :].bitcast(F32), ALU.subtract).then_inc(z_low, 1)

            def residual(u, half):
                dve.wait_ge(wo_done, 2 * u + half + 1)
                if half == 0:
                    dve.wait_ge(x_bias, u + 1)
                    need(dve, x1_biased, u)
                    need(dve, x1_t, 2 * u)
                cols = slice(half * BANK, (half + 1) * BANK)
                dve.tensor_tensor(x1[:, cols], w_ps[:, half, :], x_raw[:, cols], ALU.add).then_inc(x1_ready, 1)

            def split_x1(u, half):
                dve.wait_ge(x1_high, 2 * u + half + 1)
                dve.tensor_tensor(x1t_l[:, ks(half), :].rearrange("p k t -> p (k t)"), x_ps[:, half, :],
                                  x1t_h[:, ks(half), :].rearrange("p k t -> p (k t)").bitcast(F32), ALU.subtract).then_inc(x1_low, 1)

            def step(u, main, gating, nxt):
                v = u - 1
                if gating:
                    route(v, 0)
                if main:
                    residual(u, 0)
                if gating:
                    route(v, 1)
                if main:
                    split_x1(u, 0)
                    residual(u, 1)
                if gating:
                    dve.wait_ge(x1_biased, v + 1)
                    for n in range(2):
                        cols = slice(n * BANK, (n + 1) * BANK)
                        dve.wait_ge(base_done, 2 * v + n + 1)
                        dve.tensor_tensor(x1_out[:, cols], b_ps[:, n, :], x1_out[:, cols], ALU.add).then_inc(out_ready, 1)
                if main:
                    split_x1(u, 1)

            steps(dve, step)

        @block.tensor
        def _(pe):
            def project(u, n, k):
                if n == 0 and k % HALF == 0:
                    pe.wait_ge(at_low, 2 * u + k // HALF + 1)
                if n == 0 and isinstance(u, int) and u == 0:
                    pe.wait_ge(w_low, k + 1)
                if k == 0:
                    need(pe, x1_ready, 2 * u - 1 + n)
                for s, w in ((at_h, wo_h), (at_h, wo_l), (at_l, wo_h)):
                    mm = pe.matmul(w_ps[:, n, :], s[:, k, :], w[:, k, n * BANK:(n + 1) * BANK],
                                   start=k == 0 and s is at_h and w is wo_h, stop=k == KT - 1 and s is at_l)
                if k == KT - 1:
                    mm.then_inc(wo_done, 1)

            def transpose_z(v, r):
                pe.wait_ge(route_step, (v * 2 + r + 1) * ROUTE_STEPS)
                need(pe, z_low, 2 * v + r)
                pe.transpose(z_ps[:, 0:P], z[:, :, :].rearrange("p e r -> p (e r)"), ident[:, :]).then_inc(z_t, 1)

            def second_up(v):
                pe.wait_ge(z_low, 2 * v + 1)
                for n in (2, 0, 1):
                    cols = slice(n * BANK, min((n + 1) * BANK, FOUT))
                    o = b_ps[:, 2, GATED:2 * GATED] if n == 2 else b_ps[:, n, :]
                    for s, w in ((zt_h, g_h), (zt_h, g_l), (zt_l, g_h)):
                        mm = pe.matmul(o, s[:, :], w[:, cols], start=False, stop=n == 2 and s is zt_l, skip_group_check=n == 2)
                    if n == 2:
                        mm.then_inc(up_done, 1)

            def last_up(v):
                pe.wait_ge(z_low, 2 * v + 2)
                for n in range(2):
                    for s, w in ((zt_h, bf_h), (zt_h, bf_l), (zt_l, bf_h)):
                        mm = pe.matmul(b_ps[:, n, :], s[:, :], w[:, n * BANK:(n + 1) * BANK], start=False, stop=s is zt_l)
                    mm.then_inc(base_done, 1)

            def transpose_x1(u, half):
                pe.wait_ge(x1_ready, 2 * u + half + 1)
                need(pe, x1_low, 2 * u - 1 + half)
                for k in range(half * HALF, (half + 1) * HALF):
                    at = (k % HALF) * P
                    mm = pe.transpose(x_ps[:, half, at:at + P], x1[:, k * P:(k + 1) * P], ident[:, :])
                mm.then_inc(x1_t, 1)

            def forward(u):
                need(pe, route_step, 2 * u * ROUTE_STEPS)
                for k in range(KT):
                    if k % HALF == 0:
                        pe.wait_ge(x1_low, 2 * u + k // HALF + 1)
                    for s, w in ((x1t_h, fr_h), (x1t_h, fr_l), (x1t_l, fr_h)):
                        first = k == 0 and s is x1t_h and w is fr_h
                        for n in (2, 0, 1):
                            if first and n < 2:
                                need(pe, out_ready, 2 * u - 1 + n)
                            cols = slice(n * BANK, min((n + 1) * BANK, FCOLS))
                            mm = pe.matmul(b_ps[:, n, 0:cols.stop - cols.start], s[:, k, :], w[:, k, cols],
                                           start=first, stop=n == 2 and k == KT - 1 and s is x1t_l)
                mm.then_inc(f_done, 1)

            def step(u, main, gating, nxt):
                v = u - 1
                for k in range(KT):
                    if gating and k == 6:
                        transpose_z(v, 0)
                    if main:
                        project(u, 0, k)
                if gating:
                    second_up(v)
                for k in range(KT):
                    if gating and k == 6:
                        transpose_z(v, 1)
                        if main:
                            transpose_x1(u, 0)
                    if main:
                        project(u, 1, k)
                if main and not gating:
                    transpose_x1(u, 0)
                if gating:
                    last_up(v)
                if main:
                    transpose_x1(u, 1)
                    if isinstance(u, int) and u == 0:
                        pe.wait_ge(w_low, len(weights))
                    forward(u)

            pe.wait_ge(consts_in, 16 * len(consts))
            steps(pe, step)


def kernel(**inputs):
    import concourse.bacc as bacc
    from concourse.bass_utils import run_bass_kernel_spmd

    arrays = layout({k: np.asarray(v) for k, v in inputs.items()})
    nc = bacc.Bacc("TRN2", target_bir_lowering=False, num_devices=1, dynamic_dma_scratch_size=1024)
    tensors = {n: nc.dram_tensor(f"in_{n}", v.shape, mybir.dt.from_np(v.dtype), kind="ExternalInput").ap() for n, v in arrays.items()}
    tensors["out"] = nc.dram_tensor("out", (UNITS, P, D), F32, kind="ExternalOutput").ap()
    build(nc, tensors)
    r = run_bass_kernel_spmd(nc, [{f"in_{n}": v for n, v in arrays.items()}], core_ids=[0])
    return r.results[0]["out"].reshape(BATCH, SEQ, D)


def layout(x):
    def by_k(w):
        return w.reshape(KT, P, -1).transpose(1, 0, 2)

    def heads_first(w):
        w = w.reshape(QUADS, 4, GRP, HD, -1)
        return w.transpose(0, 2, 1, 3, 4).reshape(HEADS * HD, -1)

    tok = x["x"].reshape(UNITS, P, D)
    w_qkv, nq = x["L0_attn_w_qkv"], HEADS * HD
    w_qkv = np.concatenate([heads_first(w_qkv[:nq]), w_qkv[nq:]])
    b_qkv = x["L0_attn_b_qkv"]
    b_qkv = np.concatenate([heads_first(b_qkv[:nq])[:, 0], b_qkv[nq:]])
    last = np.concatenate([x["L0_ffn_W_base"], x["L0_ffn_W_router"], x["L0_ffn_A"].reshape(ERS, D)])
    gate2 = np.concatenate([x["L0_cond2_Wr"], x["L0_cond2_A"].reshape(ERS, D)])
    last_t = by_k(last.T)
    pos = (np.arange(P) % SEQ).astype(np.float32)
    inv = np.float32(1.0) / np.float32(10000.0) ** (np.arange(0, HD, 2, dtype=np.float32) / np.float32(HD))
    ang = (pos[:, None] * inv[None, :]).astype(np.float32)
    mask_l = np.zeros((P, P), np.float32)
    mask_l[np.arange(P) % SEQ, np.arange(P)] = 1
    mask_r = np.zeros((P, KVH, SEQ), np.float32)
    mask_r[:SEQ] = np.where(np.arange(SEQ)[:, None] >= np.arange(SEQ)[None, :], 0.0, -1e20)[:, None, :]
    part = np.arange(P)
    out = {
        "x_t": tok.reshape(UNITS, P, KT, P).transpose(0, 3, 2, 1),
        "x_tok": tok,
        "labeler": x["itok_B_0_2"].reshape(1, BATCH),
        "language": x["itok_B_0_7"].reshape(UNITS, BPU).T,
        "w_cond": by_k(x["L0_cond_W"]),
        "wqkv_t": by_k(w_qkv.T).reshape(P, KT, QKV // FCH, FCH).transpose(2, 0, 1, 3),
        "b_qkv": b_qkv,
        "lora_a": x["L0_cond_lora_A"].reshape(LAB, KT, P, LR).transpose(0, 2, 1, 3),
        "lora_b": by_k(x["L0_cond_lora_B_w"]),
        "wo_t": by_k(heads_first(x["L0_attn_w_o"].T)),
        "b_o": x["L0_attn_b_o"],
        "w_2": by_k(x["L0_cond2_W"]),
        "b2_up": by_k(x["L0_cond2_B"].transpose(1, 0, 2).reshape(D, ERS)),
        "gate2_t": by_k(gate2.T),
        "last_t": np.pad(last_t, ((0, 0), (0, 0), (0, -FOUT % FCH))).reshape(P, KT, -1, FCH).transpose(2, 0, 1, 3),
        "bf_up": x["L0_ffn_B"].transpose(0, 2, 1).reshape(ERS, D),
        "b_base": x["L0_ffn_b_base"],
        "cos": np.cos(ang).astype(np.float32),
        "sin": np.sin(ang).astype(np.float32),
        "ident": np.eye(P, dtype=np.float32),
        "mask_l": mask_l,
        "mask_r": mask_r.reshape(P, BANK),
        "hmask": (part[:, None] // HD == np.arange(4)[None, :]).astype(np.float32),
        "experts": np.broadcast_to(np.arange(EXP, dtype=np.float32), (P, EXP)),
        "before": np.broadcast_to(np.tril(np.ones((EXP, EXP), np.float32), -1).reshape(1, EXP * EXP), (P, EXP * EXP)),
    }
    return {n: np.ascontiguousarray(v) for n, v in out.items()}
```

```python
import numpy as np
import concourse.bass as bass
from concourse import mybir
from collections import namedtuple
from contextlib import ExitStack

F32 = mybir.dt.float32
F32R = mybir.dt.float32r
BF16 = mybir.dt.bfloat16
I32 = mybir.dt.int32
ALU = mybir.AluOpType
ACT = mybir.ActivationFunctionType
AX = mybir.AxisListType

P = 128
BATCH, SEQ, D = 32, 64, 1024
TOK = BATCH * SEQ
UNITS = TOK // P
BPU = P // SEQ
KT = D // P
HEADS, KVH, HD = 32, 8, 32
GRP = HEADS // KVH
QUADS = KVH // 4
QKV = (HEADS + 2 * KVH) * HD
QK = (HEADS + KVH) * HD
BANK = 512
NCH = QKV // BANK
LAB, LR = 5, 32
EXP, ER = 8, 16
ERS = EXP * ER
GATED = EXP + ERS
FOUT = D + GATED
FCOLS = FOUT + GATED
FCH = 256
SCALE = float(HD) ** -0.5
LORA_SCALE = 0.5
MOE_SCALE = 2.0
LANG_BIAS = 5.0
HALF = KT // 2


def need(engine, semaphore, value):
    if isinstance(value, int) and value <= 0:
        return
    engine.wait_ge(semaphore, value)


Programs = namedtuple("Programs", "sync scalar gpsimd vector tensor")


def build(nc, a):
    with ExitStack() as ctx:
        names = {}

        def sem(name):
            if name not in names:
                names[name] = ctx.enter_context(nc.semaphore(name))
            return names[name]

        a = dict(a, attn=nc.dram_tensor("attn_scratch", (UNITS, P, KT * P), F32, kind="Internal").ap())
        psum = ctx.enter_context(nc.psum_tensor("psum", [P, 8, BANK], F32))
        with ExitStack() as shared:
            _, lb1_h = (shared.enter_context(nc.sbuf_tensor(n, shape, dt)) for n, shape, dt in (
                ("slots_0_1", [P, 2, D], F32), ("lb_h", [P, KT, P], F32R)))
        ring = ctx.enter_context(nc.sbuf_tensor("ring", [P, 4, D], F32))
        with ExitStack() as shared:
            _, x1, x1_out, a_raw, index = (shared.enter_context(nc.sbuf_tensor(n, shape, dt)) for n, shape, dt in (
                ("x_place", [P, 2, D], F32), ("x1", [P, D], F32), ("x1_out", [P, D], F32),
                ("a_raw", [P, BPU, KT, LR], F32), ("index", [1, BATCH], I32)))
        with ExitStack() as shared:
            _, wo_raw = (shared.enter_context(nc.sbuf_tensor(n, shape, F32)) for n, shape in (
                ("c_h_place", [P, 4, D]), ("wo_raw", [P, 2, D])))
        c = ctx.enter_context(nc.sbuf_tensor("c_high_low", [P, 2, 2, KT, FCH], F32R))
        c_h, c_l = c[:, 0, :, :, :], c[:, 1, :, :, :]

        with ExitStack() as second:
            fold2 = fold_ffn(nc, a, sem, second, psum, ring, c, wo_raw)
            forward, begin_forward, first_weights = feed_forward(nc, a, sem, second, psum, ring, c_h, c_l, wo_raw, x1, x1_out, fold2)
        with ExitStack() as first:
            fold1 = fold_qkv(nc, a, sem, first, psum, ring, c, lb1_h)
            attend, begin_attend = attention(nc, a, sem, first, psum, ring, c_h, c_l, a_raw, index, fold1, fold2)
        folding1 = folding_qkv(fold1, begin_attend)
        folding2 = folding_ffn(fold2, begin_forward, first_weights)

        with nc.Block() as block:
            @block.sync
            def _(sp):
                for stage in (folding1, attend, folding2, forward):
                    stage.sync(sp)

            @block.scalar
            def _(act):
                for stage in (folding1, attend, folding2, forward):
                    stage.scalar(act)

            @block.gpsimd
            def _(pool):
                for stage in (folding1, attend, folding2, forward):
                    stage.gpsimd(pool)

            @block.vector
            def _(dve):
                for stage in (folding1, attend, folding2, forward):
                    stage.vector(dve)

            @block.tensor
            def _(pe):
                for stage in (folding1, attend, folding2, forward):
                    stage.tensor(pe)


def halves(c, b):
    flat = c[:, b, :, :].rearrange("p k c -> p (k c)")
    return flat[:, 0:D], flat[:, D:2 * D]


def by_tile(flat):
    return flat.rearrange("p (k t) -> p k t", k=KT)


class Fold:
    TILES = KT + 1
    GROUP = 3
    SETS = ((0, 1, 2), (5, 6, 7))
    FIRST = 4

    def __init__(self, sem, tag, psum, ring, c, odd, w_dram, c_dram, lb_dram, last_width,
                 w_raw, w_h, w_l, lb_h, lb_l, out_h, out_l, lora_h, lora_l, sums=None):
        self.psum, self.ring, self.c, self.c_h, self.c_l, self.odd = psum, ring, c, c[:, 0, :, :, :], c[:, 1, :, :, :], odd
        self.w_dram, self.c_dram, self.lb_dram, self.last_width = w_dram, c_dram, lb_dram, last_width
        self.w_raw, self.w_h, self.w_l, self.lb_h, self.lb_l = w_raw, w_h, w_l, lb_h, lb_l
        self.out_h, self.out_l, self.lora_h, self.lora_l = out_h, out_l, lora_h, lora_l
        self.chunks = c_dram.shape[0]
        self.sums = sums
        if sums is not None:
            self.copied, self.summed = sem(f"{tag}_copied"), sem(f"{tag}_summed")
        self.lr = lb_dram.shape[2]
        self.narrow = 4 * self.lr == P
        self.high_cols = 3 * self.lr if self.narrow else P
        self.lb_raw = ring[:, 3, 0:KT * self.lr].rearrange("p (k r) -> p k r", k=KT)
        self.lb_loaded, self.lb_high, self.lb_low = sem(f"{tag}_lb_loaded"), sem(f"{tag}_lb_high"), sem(f"{tag}_lb_low")
        self.w_loaded = [sem(f"{tag}_w_loaded{k}") for k in range(KT)]
        self.w_high, self.w_low = sem(f"{tag}_w_high"), sem(f"{tag}_w_low")
        self.chunk_loaded = [sem(f"{tag}_chunk_loaded{h}") for h in range(2)]
        self.chunk_high, self.chunk_low = sem(f"{tag}_chunk_high"), sem(f"{tag}_chunk_low")
        self.done = sem(f"{tag}_tile_done")
        self.w_free = sem(f"{tag}_w_free")
        self.out_high, self.out_low = sem(f"{tag}_out_high"), sem(f"{tag}_out_low")

    def later_chunks(self, engine, step):
        pairs = (self.chunks - 2) // 2
        if pairs > 1:
            with engine.Fori(0, pairs) as j:
                step(j, 1, FCH, False)
                step(j + 1, 0, FCH, False)
        for ch in range(2 * pairs + 1 if pairs > 1 else 1, self.chunks):
            last = ch == self.chunks - 1
            step(ch // 2, ch % 2, self.last_width if last else FCH, last)

    def buffer(self, e):
        return (e + self.odd) % 2

    def half(self, h):
        return slice(h * HALF, (h + 1) * HALF)

    def raw_chunk(self, h):
        return self.ring[:, h, :].rearrange("p (k c) -> p k c", k=HALF)

    def first_ps(self, i):
        return self.psum[:, i % self.FIRST, i // self.FIRST * FCH:(i // self.FIRST + 1) * FCH] if i < KT else self.psum[:, self.FIRST, 0:FCH]

    def tile(self, e, i, width, last):
        return self.sums[:, i % self.GROUP, 0:width] if last and self.sums is not None else self.tile_ps(e, i, width)

    def tile_ps(self, e, i, width):
        return self.psum[:, self.SETS[(e + i // self.GROUP) % 2][i % self.GROUP], 0:width]

    def load_chunk(self, sp, ch, h):
        sp.dma_start(self.raw_chunk(h), self.c_dram[bass.ds(ch, 1), :, self.half(h), :].rearrange("o p k c -> (o p) k c")).then_inc(self.chunk_loaded[h], 16)

    def load_next_chunk(self, sp, ch):
        for h in range(2):
            sp.wait_ge(self.chunk_low, 2 * ch - 1 + h)
            self.load_chunk(sp, ch, h)

    def load_w(self, sp, k):
        sp.dma_start(self.w_raw[k], self.w_dram[:, k, :]).then_inc(self.w_loaded[k], 16)

    def load_lora(self, sp):
        sp.dma_start(self.lb_raw, self.lb_dram).then_inc(self.lb_loaded, 16)

    def high_half(self, act, ch, e, h):
        act.wait_ge(self.chunk_loaded[h], 16 * (ch + 1))
        act.activation(self.c_h[:, self.buffer(e), self.half(h), :], self.raw_chunk(h), ACT.Copy).then_inc(self.chunk_high, 1)

    def high_chunk(self, act, ch, e):
        for h in range(2):
            self.high_half(act, ch, e, h)

    def high_w(self, act, k):
        act.wait_ge(self.w_loaded[k], 16)
        act.activation(self.w_h[:, k, :], self.w_raw[k], ACT.Copy).then_inc(self.w_high, 1)

    def high_lora(self, act):
        act.wait_ge(self.lb_loaded, 16)
        act.wait_ge(self.w_low, KT)
        for r in range(0, self.high_cols, self.lr):
            last = act.activation(self.lb_h[:, :, r:r + self.lr], self.lb_raw, ACT.Copy)
        last.then_inc(self.lb_high, 1)

    def high_out(self, act, i, j, e, width, src):
        dst = self.out_h(i, j, e, width) if i < KT else self.lora_h(j, e, width)
        act.activation(dst, src, ACT.Copy).then_inc(self.out_high, 1)

    def copy_side(self, act, ch, e, i, width):
        act.wait_ge(self.done, ch * self.TILES + i + 1)
        if i >= self.GROUP:
            act.wait_ge(self.out_low, ch * self.TILES + i + 1 - self.GROUP)
        act.activation(self.sums[:, i % self.GROUP, 0:width], self.tile_ps(e, i, 2 * width)[:, width:2 * width], ACT.Copy).then_inc(self.copied, 1)

    def high_first(self, act):
        for i in range(self.TILES):
            act.wait_ge(self.done, i + 1 + (self.FIRST if i < self.FIRST else 0))
            if self.FIRST <= i < KT:
                act.wait_ge(self.out_low, i - self.FIRST + 1)
            self.high_out(act, i, 0, 0, FCH, self.first_ps(i))

    def high_later(self, act, beside_last, before_end=None):
        def step(j, e, width, last):
            ch = 2 * j + e
            for i in range(self.TILES):
                if last and before_end and i == self.TILES - self.GROUP:
                    before_end()
                if last and self.sums is not None:
                    if i % self.GROUP == 0:
                        for n in range(i, i + self.GROUP):
                            self.copy_side(act, ch, e, n, width)
                    act.wait_ge(self.summed, i + 1)
                else:
                    act.wait_ge(self.done, ch * self.TILES + i + 1)
                self.high_out(act, i, j, e, width, self.tile(e, i, width, last))
                if i == 0:
                    if last:
                        beside_last(act)
                    else:
                        self.high_chunk(act, ch + 1, 1 - e)

        self.later_chunks(act, step)

    def low_half(self, dve, ch, e, h):
        dve.wait_ge(self.chunk_high, 2 * ch + h + 1)
        high = self.c_h[:, self.buffer(e), self.half(h), :]
        dve.tensor_tensor(self.c_l[:, self.buffer(e), self.half(h), :], self.raw_chunk(h), high.bitcast(F32), ALU.subtract).then_inc(self.chunk_low, 1)

    def low_chunk(self, dve, ch, e):
        for h in range(2):
            self.low_half(dve, ch, e, h)

    def low_lora(self, dve):
        dve.wait_ge(self.lb_high, 1)
        high = self.lb_h[:, :, 0:self.lr].bitcast(F32)
        if self.narrow:
            dve.tensor_copy(self.lb_l[:, :, 0:self.high_cols], self.lb_h[:, :, 0:self.high_cols].bitcast(F32))
            dve.memset(self.lb_l[:, :, self.high_cols:P].bitcast(F32), 0.0)
            low = self.lb_h[:, :, self.high_cols:P]
        else:
            low = self.lb_l[:, :, :]
        dve.tensor_tensor(low, self.lb_raw, high, ALU.subtract).then_inc(self.lb_low, 1)

    def low_out(self, dve, i, j, e, width, src):
        pairs = [(self.out_l(i, j, e, width), self.out_h(i, j, e, width), src)] if i < KT else self.lora_l(j, e, width, src)
        for lo, hi, part in pairs:
            last = dve.tensor_tensor(lo, part, hi.bitcast(F32), ALU.subtract)
        last.then_inc(self.out_low, 1)

    def low_first(self, dve):
        for i in range(self.TILES):
            dve.wait_ge(self.out_high, i + 1)
            self.low_out(dve, i, 0, 0, FCH, self.first_ps(i))

    def low_later(self, dve, before_end=None):
        def step(j, e, width, last):
            ch = 2 * j + e
            for i in range(self.TILES):
                if last and before_end and i == self.TILES - self.GROUP:
                    before_end()
                if last and self.sums is not None and i % self.GROUP == 0:
                    for n in range(i, i + self.GROUP):
                        self.add_up(dve, e, n, width)
                dve.wait_ge(self.out_high, ch * self.TILES + i + 1)
                self.low_out(dve, i, j, e, width, self.tile(e, i, width, last))
                if i == 0 and not last:
                    self.low_chunk(dve, ch + 1, 1 - e)

        self.later_chunks(dve, step)

    def add_up(self, dve, e, i, width):
        dve.wait_ge(self.copied, i + 1)
        total = self.sums[:, i % self.GROUP, 0:width]
        dve.tensor_tensor(total, self.tile_ps(e, i, width), total, ALU.add).then_inc(self.summed, 1)

    def low_w(self, dve, k):
        dve.wait_ge(self.w_high, k + 1)
        dve.tensor_tensor(self.w_l[:, k, :], self.w_raw[k], self.w_h[:, k, :].bitcast(F32), ALU.subtract).then_inc(self.w_low, 1)

    def products(self, pe, out, i, k, e, width, start, only=None, beside=False):
        cols = slice(i * P, (i + 1) * P)
        sh, sl = (self.w_h[:, k, cols], self.w_l[:, k, cols]) if i < KT else (self.lb_h[:, k, :], self.lb_l[:, k, :])
        ch, cl = (c[:, self.buffer(e), k, 0:width] for c in (self.c_h, self.c_l))
        if beside:
            both = self.c[:, :, self.buffer(e), k, 0:width]
            passes = ((sh, both, out), (sl, ch, out[:, 0:width]))
        elif i == KT and self.narrow:
            passes = ((sh, ch, out), (sl, cl, out))
        else:
            passes = ((sh, ch, out), (sh, cl, out), (sl, ch, out))
        for n in range(len(passes)) if only is None else (only,):
            stationary, moving, to = passes[n]
            mm = pe.matmul(to, stationary, moving, start=start and n == 0, stop=k == KT - 1 and n == len(passes) - 1, skip_group_check=True)
        if k == KT - 1 and n == len(passes) - 1:
            mm.then_inc(self.done, 1)
        return mm

    def first(self, pe, k):
        if k % HALF == 0:
            pe.wait_ge(self.chunk_low, k // HALF + 1)
        for n in range(3):
            if n == 0:
                pe.wait_ge(self.w_high, k + 1)
            elif n == 2:
                pe.wait_ge(self.w_low, k + 1)
            for i in range(KT):
                self.products(pe, self.first_ps(i), i, k, 0, FCH, k == 0 and i < self.FIRST, n)

    def first_lora(self, pe):
        pe.wait_ge(self.lb_low, 1)
        for k in range(KT):
            self.products(pe, self.first_ps(KT), KT, k, 0, FCH, k == 0)

    def later(self, pe):
        def step(j, e, width, last):
            ch = 2 * j + e
            for g in range(0, self.TILES, self.GROUP):
                for k in range(KT):
                    if g == 0 and k % HALF == 0:
                        pe.wait_ge(self.chunk_low, 2 * ch + k // HALF + 1)
                    for i in range(g, g + self.GROUP):
                        if k == 0 and not (isinstance(ch, int) and ch == 1 and g == 0):
                            pe.wait_ge(self.out_low, ch * self.TILES + i + 1 - 2 * self.GROUP)
                        beside = last and self.sums is not None
                        mm = self.products(pe, self.tile_ps(e, i, 2 * width if beside else width), i, k, e, width, k == 0, beside=beside)
                    if last and g + self.GROUP == self.TILES and k < KT - 1:
                        mm.then_inc(self.w_free, 1)

        self.later_chunks(pe, step)


def fold_qkv(nc, a, sem, keep, psum, ring, c, lb_h):
    def sb(name, shape, dt=F32R, stack=keep):
        return stack.enter_context(nc.sbuf_tensor(name, shape, dt))

    with nc.sbuf_tensor("w_raw", [P, KT, D], F32) as raw:
        w_raw = [raw[:, k, :] for k in range(KT)]
    chunks = QKV // FCH
    p1_h, p1_l = sb("p1_h", [P, chunks - 1, KT, FCH]), sb("p1_l", [P, chunks - 1, KT, FCH])
    end_h, end_l = sb("end_h", [P, KT, FCH + BPU * LR]), sb("end_l", [P, KT, FCH + BPU * LR])
    pb = sb("pb", [P, QKV])
    with ExitStack() as st:
        w_h, w_l = sb("w_h", [P, KT, D], stack=st), sb("w_l", [P, KT, D], stack=st)
        lb_l = sb("lb_l", [P, KT, P], stack=st)

    def part(p1, end):
        def columns(i, j, e, w):
            if isinstance(j, int) and 2 * j + e == chunks - 1:
                return end[:, i, 0:w]
            return p1[:, bass.ds(2 * j + e, 1), i, :].rearrange("p o c -> p (o c)")
        return columns

    def up(j, e, w):
        return pb[:, bass.ds((2 * j + e) * FCH, w)]

    def low_rows(j, e, w, src):
        r = slice(LR, 2 * LR)
        out = up(j, e, w)[r]
        return [(out, out, src[r])]

    fold = Fold(sem, "f1", psum, ring, c, 0, a["w_cond"], a["wqkv_t"], a["lora_b"], FCH,
                w_raw, w_h, w_l, lb_h, lb_l, part(p1_h, end_h), part(p1_l, end_l), up, low_rows)
    fold.weights_h, fold.weights_l, fold.pb = (p1_h, end_h), (p1_l, end_l), pb
    return fold


def folding_qkv(fold, begin_next):
    def sync(sp):
        for k in range(KT):
            if k < 2:
                fold.load_chunk(sp, 0, k)
            fold.load_w(sp, k)
        fold.load_lora(sp)

        def step(j, e, width, last):
            fold.load_next_chunk(sp, 2 * j + e)

        fold.later_chunks(sp, step)

    def scalar(act):
        for k in range(KT):
            if k < 2:
                fold.high_half(act, 0, 0, k)
            fold.high_w(act, k)
        fold.high_chunk(act, 1, 1)
        fold.high_lora(act)
        fold.high_first(act)
        fold.high_later(act, begin_next)

    def gpsimd(pool):
        pass

    def vector(dve):
        for k in range(KT):
            if k < 2:
                fold.low_half(dve, 0, 0, k)
            fold.low_w(dve, k)
        fold.low_chunk(dve, 1, 1)
        fold.low_lora(dve)
        fold.low_first(dve)
        fold.low_later(dve)

    def tensor(pe):
        for k in range(KT):
            fold.first(pe, k)
        fold.first_lora(pe)
        fold.later(pe)

    return Programs(sync, scalar, gpsimd, vector, tensor)


def load_unit(sp, sem, a, ring, u, half):
    cols = slice(half * HALF * P, (half + 1) * HALF * P)
    sp.dma_start(ring[:, 3, cols], a["x_t"][bass.ds(u, 1), :, half * HALF:(half + 1) * HALF, :]
                 .rearrange("o p k t -> (o p) (k t)")).then_inc(sem(f"x_in{half}"), 16)


def attention(nc, a, sem, keep, psum, ring, c_h, c_l, a_raw, index, fold1, fold2):
    def sb(name, shape, dt=F32):
        return keep.enter_context(nc.sbuf_tensor(name, shape, dt))

    w_h, w_l, pb = fold1.weights_h, fold1.weights_l, fold1.pb
    x_raw = by_tile(ring[:, 3, :])
    x_h, x_l = (by_tile(part) for part in halves(c_h, 0))
    a_h, a_l = (w[1][:, :, FCH:FCH + BPU * LR] for w in (w_h, w_l))
    low4 = sb("low4", [P, 4, LR])
    lows = sb("lows", [P, P], F32R)
    qkv = sb("qkv", [P, QKV])
    b_bc = sb("b_bc", [P, QKV])
    NH = HEADS + KVH
    rot_t = sb("rot_t", [P, 2, NH, HD // 2])
    roped = sb("roped", [P, NH, HD // 2, 2])
    q_h, q_l = (sb(n, [P, BPU, QUADS * GRP, SEQ], F32R) for n in ("q_h", "q_l"))
    keys = sb("keys", [P, QUADS * P])
    k_h, k_l = (sb(n, [P, QUADS, BPU, 4, SEQ], F32R) for n in ("k_h", "k_l"))
    v_hl = sb("v_hl", [P, 2, QUADS, 2, 2, HD], F32R)
    vb_h, vb_l = (sb(n, [P, BPU, QUADS, 2, 4, HD], F32R) for n in ("vb_h", "vb_l"))
    prob = sb("prob", [P, BPU, 2, KVH, SEQ])
    smax, ssum, sinv = (sb(n, [P, BPU, 2, KVH]) for n in ("smax", "ssum", "sinv"))
    pt_h, pt_l = (sb(n, [P, QUADS, 2, 2, P], F32R) for n in ("pt_h", "pt_l"))
    attn = ring[:, 2, :].rearrange("p (k b t) -> p k b t", k=KT, b=BPU)
    cos, sin = sb("cos", [P, HD // 2]), sb("sin", [P, HD // 2])
    hmask = sb("hmask", [P, 4])
    ident = sb("ident", [P, P])
    mask_l = sb("mask_l", [P, P], BF16)
    mask_r = sb("mask_r", [P, BANK], BF16)
    mask_f = prob[:, 0, :, :, :].rearrange("p g c k -> p (g c k)")
    out = [psum[:, n, :].rearrange("p (o c) -> p o c", o=2) for n in range(2)] + [psum[:, 2, 0:FCH], psum[:, 3, 0:FCH]]
    down_ps = psum[:, 3, FCH:FCH + BPU * LR]
    s_ps, t_ps = psum[:, 4:6, :], psum[:, 6:8, :]
    low_ps = t_ps[:, 1, 0:P]

    const_in, index_in, mask_ready = sem("const_in"), sem("index_in"), sem("mask_ready")
    x_in = [sem("x_in0"), sem("x_in1")]
    a_in = sem("a_in")
    x_high, x_low, a_high, a_low = sem("x_high"), sem("x_low"), sem("a_high"), sem("a_low")
    half_done = sem("half_done")
    low_copied, low_t, low_high, low_ready = sem("low_copied"), sem("low_t"), sem("low_high"), sem("low_ready")
    qkv_done, qkv_out = sem("qkv_done"), sem("qkv_out")
    bank_out, low_done = sem("bank_out"), sem("low_done")
    rot_re, rot_im, rotated = sem("rot_re"), sem("rot_im"), sem("rotated")
    qk_t, qk_high, qk_low = sem("qk_t"), sem("qk_high"), sem("qk_low")
    k_out, k_high, k_low = sem("k_out"), sem("k_high"), sem("k_low")
    v_high, v_low, vb_zero, vb_high, vb_low = (sem(n) for n in ("v_high", "v_low", "vb_zero", "vb_high", "vb_low"))
    s_done, s_max, s_sub, s_exp, s_sum, s_inv, s_norm = (
        sem(n) for n in ("s_done", "s_max", "s_sub", "s_exp", "s_sum", "s_inv", "s_norm"))
    pt_done, pt_high, pt_low = sem("pt_done"), sem("pt_high"), sem("pt_low")
    pv_done, pv_out, stored = sem("pv_done"), sem("pv_out"), sem("attn_stored")
    consts = [(b_bc[:, :], a["b_qkv"].partition_broadcast(P)), (cos[:, :], a["cos"]), (sin[:, :], a["sin"]),
              (hmask[:, :], a["hmask"]), (ident[:, :], a["ident"]), (mask_f[:, BANK:BANK + P], a["mask_l"]),
              (mask_f[:, 0:BANK], a["mask_r"])]

    def k_tiles():
        return keys[:, :].rearrange("p (n t) -> p n t", t=SEQ)

    def q_ps(turn, at, n):
        return t_ps[:, turn, at * P:(at + n) * P].rearrange("p (n b t) -> p n b t", n=n, b=BPU)

    def diag(vb, b, h):
        flat = vb[h * SEQ:(h + 1) * SEQ, b, :, :, :, :].rearrange("p q j c d -> p q (j c d)")
        return flat.rearrange("p q (m d) -> p q m d", d=HD)[:, :, h:h + 7:6, :]

    TURNS = [(0, ["k0", "k1", 0, 1]), (1, [2, 3, 4, 5]), (0, [6, 7])]

    def steps(engine, step):
        step(0, True, False, False, True)
        step(1, True, True, False, True)
        with engine.Fori(2, UNITS - 1) as u:
            step(u, True, True, True, True)
        step(UNITS - 1, True, True, True, False)
        step(UNITS, False, True, True, False)
        step(UNITS + 1, False, False, True, False)

    def ks(half):
        return slice(half * HALF, (half + 1) * HALF)

    def sync(sp):
        def load_x(u):
            for half in range(2):
                need(sp, x_low, 2 * u + half - 1)
                load_unit(sp, sem, a, ring, u, half)

        def load_a(u):
            need(sp, a_low, u)
            for b in range(BPU):
                lab = sp.value_load(index[0:1, bass.ds(u * BPU + b, 1)], min_val=0, max_val=LAB - 1)
                sp.dma_start(a_raw[:, b, :, :], a["lora_a"][bass.ds(lab, 1), :, :, :].rearrange("o p k r -> (o p) k r")).then_inc(a_in, 16)

        def step(u, main, score, value, nxt):
            w = u - 2
            if nxt:
                load_x(u + 1)
                load_a(u + 1)
            if score and not value:
                sp.wait_ge(fold2.chunk_low, 2)
                for k in range(fold2.early):
                    fold2.load_w(sp, k)
            if score and not main:
                sp.wait_ge(half_done, 2 * UNITS)
                for k in range(fold2.early, KT):
                    fold2.load_w(sp, k)
                sp.wait_ge(x_low, 2 * UNITS)
                fold2.load_lora(sp)
                sp.wait_ge(fold2.w_low, fold2.early)
                for h in range(2):
                    fold2.load_chunk(sp, 1, h)
            if value:
                sp.wait_ge(pv_out, 2 * w + 2)
                sp.dma_start(a["attn"][bass.ds(w, 1), :, :].rearrange("o p c -> (o p) c"),
                             attn[:, :, :, :].rearrange("p k b t -> p (k b t)")).then_inc(stored, 16)

        sp.wait_ge(fold1.lb_low, 1)
        for half in range(2):
            load_unit(sp, sem, a, ring, 0, half)
        sp.wait_ge(fold1.done, fold1.TILES * (fold1.chunks - 1))
        sp.dma_start(index[:, :], a["labeler"]).then_inc(index_in, 16)
        sp.wait_ge(index_in, 16)
        load_a(0)
        sp.wait_ge(fold1.done, fold1.TILES * fold1.chunks)
        for dst, src in consts:
            sp.dma_start(dst, src).then_inc(const_in, 16)
        for h in range(2):
            fold2.load_chunk(sp, 0, h)
        steps(sp, step)
        sp.wait_ge(stored, 16 * UNITS)

    def high_x(act, u, half):
        act.wait_ge(x_in[half], 16 * (u + 1))
        need(act, half_done, 2 * u + half - 1)
        act.activation(x_h[:, ks(half), :], x_raw[:, ks(half), :], ACT.Copy).then_inc(x_high, 1)

    def high_a(act, u):
        act.wait_ge(a_in, 32 * (u + 1))
        need(act, low_done, u)
        act.activation(a_h[:, :, :].rearrange("p k (b r) -> p b k r", b=BPU), a_raw[:, :, :, :], ACT.Copy).then_inc(a_high, 1)

    def begin(act):
        high_x(act, 0, 0)
        high_a(act, 0)
        high_x(act, 0, 1)

    def scalar(act):
        def queries(v, turn, at, n0, n1):
            return act.activation(q_h[:, :, n0:n1, :].rearrange("p b n t -> p n b t"), q_ps(turn, at, n1 - n0), ACT.Copy)

        def values_out(w, b):
            act.wait_ge(pv_done, 2 * w + b + 1)
            if b == 0:
                need(act, stored, 16 * w)
            act.activation(attn[:, :, b, :], s_ps[:, b, :].rearrange("p (k t) -> p k t", k=KT), ACT.Copy).then_inc(pv_out, 1)

        def probs_high(w, b):
            act.wait_ge(pt_done, 2 * w + b + 1)
            act.activation(pt_h[:, :, :, :, :].rearrange("p q j g t -> p q (j g t)"), t_ps[:, :, :], ACT.Copy).then_inc(pt_high, 1)

        def exp_scores(v, b, sums):
            act.wait_ge(s_sub, 2 * v + b + 1)
            if sums:
                for g in range(2):
                    for c in range(KVH):
                        last = act.activation(prob[:, 0, g, c, :], prob[:, 0, g, c, :], ACT.Exp, scale=SCALE, accum_out=ssum[:, 0, g, c:c + 1])
            else:
                last = act.activation(prob[:, b, :, :, :], prob[:, b, :, :, :], ACT.Exp, scale=SCALE)
            last.then_inc(s_exp, 1)

        def step(u, main, score, value, nxt):
            v, w = u - 1, u - 2
            if value:
                probs_high(w, 0)
            if score:
                act.wait_ge(qkv_out, v + 1)
                act.activation(v_hl[:, 0, :, :, :, :].rearrange("p q j h d -> p (q j h d)"), qkv[:, QK:QKV], ACT.Copy).then_inc(v_high, 1)
            if value:
                if score and not main:
                    fold2.high_w(act, 1)
                values_out(w, 0)
                if not score:
                    fold2.high_lora(act)
                probs_high(w, 1)
                if not main:
                    if score:
                        fold2.high_w(act, 2)
                        fold2.high_w(act, 3)
                    else:
                        fold2.high_chunk(act, 1, 1)
                values_out(w, 1)
            if score:
                act.wait_ge(qk_t, 3 * v + 1)
                need(act, k_low, v)
                act.activation(keys[:, :], t_ps[:, 0, 0:QUADS * P], ACT.Copy).then_inc(k_out, 1)
                queries(v, 0, 2, 0, 2).then_inc(qk_high, 1)
                act.wait_ge(qk_t, 3 * v + 2)
                queries(v, 1, 0, 2, 6).then_inc(qk_high, 1)
                act.wait_ge(k_out, v + 1)
                for c in range(4):
                    act.activation(k_h[:, :, :, c, :].rearrange("p q b t -> p (q b) t"), k_tiles(), ACT.Copy, scale=hmask[:, c:c + 1]).then_inc(k_high, 1)
                act.wait_ge(qk_t, 3 * v + 3)
                queries(v, 0, 0, 6, 8).then_inc(qk_high, 1)
                act.wait_ge(v_high, v + 1)
                act.wait_ge(vb_zero, 2)
                need(act, pv_done, 2 * v)
                for b in range(BPU):
                    for h in range(2):
                        last = act.activation(diag(vb_h, b, h), v_hl[b * SEQ:(b + 1) * SEQ, 0, :, :, h, :].bitcast(F32), ACT.Copy)
                last.then_inc(vb_high, 1)
                if not main:
                    fold2.high_w(act, 4)
            if nxt:
                high_x(act, u + 1, 0)
            if score:
                if not main:
                    fold2.high_w(act, 5)
                    fold2.high_w(act, 6)
                exp_scores(v, 0, main)
                if not main:
                    fold2.high_w(act, 7)
                exp_scores(v, 1, False)
            if main:
                act.wait_ge(low_done, u + 1)
                for b in range(BPU):
                    rows = slice(b * SEQ, (b + 1) * SEQ)
                    last = act.activation(low4[rows, :, :], down_ps[rows, b * LR:(b + 1) * LR].unsqueeze(1).to_broadcast([SEQ, 4, LR]), ACT.Copy, scale=LORA_SCALE)
                last.then_inc(low_copied, 1)
                act.wait_ge(low_t, u + 1)
                act.activation(lows[:, :], low_ps, ACT.Copy).then_inc(low_high, 1)
            if nxt:
                high_a(act, u + 1)
                high_x(act, u + 1, 1)
            elif main:
                act.wait_ge(half_done, 2 * UNITS)
                fold2.high_w(act, 0)

        act.wait_ge(const_in, 16 * len(consts))
        act.activation(mask_r[:, :], mask_f[:, 0:BANK], ACT.Copy)
        act.activation(mask_l[:, :], mask_f[:, BANK:BANK + P], ACT.Copy).then_inc(mask_ready, 1)
        fold2.high_chunk(act, 0, 0)
        steps(act, step)

    def gpsimd(pool):
        def split_x(u, half):
            pool.wait_ge(x_high, 2 * u + half + 1)
            pool.tensor_tensor(x_l[:, ks(half), :], x_raw[:, ks(half), :], x_h[:, ks(half), :].bitcast(F32), ALU.subtract).then_inc(x_low, 1)

        def split_a(u):
            pool.wait_ge(a_high, u + 1)
            pool.tensor_tensor(a_l[:, :, :].rearrange("p k (b r) -> p b k r", b=BPU), a_raw[:, :, :, :],
                               a_h[:, :, :].bitcast(F32).rearrange("p k (b r) -> p b k r", b=BPU), ALU.subtract).then_inc(a_low, 1)

        def normalise(v, b):
            pool.wait_ge(s_inv, 2 * v + b + 1)
            rows = prob[:, b, :, :, :].rearrange("p g c k -> p (g c) k")
            pool.tensor_tensor(rows, rows, sinv[:, b, :, :].rearrange("p g c -> p (g c)").unsqueeze(2).to_broadcast([P, 2 * KVH, SEQ]),
                               ALU.mult).then_inc(s_norm, 1)

        def step(u, main, score, value, nxt):
            v = u - 1
            if score:
                pool.wait_ge(rot_re, v + 1)
                pool.tensor_tensor(roped[:, :, :, 0], roped[:, :, :, 0], rot_t[:, 0, :, :], ALU.subtract).then_inc(rotated, 1)
                pool.wait_ge(rot_im, v + 1)
                pool.tensor_tensor(roped[:, :, :, 1], roped[:, :, :, 1], rot_t[:, 1, :, :], ALU.add).then_inc(rotated, 1)
            if nxt:
                split_x(u + 1, 0)
            if score:
                normalise(v, 0)
            if nxt:
                split_a(u + 1)
                split_x(u + 1, 1)
            if score:
                normalise(v, 1)

        split_x(0, 0)
        split_a(0)
        split_x(0, 1)
        pool.wait_ge(fold1.done, fold1.TILES * fold1.chunks)
        pool.memset(vb_h[:, :, :, :, :, :].bitcast(F32), 0.0).then_inc(vb_zero, 1)
        pool.memset(vb_l[:, :, :, :, :, :].bitcast(F32), 0.0).then_inc(vb_zero, 1)
        steps(pool, step)

    def vector(dve):
        def rotate(v, part):
            pairs = qkv[:, 0:QK].rearrange("p (h i two) -> p h i two", i=HD // 2, two=2)
            for n, (dst, table) in enumerate(((roped[:, :, :, part], (cos, sin)[part]), (rot_t[:, part, :, :], (sin, cos)[part]))):
                last = dve.tensor_tensor(dst, pairs[:, :, :, n], table[:, :].unsqueeze(1).to_broadcast([P, NH, HD // 2]), ALU.mult)
            last.then_inc((rot_re, rot_im)[part], 1)

        def probs_low(w, b):
            dve.wait_ge(pt_high, 2 * w + b + 1)
            dve.tensor_tensor(pt_l[:, :, :, :, :].rearrange("p q j g t -> p q (j g t)"), t_ps[:, :, :],
                              pt_h[:, :, :, :, :].bitcast(F32).rearrange("p q j g t -> p q (j g t)"), ALU.subtract).then_inc(pt_low, 1)

        def queries(v, turn, at, n0, n1):
            dve.tensor_tensor(q_l[:, :, n0:n1, :].rearrange("p b n t -> p n b t"), q_ps(turn, at, n1 - n0),
                              q_h[:, :, n0:n1, :].bitcast(F32).rearrange("p b n t -> p n b t"), ALU.subtract).then_inc(qk_low, 1)

        def flat(b):
            return prob[:, b, :, :, :].rearrange("p g c k -> p (g c) k")

        def row(t, b):
            return t[:, b, :, :].rearrange("p g c -> p (g c)")

        def inverse_sum(v, b, summed=False):
            dve.wait_ge(s_exp, 2 * v + b + 1)
            if not summed:
                dve.tensor_reduce(row(ssum, b), flat(b), AX.X, ALU.add).then_inc(s_sum, 1)
                dve.wait_ge(s_sum, UNITS + b if isinstance(v, int) and v == UNITS - 1 else v + 1)
            dve.reciprocal(row(sinv, b), row(ssum, b)).then_inc(s_inv, 1)

        def step(u, main, score, value, nxt):
            v, w = u - 1, u - 2
            if value:
                if score and not main:
                    fold2.low_w(dve, 0)
                probs_low(w, 0)
            if score:
                dve.wait_ge(qkv_out, v + 1)
                dve.wait_ge(const_in, 16 * len(consts))
                need(dve, rotated, 2 * v)
                need(dve, qk_t, 3 * v)
                rotate(v, 0)
                rotate(v, 1)
                dve.wait_ge(v_high, v + 1)
                dve.tensor_tensor(v_hl[:, 1, :, :, :, :].rearrange("p q j h d -> p (q j h d)"), qkv[:, QK:QKV],
                                  v_hl[:, 0, :, :, :, :].rearrange("p q j h d -> p (q j h d)").bitcast(F32), ALU.subtract).then_inc(v_low, 1)
            if value and not score:
                inverse_sum(w, 1)
                fold2.low_w(dve, 7)
                fold2.low_lora(dve)
            if score and not main:
                fold2.low_w(dve, 1)
            if value:
                probs_low(w, 1)
            if score and not main:
                fold2.low_w(dve, 2)
                fold2.low_w(dve, 3)
            if value and not score:
                fold2.low_chunk(dve, 1, 1)
            if score:
                dve.wait_ge(qk_high, 3 * v + 1)
                queries(v, 0, 2, 0, 2)
                dve.wait_ge(qk_high, 3 * v + 2)
                queries(v, 1, 0, 2, 6)
                for c in range(4):
                    dve.wait_ge(k_high, 4 * v + c + 1)
                    last = dve.scalar_tensor_tensor(k_l[:, :, :, c, :].rearrange("p q b t -> p (q b) t"), k_tiles(), hmask[:, c:c + 1],
                                                    k_h[:, :, :, c, :].bitcast(F32).rearrange("p q b t -> p (q b) t"), ALU.mult, ALU.subtract)
                last.then_inc(k_low, 1)
                dve.wait_ge(qk_high, 3 * v + 3)
                queries(v, 0, 0, 6, 8)
                dve.wait_ge(v_low, v + 1)
                dve.wait_ge(vb_zero, 2)
                need(dve, pv_done, 2 * v)
                for b in range(BPU):
                    for h in range(2):
                        last = dve.tensor_copy(diag(vb_l, b, h), v_hl[b * SEQ:(b + 1) * SEQ, 1, :, :, h, :].bitcast(F32))
                last.then_inc(vb_low, 1)
                if not main:
                    fold2.low_w(dve, 4)
                scores = s_ps[:, :, :].rearrange("p g (c k) -> p (g c) k", k=SEQ)

                def less_max(b):
                    dve.wait_ge(s_done, 2 * v + b + 1)
                    dve.tensor_reduce(row(smax, b), scores, AX.X, ALU.max).then_inc(s_max, 1)
                    dve.wait_ge(s_max, 2 * v + b + 1)
                    dve.tensor_tensor(flat(b), scores, row(smax, b).unsqueeze(2).to_broadcast([P, 2 * KVH, SEQ]), ALU.subtract).then_inc(s_sub, 1)

                less_max(0)
                if main:
                    less_max(1)
                    inverse_sum(v, 0, True)
                else:
                    fold2.low_w(dve, 5)
                    inverse_sum(v, 0)
                    fold2.low_w(dve, 6)
                    less_max(1)
            if score and main:
                inverse_sum(v, 1)
            if main:
                dve.wait_ge(low_high, u + 1)
                rows = slice(2 * LR, 3 * LR)
                dve.tensor_tensor(lows[rows, :], low_ps[rows, :], lows[rows, :].bitcast(F32), ALU.subtract).then_inc(low_ready, 1)
                need(dve, v_high, u)
                need(dve, v_low, u)
                need(dve, rot_im, u)
                dve.wait_ge(const_in, 16 * len(consts))
                for n in range(NCH):
                    dve.wait_ge(qkv_done, NCH * u + n + 1)
                    to, bias = (t[:, n * BANK:(n + 1) * BANK].rearrange("p (o c) -> p o c", o=2) for t in (qkv, b_bc))
                    dve.tensor_tensor(to, out[n] if n < NCH - 1 else psum[:, 2:4, 0:FCH], bias, ALU.add).then_inc(bank_out if n < NCH - 1 else qkv_out, 1)

        fold2.low_chunk(dve, 0, 0)
        steps(dve, step)

    def tensor(pe):
        PASSES = ((x_h, w_h), (x_h, w_l), (x_l, w_h))

        def moving(w, n, k):
            chunks, end = w
            return chunks[:, 2 * n:2 * n + 2, k, :] if n < 2 else chunks[:, 4, k, :] if n == 2 else end[:, k, :]

        def parts(k):
            every = range(len(PASSES))
            if k == 0:
                return [[(n, p) for n in pieces for p in every] for pieces in ((0,), (1,), (2, 3))]
            if k < KT - 1:
                return [[(n, p) for n in range(4)] for p in every]
            rest = [[(n, p) for n in range(3)] for p in every]
            return [[(3, p) for p in every] + rest[0]] + rest[1:]

        def project(u, k, part):
            if k % HALF == 0 and part == 0:
                pe.wait_ge(x_low, 2 * u + k // HALF + 1)
            if k == 0 and part == 0:
                pe.wait_ge(a_low, u + 1)
            if isinstance(u, int) and u == 0 and part == 0:
                pe.wait_ge(fold1.out_low, (fold1.chunks - 1) * fold1.TILES + max(k + 1, 2 * fold1.GROUP))
            for n, p in parts(k)[part]:
                first = k == 0 and p == 0
                if first and n < NCH - 1:
                    need(pe, bank_out, (NCH - 1) * (u - 1) + n + 1)
                elif first:
                    need(pe, qkv_out, u)
                to = out[n] if n < 3 else psum[:, 3, 0:FCH + BPU * LR]
                sx, w = PASSES[p]
                mm = pe.matmul(to, sx[:, k, :], moving(w, n, k), start=first, stop=False, skip_group_check=True)
                if k == KT - 1 and n == 3 and p == len(PASSES) - 1:
                    mm.then_inc(low_done, 1)
            if k == KT - 1 and part == 0:
                transpose_down(u)
            if k % HALF == HALF - 1 and part == len(PASSES) - 1:
                mm.then_inc(half_done, 1)

        def transpose_qk(v, turns):
            if 0 in turns:
                pe.wait_ge(rotated, 2 * v + 2)
                need(pe, pt_low, 2 * v)
            flat = roped[:, :, :, :].rearrange("p h i two -> p (h i two)")
            for turn in turns:
                to, tiles = TURNS[turn]
                if turn == 2:
                    pe.wait_ge(qk_low, 3 * v + 1)
                for at, n in enumerate(tiles):
                    col = (QUADS * GRP + int(n[1]) if isinstance(n, str) else n) * P
                    mm = pe.transpose(t_ps[:, to, at * P:(at + 1) * P], flat[:, col:col + P], ident[:, :])
                mm.then_inc(qk_t, 1)

        def scores(v, b):
            if b == 0:
                pe.wait_ge(qk_low, 3 * v + 3)
                pe.wait_ge(k_low, v + 1)
                need(pe, pv_out, 2 * v)
            else:
                pe.wait_ge(s_sub, 2 * v + 1)
            for g in range(2):
                pe.matmul(s_ps[:, g, :], mask_l[:, :], mask_r[:, :], start=True, stop=False)
                for q in range(QUADS):
                    o = s_ps[:, g, q * 4 * SEQ:(q + 1) * 4 * SEQ]
                    cols = slice(q * GRP + 2 * g, q * GRP + 2 * g + 2)
                    for n, (qq, kk) in enumerate(((q_h, k_h), (q_h, k_l), (q_l, k_h))):
                        mm = pe.matmul(o, qq[:, b, cols, :].rearrange("p g t -> p (g t)"), kk[:, q, b, :, :].rearrange("p c t -> p (c t)"),
                                       start=False, stop=q == QUADS - 1 and n == 2)
            mm.then_inc(s_done, 1)

        def transpose_p(v, b):
            pe.wait_ge(s_norm, 2 * v + b + 1)
            if b == 1:
                pe.wait_ge(pt_low, 2 * v + 1)
            for q in range(QUADS):
                for j in range(2):
                    for g in range(2):
                        at = (j * 2 + g) * P
                        c = q * 4 + j * 2
                        mm = pe.transpose(t_ps[:, q, at:at + P], prob[:, b, g, c:c + 2, :].rearrange("p c k -> p (c k)"), ident[:, :])
            mm.then_inc(pt_done, 1)

        def attend(v, b):
            pe.wait_ge(pt_high, 2 * v + b + 1)
            if b == 0:
                pe.wait_ge(vb_high, v + 1)
                pe.wait_ge(vb_low, v + 1)
                pe.wait_ge(s_sub, 2 * v + 2)
            n = 0
            for vv, pp in ((vb_h, pt_h), (vb_l, pt_h), (vb_h, pt_l)):
                if pp is pt_l:
                    pe.wait_ge(pt_low, 2 * v + b + 1)
                for q in range(QUADS):
                    for j in range(2):
                        mm = pe.matmul(s_ps[:, b, q * 4 * SEQ:(q + 1) * 4 * SEQ], vv[:, b, q, j, :, :].rearrange("p c d -> p (c d)"),
                                       pp[:, q, j, :, :].rearrange("p g t -> p (g t)"), start=n == 0, stop=pp is pt_l and j == 1, skip_group_check=True)
                        n += 1
            mm.then_inc(pv_done, 1)

        def transpose_down(u):
            if isinstance(u, int) and u == 0:
                pe.wait_ge(const_in, 16 * len(consts))
                pe.wait_ge(mask_ready, 1)
                pe.wait_ge(fold1.out_low, fold1.chunks * fold1.TILES)
            pe.wait_ge(low_copied, u + 1)
            pe.transpose(low_ps, low4[:, :, :].rearrange("p n r -> p (n r)"), ident[:, :]).then_inc(low_t, 1)

        def up(u):
            pe.wait_ge(low_ready, u + 1)
            for n in range(4):
                cols = pb[:, n * BANK:(n + 1) * BANK].rearrange("p (o c) -> p o c", o=2) if n < 2 else pb[:, (n + 2) * FCH:(n + 3) * FCH]
                mm = pe.matmul(out[n], lows[:, :], cols, start=False, stop=True, skip_group_check=True)
                if n != 2:
                    mm.then_inc(qkv_done, 1)

        BESIDE = {(0, 0): [(transpose_p, 2, 0)], (1, 0): [(attend, 2, 0), (transpose_p, 2, 1)],
                  (2, 1): [(attend, 2, 1), (transpose_qk, 1, (0, 1))], (3, 1): [(transpose_qk, 1, (2,))],
                  (4, 0): [(scores, 1, 0)], (5, 1): [(scores, 1, 1)]}

        def last_values():
            v = UNITS - 1
            transpose_p(v, 0)
            fold2.first(pe, KT - 2)
            attend(v, 0)
            fold2.first(pe, KT - 1)
            transpose_p(v, 1)
            pe.wait_ge(pv_out, 2 * v + 1)
            fold2.first_lora(pe)
            attend(v, 1)

        def step(u, main, score, value, nxt):
            if not main and not score:
                last_values()
                return
            for k in range(KT):
                for part in range(3):
                    for what, back, which in BESIDE.get((k, part), []):
                        if (back == 1 and score) or (back == 2 and value):
                            what(u - back, which)
                    if main:
                        project(u, k, part)
                if not main and k < KT - 2:
                    if k == 0:
                        pe.wait_ge(qkv_out, UNITS)
                    fold2.first(pe, k)
            if main:
                up(u)

        steps(pe, step)
        pe.wait_ge(pv_out, 2 * UNITS)

    return Programs(sync, scalar, gpsimd, vector, tensor), begin


def fold_ffn(nc, a, sem, keep, psum, ring, c, wo_raw):
    def sb(name, shape, dt=F32R):
        return keep.enter_context(nc.sbuf_tensor(name, shape, dt))

    early = [wo_raw[:, 1, :], ring[:, 0, :], ring[:, 1, :]]
    with nc.sbuf_tensor("w2_raw", [P, KT - len(early), D], F32) as raw:
        w_raw = early + [raw[:, k, :] for k in range(KT - len(early))]
    g_h, g_l = sb("g_h", [P, FOUT]), sb("g_l", [P, FOUT])
    lb_h, lb_l = sb("lb2_h", [P, KT, P]), sb("lb2_l", [P, KT, P])
    spare = sb("spare", [P, (KT - 1) * D - 2 * FOUT - 2 * KT * P], F32)
    sums, spare = spare[:, 0:Fold.GROUP * GATED].rearrange("p (n c) -> p n c", c=GATED), spare[:, Fold.GROUP * GATED:]
    w_h, w_l = sb("w2_h", [P, KT, D]), sb("w2_l", [P, KT, D])
    fr_h, fr_l = sb("fr_h", [P, KT, FCOLS]), sb("fr_l", [P, KT, FCOLS])

    def part(fr):
        return lambda i, j, e, w: fr[:, i, bass.ds((2 * j + e) * FCH, w)] if w == FCH else fr[:, i, FOUT:FCOLS]

    def up(g):
        return lambda j, e, w: g[:, bass.ds((2 * j + e) * FCH, w)]

    fold = Fold(sem, "f2", psum, ring, c, 1, a["w_2"], a["last_t"], a["b2_up"], GATED,
                w_raw, w_h, w_l, lb_h, lb_l, part(fr_h), part(fr_l), up(g_h),
                lambda j, e, w, src: [(up(g_l)(j, e, w), up(g_h)(j, e, w), src)], sums)
    fold.fr_h, fold.fr_l, fold.g_h, fold.g_l, fold.spare, fold.early = fr_h, fr_l, g_h, g_l, spare, len(early)
    return fold


def folding_ffn(fold, begin_next, first_weights):
    def sync(sp):
        def step(j, e, width, last):
            if j > 0:
                fold.load_next_chunk(sp, 2 * j + e)

        fold.later_chunks(sp, step)

    def scalar(act):
        fold.high_first(act)
        fold.high_later(act, begin_next, lambda: first_weights[0](act))

    def gpsimd(pool):
        pass

    def vector(dve):
        fold.low_first(dve)
        fold.low_later(dve, lambda: first_weights[1](dve))

    def tensor(pe):
        fold.later(pe)

    return Programs(sync, scalar, gpsimd, vector, tensor)


WEIGHTS = KT + 3


def weight_slot(n):
    return (n % 4, n // 4 + 1) if n < KT else (2 + n % 2, KT // 4 + 1 + (n - KT) // 2)


def weight_piece(ring, wo_raw, a, n):
    at = weight_slot(n)[0]
    slot = wo_raw[:, at, :] if at < 2 else ring[:, at - 2, :]
    if n < KT:
        return slot, a["wo_t"][:, n, :]
    if n == WEIGHTS - 1:
        return slot, a["bf_up"]
    h = n - KT
    return (slot[:, 0:HALF * GATED].rearrange("p (k c) -> p k c", k=HALF), a["gate2_t"][:, h * HALF:(h + 1) * HALF, :])


def load_attn(sp, sem, a, ring, u, half):
    cols = slice(half * HALF * P, (half + 1) * HALF * P)
    sp.dma_start(ring[:, 3, cols], a["attn"][bass.ds(u, 1), :, cols].rearrange("o p c -> (o p) c")).then_inc(sem(f"at_in{half}"), 16)


def load_tokens(sp, sem, a, ring, u):
    sp.dma_start(ring[:, 2, :], a["x_tok"][bass.ds(u, 1), :, :].rearrange("o p d -> (o p) d")).then_inc(sem("xt_in"), 16)


def feed_forward(nc, a, sem, keep, psum, ring, c_h, c_l, wo_raw, x1, x1_out, fold2):
    def sb(name, shape, dt=F32):
        return keep.enter_context(nc.sbuf_tensor(name, shape, dt))

    used = [0]

    def take(*shape, dt=F32):
        at, used[0] = used[0], used[0] + int(np.prod(shape))
        assert used[0] <= fold2.spare.shape[1]
        flat = fold2.spare[:, at:used[0]]
        flat = flat if dt is F32 else flat.bitcast(dt)
        return flat if len(shape) == 1 else flat.rearrange("p (m n) -> p m n", m=shape[0])

    fr_h, fr_l, g_h, g_l = fold2.fr_h, fold2.fr_l, fold2.g_h, fold2.g_l
    wo_h, wo_l = fold2.w_h, fold2.w_l
    at_raw = by_tile(ring[:, 3, :])
    x_raw = ring[:, 2, :]
    at_h, at_l = (by_tile(part) for part in halves(c_h, 0))
    bf_h, bf_l = halves(c_l, 0)
    x1t_h, x1t_l = (by_tile(part) for part in halves(c_l, 1))
    bo_bc, bb_bc = take(D), take(D)
    ident = take(P)
    before = take(EXP, EXP)
    experts = take(EXP)
    lang, lang_f = take(UNITS, dt=I32), take(UNITS)
    lang_bias = sb("lang_bias", [P, UNITS, EXP])
    lg, ex, rank, pick, gate = (sb(n, [P, EXP]) for n in ("lg", "ex", "rank", "pick", "gate"))
    above, ties = sb("above", [P, EXP, EXP]), sb("ties", [P, EXP, EXP])
    top, total, share = sb("top", [P, 1]), sb("total", [P, 1]), sb("share", [P, 1])
    z = sb("z", [P, EXP, ER])
    zt_h, zt_l = fold2.lb_h[:, 0, :], fold2.lb_h[:, 1, :]
    w_ps = psum[:, 3:5, :]
    b_ps = psum[:, 0:3, :]
    x_ps = psum[:, 5:7, :]
    z_ps = psum[:, 7, :]

    consts_in = sem("consts4_in")
    w_in = [sem(f"w4_in{at}") for at in range(4)]
    w_high, w_low = sem("w4_high"), sem("w4_low")
    at_in = [sem("at_in0"), sem("at_in1")]
    x_in, x_bias = sem("xt_in"), sem("x_bias")
    at_high, at_low, wo_done = sem("at_high"), sem("at_low"), sem("wo_done")
    x1_ready, x1_t, x1_high, x1_low, x1_biased = (sem(n) for n in ("x1_ready", "x1_t", "x1_high", "x1_low", "x1_biased"))
    lang_step, f_done, up_done, base_done = sem("lang_step"), sem("f_done"), sem("up_done"), sem("base_done")
    route_step, route_exp = sem("route_step"), sem("route_exp")
    z_t, z_high, z_low = sem("z_t"), sem("z_high"), sem("z_low")
    out_ready, out_stored = sem("out_ready"), sem("out_stored")
    FIRST = 4
    ROUTE_STEPS = 13
    consts = [(bo_bc[:, :], a["b_o"].partition_broadcast(P)), (bb_bc[:, :], a["b_base"].partition_broadcast(P)),
              (ident[:, :], a["ident"]), (before[:, :, :].rearrange("p e j -> p (e j)"), a["before"]), (experts[:, :], a["experts"])]
    consts += [(lang[b * SEQ:(b + 1) * SEQ, :], a["language"][b, :].partition_broadcast(SEQ)) for b in range(BPU)]
    weights = [(wo_h[:, k, :], wo_l[:, k, :]) for k in range(KT)]
    weights += [(fr_h[:, ks, D:FOUT], fr_l[:, ks, D:FOUT]) for ks in (slice(0, HALF), slice(HALF, KT))] + [(bf_h[:, :], bf_l[:, :])]

    def steps(engine, step):
        step(0, True, False, True)
        with engine.Fori(1, UNITS - 1) as u:
            step(u, True, True, True)
        step(UNITS - 1, True, True, False)
        step(UNITS, False, True, False)

    def ks(half):
        return slice(half * HALF, (half + 1) * HALF)

    def sync(sp):
        sp.wait_ge(fold2.lb_low, 1)
        for half in range(2):
            load_attn(sp, sem, a, ring, 0, half)
        load_tokens(sp, sem, a, ring, 0)
        sp.wait_ge(fold2.w_low, KT)
        for dst, src in consts:
            sp.dma_start(dst, src).then_inc(consts_in, 16)
        for n in range(WEIGHTS):
            at, times = weight_slot(n)
            if n < 2:
                sp.wait_ge(fold2.done, fold2.TILES * (fold2.chunks - 1))
            elif n < 4:
                sp.wait_ge(fold2.chunk_low, 2 * fold2.chunks - 3 + n)
            else:
                sp.wait_ge(w_low, n - 3 if n < KT else n - 1)
            dst, src = weight_piece(ring, wo_raw, a, n)
            sp.dma_start(dst, src).then_inc(w_in[at], 16)

        def step(u, main, gating, nxt):
            v = u - 1
            if nxt:
                for half in range(2):
                    sp.wait_ge(at_low, 2 * u + half + 1)
                    load_attn(sp, sem, a, ring, u + 1, half)
                sp.wait_ge(x1_ready, 2 * u + 2)
                load_tokens(sp, sem, a, ring, u + 1)
            if gating:
                sp.wait_ge(out_ready, 2 * v + 2)
                sp.dma_start(a["out"][bass.ds(v, 1), :, :].rearrange("o p d -> (o p) d"), x1_out[:, :]).then_inc(out_stored, 16)

        steps(sp, step)
        sp.wait_ge(out_stored, 16 * UNITS)

    def high_attn(act, u, half):
        act.wait_ge(at_in[half], 16 * (u + 1))
        need(act, wo_done, 2 * u)
        act.activation(at_h[:, ks(half), :], at_raw[:, ks(half), :], ACT.Copy).then_inc(at_high, 1)

    def high_weight(act, n):
        at, times = weight_slot(n)
        act.wait_ge(w_in[at], 16 * times)
        act.activation(weights[n][0], weight_piece(ring, wo_raw, a, n)[0], ACT.Copy).then_inc(w_high, 1)

    def low_weight(dve, n):
        dve.wait_ge(w_high, n + 1)
        dve.tensor_tensor(weights[n][1], weight_piece(ring, wo_raw, a, n)[0], weights[n][0].bitcast(F32), ALU.subtract).then_inc(w_low, 1)

    def high_first(act):
        for n in range(FIRST):
            act.wait_ge(fold2.w_free, n + 1)
            high_weight(act, n)

    def low_first(dve):
        for n in range(FIRST):
            low_weight(dve, n)

    def begin(act):
        for half in range(2):
            high_attn(act, 0, half)

    def scalar(act):
        def gated(v, r):
            act.wait_ge(route_step, (v * 2 + r) * ROUTE_STEPS + 3)
            act.activation(ex[:, :], ex[:, :], ACT.Exp).then_inc(route_exp, 1)
            act.wait_ge(z_t, 2 * v + r + 1)
            act.activation(zt_h[:, :], z_ps[:, 0:P], ACT.Copy).then_inc(z_high, 1)

        def step(u, main, gating, nxt):
            v = u - 1
            if gating:
                gated(v, 0)
                gated(v, 1)
            if main:
                for half in range(2):
                    act.wait_ge(x1_t, 2 * u + half + 1)
                    act.activation(x1t_h[:, ks(half), :].rearrange("p k t -> p (k t)"), x_ps[:, half, :], ACT.Copy).then_inc(x1_high, 1)
                    if not gating:
                        high_weight(act, KT + half)
                if not gating:
                    high_weight(act, WEIGHTS - 1)
            if nxt:
                high_attn(act, u + 1, 0)
                high_attn(act, u + 1, 1)

        for n in range(FIRST, KT):
            high_weight(act, n)
        steps(act, step)

    def gpsimd(pool):
        def split_attn(u, half):
            pool.wait_ge(at_high, 2 * u + half + 1)
            pool.tensor_tensor(at_l[:, ks(half), :], at_raw[:, ks(half), :], at_h[:, ks(half), :].bitcast(F32), ALU.subtract).then_inc(at_low, 1)

        def bias_x(u):
            pool.wait_ge(x_in, 16 * (u + 1))
            pool.tensor_tensor(x_raw, x_raw, bo_bc[:, :], ALU.add).then_inc(x_bias, 1)

        def step(u, main, gating, nxt):
            if main:
                pool.wait_ge(x1_ready, 2 * u + 2)
                need(pool, out_stored, 16 * u)
                pool.tensor_tensor(x1_out[:, :], x1[:, :], bb_bc[:, :], ALU.add).then_inc(x1_biased, 1)
            if nxt:
                split_attn(u + 1, 0)
                split_attn(u + 1, 1)
                bias_x(u + 1)

        pool.wait_ge(consts_in, 16 * len(consts))
        split_attn(0, 0)
        split_attn(0, 1)
        bias_x(0)
        steps(pool, step)

    def vector(dve):
        dve.wait_ge(consts_in, 16 * len(consts))
        dve.tensor_copy(lang_f[:, :], lang[:, :]).then_inc(lang_step, 1)
        dve.wait_ge(lang_step, 1)
        dve.tensor_tensor(lang_bias[:, :, :], experts[:, :].unsqueeze(1).to_broadcast([P, UNITS, EXP]),
                          lang_f[:, :].unsqueeze(2).to_broadcast([P, UNITS, EXP]), ALU.is_equal).then_inc(lang_step, 1)
        dve.wait_ge(lang_step, 2)
        dve.tensor_scalar(lang_bias[:, :, :], lang_bias[:, :, :], LANG_BIAS, None, ALU.mult).then_inc(lang_step, 1)
        dve.wait_ge(lang_step, 3)
        for n in range(FIRST, KT):
            low_weight(dve, n)

        def route(v, r):
            steps_before = (v * 2 + r) * ROUTE_STEPS
            count = [0]

            def link(instruction):
                count[0] += 1
                instruction.then_inc(route_step, 1)
                dve.wait_ge(route_step, steps_before + count[0])

            at = r * GATED
            logits, down = b_ps[:, 2, at:at + EXP], b_ps[:, 2, at + EXP:at + GATED]
            if r == 0:
                dve.wait_ge(f_done, v + 1)
                link(dve.tensor_tensor(lg[:, :], logits, lang_bias[:, bass.ds(v, 1), :].rearrange("p o e -> p (o e)"), ALU.add))
            else:
                dve.wait_ge(up_done, v + 1)
                link(dve.tensor_copy(lg[:, :], logits))
            link(dve.tensor_reduce(top[:, :], lg[:, :], AX.X, ALU.max))
            link(dve.tensor_scalar(ex[:, :], lg[:, :], top[:, :], None, ALU.subtract))
            mine = lg[:, :].unsqueeze(2).to_broadcast([P, EXP, EXP])
            other = lg[:, :].unsqueeze(1).to_broadcast([P, EXP, EXP])
            link(dve.tensor_tensor(ties[:, :, :], other, mine, ALU.is_equal))
            link(dve.tensor_tensor(above[:, :, :], other, mine, ALU.is_gt))
            link(dve.tensor_tensor(ties[:, :, :], ties[:, :, :], before[:, :, :], ALU.mult))
            link(dve.tensor_tensor(above[:, :, :], above[:, :, :], ties[:, :, :], ALU.add))
            link(dve.tensor_reduce(rank[:, :], above[:, :, :], AX.X, ALU.add))
            dve.wait_ge(route_exp, 2 * v + r + 1)
            link(dve.scalar_tensor_tensor(pick[:, :], rank[:, :], 1.5, ex[:, :], ALU.is_lt, ALU.mult))
            link(dve.tensor_reduce(total[:, :], pick[:, :], AX.X, ALU.add))
            link(dve.reciprocal(share[:, :], total[:, :]))
            link(dve.tensor_scalar(gate[:, :], pick[:, :], share[:, :], MOE_SCALE, ALU.mult, ALU.mult))
            link(dve.tensor_tensor(z[:, :, :], down.rearrange("p (e r) -> p e r", e=EXP),
                                   gate[:, :].unsqueeze(2).to_broadcast([P, EXP, ER]), ALU.mult))
            assert count[0] == ROUTE_STEPS
            dve.wait_ge(z_high, 2 * v + r + 1)
            dve.tensor_tensor(zt_l[:, :], z_ps[:, 0:P], zt_h[:, :].bitcast(F32), ALU.subtract).then_inc(z_low, 1)

        def residual(u, half):
            dve.wait_ge(wo_done, 2 * u + half + 1)
            if half == 0:
                dve.wait_ge(x_bias, u + 1)
                need(dve, x1_biased, u)
                need(dve, x1_t, 2 * u)
            cols = slice(half * BANK, (half + 1) * BANK)
            dve.tensor_tensor(x1[:, cols], w_ps[:, half, :], x_raw[:, cols], ALU.add).then_inc(x1_ready, 1)

        def split_x1(u, half):
            dve.wait_ge(x1_high, 2 * u + half + 1)
            dve.tensor_tensor(x1t_l[:, ks(half), :].rearrange("p k t -> p (k t)"), x_ps[:, half, :],
                              x1t_h[:, ks(half), :].rearrange("p k t -> p (k t)").bitcast(F32), ALU.subtract).then_inc(x1_low, 1)

        def step(u, main, gating, nxt):
            v = u - 1
            if gating:
                route(v, 0)
            if main:
                residual(u, 0)
            if gating:
                route(v, 1)
            if main:
                split_x1(u, 0)
                residual(u, 1)
                if not gating:
                    low_weight(dve, KT)
            if gating:
                dve.wait_ge(x1_biased, v + 1)
                for n in range(2):
                    cols = slice(n * BANK, (n + 1) * BANK)
                    dve.wait_ge(base_done, 2 * v + n + 1)
                    dve.tensor_tensor(x1_out[:, cols], b_ps[:, n, :], x1_out[:, cols], ALU.add).then_inc(out_ready, 1)
            if main:
                split_x1(u, 1)
            if main and not gating:
                for n in range(KT + 1, WEIGHTS):
                    low_weight(dve, n)

        steps(dve, step)

    def tensor(pe):
        def project(u, n, k):
            if n == 0 and k % HALF == 0:
                pe.wait_ge(at_low, 2 * u + k // HALF + 1)
            if n == 0 and isinstance(u, int) and u == 0:
                pe.wait_ge(w_low, k + 1)
            if k == 0:
                need(pe, x1_ready, 2 * u - 1 + n)
            for s, w in ((at_h, wo_h), (at_h, wo_l), (at_l, wo_h)):
                mm = pe.matmul(w_ps[:, n, :], s[:, k, :], w[:, k, n * BANK:(n + 1) * BANK],
                               start=k == 0 and s is at_h and w is wo_h, stop=k == KT - 1 and s is at_l)
            if k == KT - 1:
                mm.then_inc(wo_done, 1)

        def transpose_z(v, r):
            pe.wait_ge(route_step, (v * 2 + r + 1) * ROUTE_STEPS)
            need(pe, z_low, 2 * v + r)
            pe.transpose(z_ps[:, 0:P], z[:, :, :].rearrange("p e r -> p (e r)"), ident[:, :]).then_inc(z_t, 1)

        def second_up(v):
            pe.wait_ge(z_low, 2 * v + 1)
            for n in (2, 0, 1):
                cols = slice(n * BANK, min((n + 1) * BANK, FOUT))
                o = b_ps[:, 2, GATED:2 * GATED] if n == 2 else b_ps[:, n, :]
                for s, w in ((zt_h, g_h), (zt_h, g_l), (zt_l, g_h)):
                    mm = pe.matmul(o, s[:, :], w[:, cols], start=False, stop=n == 2 and s is zt_l, skip_group_check=n == 2)
                if n == 2:
                    mm.then_inc(up_done, 1)

        def last_up(v):
            pe.wait_ge(z_low, 2 * v + 2)
            for n in range(2):
                for s, w in ((zt_h, bf_h), (zt_h, bf_l), (zt_l, bf_h)):
                    mm = pe.matmul(b_ps[:, n, :], s[:, :], w[:, n * BANK:(n + 1) * BANK], start=False, stop=s is zt_l)
                mm.then_inc(base_done, 1)

        def transpose_x1(u, half):
            pe.wait_ge(x1_ready, 2 * u + half + 1)
            need(pe, x1_low, 2 * u - 1 + half)
            for k in range(half * HALF, (half + 1) * HALF):
                at = (k % HALF) * P
                mm = pe.transpose(x_ps[:, half, at:at + P], x1[:, k * P:(k + 1) * P], ident[:, :])
            mm.then_inc(x1_t, 1)

        def forward(u):
            need(pe, route_step, 2 * u * ROUTE_STEPS)

            def piece(n, k):
                for s, w in ((x1t_h, fr_h), (x1t_h, fr_l), (x1t_l, fr_h)):
                    first = k == 0 and s is x1t_h and w is fr_h
                    if first and n < 2:
                        need(pe, out_ready, 2 * u - 1 + n)
                    cols = slice(n * BANK, min((n + 1) * BANK, FCOLS))
                    mm = pe.matmul(b_ps[:, n, 0:cols.stop - cols.start], s[:, k, :], w[:, k, cols],
                                   start=first, stop=n == 2 and k == KT - 1 and s is x1t_l)
                return mm

            for half in range(2):
                pe.wait_ge(x1_low, 2 * u + half + 1)
                if isinstance(u, int) and u == 0:
                    pe.wait_ge(w_low, KT + half + 1)
                for k in range(half * HALF, (half + 1) * HALF):
                    mm = piece(2, k)
                if half == 1:
                    mm.then_inc(f_done, 1)
                for n in range(2):
                    for k in range(half * HALF, (half + 1) * HALF):
                        piece(n, k)

        def step(u, main, gating, nxt):
            v = u - 1
            for k in range(KT):
                if gating and k == 6:
                    transpose_z(v, 0)
                if main:
                    project(u, 0, k)
                    if not gating and k < HALF:
                        project(u, 1, k)
            if gating:
                second_up(v)
            for k in range(KT):
                if k == 6:
                    if gating:
                        transpose_z(v, 1)
                    if main:
                        transpose_x1(u, 0)
                if main and (gating or k >= HALF):
                    project(u, 1, k)
            if gating:
                last_up(v)
            if main:
                transpose_x1(u, 1)
                if isinstance(u, int) and u == 0:
                    pe.wait_ge(fold2.out_low, fold2.chunks * fold2.TILES)
                forward(u)

        pe.wait_ge(consts_in, 16 * len(consts))
        steps(pe, step)

    return Programs(sync, scalar, gpsimd, vector, tensor), begin, (high_first, low_first)


def kernel(**inputs):
    import concourse.bacc as bacc
    from concourse.bass_utils import run_bass_kernel_spmd

    arrays = layout({k: np.asarray(v) for k, v in inputs.items()})
    nc = bacc.Bacc("TRN2", target_bir_lowering=False, num_devices=1, dynamic_dma_scratch_size=1024)
    tensors = {n: nc.dram_tensor(f"in_{n}", v.shape, mybir.dt.from_np(v.dtype), kind="ExternalInput").ap() for n, v in arrays.items()}
    tensors["out"] = nc.dram_tensor("out", (UNITS, P, D), F32, kind="ExternalOutput").ap()
    build(nc, tensors)
    r = run_bass_kernel_spmd(nc, [{f"in_{n}": v for n, v in arrays.items()}], core_ids=[0])
    return r.results[0]["out"].reshape(BATCH, SEQ, D)


def layout(x):
    def by_k(w):
        return w.reshape(KT, P, -1).transpose(1, 0, 2)

    def heads_first(w):
        w = w.reshape(QUADS, 4, GRP, HD, -1)
        return w.transpose(0, 2, 1, 3, 4).reshape(HEADS * HD, -1)

    tok = x["x"].reshape(UNITS, P, D)
    w_qkv, nq = x["L0_attn_w_qkv"], HEADS * HD
    w_qkv = np.concatenate([heads_first(w_qkv[:nq]), w_qkv[nq:]])
    b_qkv = x["L0_attn_b_qkv"]
    b_qkv = np.concatenate([heads_first(b_qkv[:nq])[:, 0], b_qkv[nq:]])
    last = np.concatenate([x["L0_ffn_W_base"], x["L0_ffn_W_router"], x["L0_ffn_A"].reshape(ERS, D)])
    gate2 = np.concatenate([x["L0_cond2_Wr"], x["L0_cond2_A"].reshape(ERS, D)])
    last_t = by_k(last.T)
    pos = (np.arange(P) % SEQ).astype(np.float32)
    inv = np.float32(1.0) / np.float32(10000.0) ** (np.arange(0, HD, 2, dtype=np.float32) / np.float32(HD))
    ang = (pos[:, None] * inv[None, :]).astype(np.float32)
    mask_l = np.zeros((P, P), np.float32)
    mask_l[np.arange(P) % SEQ, np.arange(P)] = 1
    mask_r = np.zeros((P, KVH, SEQ), np.float32)
    mask_r[:SEQ] = np.where(np.arange(SEQ)[:, None] >= np.arange(SEQ)[None, :], 0.0, -1e20)[:, None, :]
    part = np.arange(P)
    out = {
        "x_t": tok.reshape(UNITS, P, KT, P).transpose(0, 3, 2, 1),
        "x_tok": tok,
        "labeler": x["itok_B_0_2"].reshape(1, BATCH),
        "language": x["itok_B_0_7"].reshape(UNITS, BPU).T,
        "w_cond": by_k(x["L0_cond_W"]),
        "wqkv_t": by_k(w_qkv.T).reshape(P, KT, QKV // FCH, FCH).transpose(2, 0, 1, 3),
        "b_qkv": b_qkv,
        "lora_a": x["L0_cond_lora_A"].reshape(LAB, KT, P, LR).transpose(0, 2, 1, 3),
        "lora_b": by_k(x["L0_cond_lora_B_w"]),
        "wo_t": by_k(heads_first(x["L0_attn_w_o"].T)),
        "b_o": x["L0_attn_b_o"],
        "w_2": by_k(x["L0_cond2_W"]),
        "b2_up": by_k(x["L0_cond2_B"].transpose(1, 0, 2).reshape(D, ERS)),
        "gate2_t": by_k(gate2.T),
        "last_t": np.pad(last_t, ((0, 0), (0, 0), (0, -FOUT % FCH))).reshape(P, KT, -1, FCH).transpose(2, 0, 1, 3),
        "bf_up": x["L0_ffn_B"].transpose(0, 2, 1).reshape(ERS, D),
        "b_base": x["L0_ffn_b_base"],
        "cos": np.cos(ang).astype(np.float32),
        "sin": np.sin(ang).astype(np.float32),
        "ident": np.eye(P, dtype=np.float32),
        "mask_l": mask_l,
        "mask_r": mask_r.reshape(P, BANK),
        "hmask": (part[:, None] // HD == np.arange(4)[None, :]).astype(np.float32),
        "experts": np.broadcast_to(np.arange(EXP, dtype=np.float32), (P, EXP)),
        "before": np.broadcast_to(np.tril(np.ones((EXP, EXP), np.float32), -1).reshape(1, EXP * EXP), (P, EXP * EXP)),
    }
    return {n: np.ascontiguousarray(v) for n, v in out.items()}
```
